# Optimizing a Trainium2 kernel written in Bass

```python
import numpy as np
import jax
import jax.numpy as jnp

def _softmax(x, axis=-1):
    return jax.nn.softmax(x, axis=axis)

def _gelu(x):
    return jax.nn.gelu(x, approximate=True)

def _silu(x):
    return jax.nn.silu(x)

def _sigmoid(x):
    return jax.nn.sigmoid(x)

def _layernorm(x, axis=-1, eps=1e-05):
    m = jnp.mean(x, axis=axis, keepdims=True)
    v = jnp.var(x, axis=axis, keepdims=True)
    return (x - m) / jnp.sqrt(v + eps)

def _scatter_add(tgt, idx, src, axis=0):
    return tgt.at[idx].add(src)

def _segment_sum(src, seg, n):
    return jax.ops.segment_sum(src, seg, n)
kernel_name = 'mk_vit_tower_d1_tok_img768_r4_38cf2f'

def setup_inputs(seed: int=0):
    np.random.seed(seed)
    _w = jnp.asarray

    def _rec_inputs():
        import jax
        import jax.numpy as jnp
        _rk = jax.random.key(seed)
        x = 7.57192e-06 + 1.00007 * jax.random.normal(jax.random.fold_in(_rk, 1), (64, 3, 84, 84), jnp.float32)
        return x
    x = _rec_inputs()

    def _L0_tok_setup():
        import jax, jax.numpy as jnp
        import numpy as np
        import math
        EMB = 64
        M = 32

        def _unfold(x, k, s, p):
            patches = jax.lax.conv_general_dilated_patches(x, filter_shape=(k, k), window_strides=(s, s), padding=((p, p), (p, p)), dimension_numbers=('NCHW', 'OIHW', 'NCHW'))
            B, D, Ho, Wo = patches.shape
            return patches.reshape(B, D, Ho * Wo).transpose(0, 2, 1)

        def _ln(x, g, b):
            mu = jnp.mean(x, -1, keepdims=True)
            var = jnp.var(x, -1, keepdims=True)
            return (x - mu) * jax.lax.rsqrt(var + 1e-05) * g + b

        def _prm_exp(x, w):
            xd = jnp.sum(x * x, -1, keepdims=True) * 0.5
            wtx = jnp.einsum('btd,md->btm', x, w)
            return jnp.exp(wtx - xd) / jnp.sqrt(jnp.float32(w.shape[0]))

        def _performer(x, n1g, n1b, kqvw, kqvb, projw, projb, n2g, n2b, w1, b1, w2, b2, wrand):
            h = _ln(x, n1g, n1b)
            kqv = h @ kqvw + kqvb
            k, q, v = (kqv[..., :EMB], kqv[..., EMB:2 * EMB], kqv[..., 2 * EMB:])
            kp, qp = (_prm_exp(k, wrand), _prm_exp(q, wrand))
            D = jnp.einsum('btm,bm->bt', qp, jnp.sum(kp, 1))[..., None]
            kptv = jnp.einsum('btd,btm->bdm', v, kp)
            y = jnp.einsum('btm,bdm->btd', qp, kptv) / (D + 1e-08)
            y = v + (y @ projw + projb)
            h2 = _ln(y, n2g, n2b)
            return y + (jax.nn.gelu(h2 @ w1 + b1, approximate=False) @ w2 + b2)

        def _forward(x, a1, a2, proj_w, proj_b):
            t = _unfold(x, 7, 4, 2)
            t = _performer(t, *a1)
            B, L, C = t.shape
            s = round(math.sqrt(L))
            t = t.transpose(0, 2, 1).reshape(B, C, s, s)
            t = _unfold(t, 3, 2, 1)
            t = _performer(t, *a2)
            B, L, C = t.shape
            s = round(math.sqrt(L))
            t = t.transpose(0, 2, 1).reshape(B, C, s, s)
            t = _unfold(t, 3, 2, 1)
            return t @ proj_w + proj_b
        key = jax.random.key(seed)
        ks = iter(jax.random.split(key, 40))

        def nrm(shape, s=0.02):
            return jax.random.normal(next(ks), shape, jnp.float32) * s

        def ortho():
            a = jax.random.normal(next(ks), (EMB, M), jnp.float32)
            q, _ = jnp.linalg.qr(a)
            return q.T * jnp.sqrt(jnp.float32(M))

        def attn_params(dim):
            return dict(n1g=jnp.ones((dim,), jnp.float32), n1b=jnp.zeros((dim,), jnp.float32), kqvw=nrm((dim, 3 * EMB)), kqvb=jnp.zeros((3 * EMB,), jnp.float32), projw=nrm((EMB, EMB)), projb=jnp.zeros((EMB,), jnp.float32), n2g=jnp.ones((EMB,), jnp.float32), n2b=jnp.zeros((EMB,), jnp.float32), w1=nrm((EMB, EMB)), b1=jnp.zeros((EMB,), jnp.float32), w2=nrm((EMB, EMB)), b2=jnp.zeros((EMB,), jnp.float32), w=ortho())
        inp = {'x': jax.random.normal(next(ks), (64, 3, 224, 224), jnp.float32)}
        for pre, dim in (('a1_', 3 * 7 * 7), ('a2_', EMB * 3 * 3)):
            for k2, v in attn_params(dim).items():
                inp[pre + k2] = v
        inp['proj_w'] = nrm((EMB * 9, 192))
        inp['proj_b'] = jnp.zeros((192,), jnp.float32)
        return inp
    _L0_tok_all = _L0_tok_setup()
    _L0_tok_in = {k: v for k, v in _L0_tok_all.items() if k in ('a1_n1g', 'a1_n1b', 'a1_kqvw', 'a1_kqvb', 'a1_projw', 'a1_projb', 'a1_n2g', 'a1_n2b', 'a1_w1', 'a1_b1', 'a1_w2', 'a1_b2', 'a1_w', 'a2_n1g', 'a2_n1b', 'a2_kqvw', 'a2_kqvb', 'a2_projw', 'a2_projb', 'a2_n2g', 'a2_n2b', 'a2_w1', 'a2_b1', 'a2_w2', 'a2_b2', 'a2_w', 'proj_w', 'proj_b')}
    del _L0_tok_all

    def _L0_attn_setup():
        import jax, jax.numpy as jnp
        import numpy as np
        DIM = 192
        NUM_HEADS = 12
        HEAD_DIM = DIM // NUM_HEADS
        SPARSITY_RATIO = 0.5
        key = jax.random.key(seed)
        ks = jax.random.split(key, 6)
        B, N = (4, 256)
        x = jax.random.normal(ks[0], (B, N, DIM), dtype=jnp.float32)
        s = 1.0 / np.sqrt(DIM)
        qkv_w = jax.random.uniform(ks[1], (3 * DIM, DIM), jnp.float32, -s, s)
        qkv_b = jax.random.uniform(ks[2], (3 * DIM,), jnp.float32, -s, s)
        proj_w = jax.random.uniform(ks[3], (DIM, DIM), jnp.float32, -s, s)
        proj_b = jax.random.uniform(ks[4], (DIM,), jnp.float32, -s, s)
        temperature = jnp.ones((1,), jnp.float32) * 0.1
        return {'x': x, 'qkv_w': qkv_w, 'qkv_b': qkv_b, 'proj_w': proj_w, 'proj_b': proj_b, 'temperature': temperature}
    _L0_attn_all = _L0_attn_setup()
    _L0_attn_in = {k: v for k, v in _L0_attn_all.items() if k in ('qkv_w', 'qkv_b', 'proj_w', 'proj_b', 'temperature')}
    del _L0_attn_all

    def _L0_ffn_setup():
        import jax, jax.numpy as jnp
        import numpy as np
        B_SZ, S, D = (8, 128, 192)
        H = 12
        N_EXP = 8
        RANK = 16
        ALPHA = 32
        TOP_K = 2
        key = jax.random.key(seed)
        ks = jax.random.split(key, 9)
        x = jax.random.normal(ks[0], (B_SZ, S, D), jnp.float32)
        W_qkv = jax.random.normal(ks[1], (3 * D, D), jnp.float32) * 0.02
        b_qkv = jnp.zeros((3 * D,), jnp.float32)
        W_gate = jax.random.normal(ks[2], (N_EXP, D), jnp.float32) * 0.02
        b_gate = jnp.zeros((N_EXP,), jnp.float32)
        A = jax.random.normal(ks[3], (N_EXP, RANK, D), jnp.float32) * 0.02
        B_lora = jax.random.normal(ks[4], (N_EXP, 3 * D, RANK), jnp.float32) * 0.02
        W_proj = jax.random.normal(ks[5], (D, D), jnp.float32) * 0.02
        b_proj = jnp.zeros((D,), jnp.float32)
        return {'x': x, 'W_qkv': W_qkv, 'b_qkv': b_qkv, 'W_gate': W_gate, 'b_gate': b_gate, 'A': A, 'B_lora': B_lora, 'W_proj': W_proj, 'b_proj': b_proj}
    _L0_ffn_all = _L0_ffn_setup()
    _L0_ffn_in = {k: v for k, v in _L0_ffn_all.items() if k in ('W_qkv', 'b_qkv', 'W_gate', 'b_gate', 'A', 'B_lora', 'W_proj', 'b_proj')}
    del _L0_ffn_all
    return {'x': x, 'L0_tok_a1_n1g': _L0_tok_in['a1_n1g'], 'L0_tok_a1_n1b': _L0_tok_in['a1_n1b'], 'L0_tok_a1_kqvw': _L0_tok_in['a1_kqvw'], 'L0_tok_a1_kqvb': _L0_tok_in['a1_kqvb'], 'L0_tok_a1_projw': _L0_tok_in['a1_projw'], 'L0_tok_a1_projb': _L0_tok_in['a1_projb'], 'L0_tok_a1_n2g': _L0_tok_in['a1_n2g'], 'L0_tok_a1_n2b': _L0_tok_in['a1_n2b'], 'L0_tok_a1_w1': _L0_tok_in['a1_w1'], 'L0_tok_a1_b1': _L0_tok_in['a1_b1'], 'L0_tok_a1_w2': _L0_tok_in['a1_w2'], 'L0_tok_a1_b2': _L0_tok_in['a1_b2'], 'L0_tok_a1_w': _L0_tok_in['a1_w'], 'L0_tok_a2_n1g': _L0_tok_in['a2_n1g'], 'L0_tok_a2_n1b': _L0_tok_in['a2_n1b'], 'L0_tok_a2_kqvw': _L0_tok_in['a2_kqvw'], 'L0_tok_a2_kqvb': _L0_tok_in['a2_kqvb'], 'L0_tok_a2_projw': _L0_tok_in['a2_projw'], 'L0_tok_a2_projb': _L0_tok_in['a2_projb'], 'L0_tok_a2_n2g': _L0_tok_in['a2_n2g'], 'L0_tok_a2_n2b': _L0_tok_in['a2_n2b'], 'L0_tok_a2_w1': _L0_tok_in['a2_w1'], 'L0_tok_a2_b1': _L0_tok_in['a2_b1'], 'L0_tok_a2_w2': _L0_tok_in['a2_w2'], 'L0_tok_a2_b2': _L0_tok_in['a2_b2'], 'L0_tok_a2_w': _L0_tok_in['a2_w'], 'L0_tok_proj_w': _L0_tok_in['proj_w'], 'L0_tok_proj_b': _L0_tok_in['proj_b'], 'L0_attn_qkv_w': _L0_attn_in['qkv_w'], 'L0_attn_qkv_b': _L0_attn_in['qkv_b'], 'L0_attn_proj_w': _L0_attn_in['proj_w'], 'L0_attn_proj_b': _L0_attn_in['proj_b'], 'L0_attn_temperature': _L0_attn_in['temperature'], 'L0_ffn_W_qkv': _L0_ffn_in['W_qkv'], 'L0_ffn_b_qkv': _L0_ffn_in['b_qkv'], 'L0_ffn_W_gate': _L0_ffn_in['W_gate'], 'L0_ffn_b_gate': _L0_ffn_in['b_gate'], 'L0_ffn_A': _L0_ffn_in['A'], 'L0_ffn_B_lora': _L0_ffn_in['B_lora'], 'L0_ffn_W_proj': _L0_ffn_in['W_proj'], 'L0_ffn_b_proj': _L0_ffn_in['b_proj']}

def reference(x, L0_tok_a1_n1g, L0_tok_a1_n1b, L0_tok_a1_kqvw, L0_tok_a1_kqvb, L0_tok_a1_projw, L0_tok_a1_projb, L0_tok_a1_n2g, L0_tok_a1_n2b, L0_tok_a1_w1, L0_tok_a1_b1, L0_tok_a1_w2, L0_tok_a1_b2, L0_tok_a1_w, L0_tok_a2_n1g, L0_tok_a2_n1b, L0_tok_a2_kqvw, L0_tok_a2_kqvb, L0_tok_a2_projw, L0_tok_a2_projb, L0_tok_a2_n2g, L0_tok_a2_n2b, L0_tok_a2_w1, L0_tok_a2_b1, L0_tok_a2_w2, L0_tok_a2_b2, L0_tok_a2_w, L0_tok_proj_w, L0_tok_proj_b, L0_attn_qkv_w, L0_attn_qkv_b, L0_attn_proj_w, L0_attn_proj_b, L0_attn_temperature, L0_ffn_W_qkv, L0_ffn_b_qkv, L0_ffn_W_gate, L0_ffn_b_gate, L0_ffn_A, L0_ffn_B_lora, L0_ffn_W_proj, L0_ffn_b_proj):
    import jax
    import jax.numpy as jnp

    def _L0_tok_ref(x, a1_n1g, a1_n1b, a1_kqvw, a1_kqvb, a1_projw, a1_projb, a1_n2g, a1_n2b, a1_w1, a1_b1, a1_w2, a1_b2, a1_w, a2_n1g, a2_n1b, a2_kqvw, a2_kqvb, a2_projw, a2_projb, a2_n2g, a2_n2b, a2_w1, a2_b1, a2_w2, a2_b2, a2_w, proj_w, proj_b):
        import jax, jax.numpy as jnp
        import numpy as np
        import math
        EMB = 64
        M = 32

        def _unfold(x, k, s, p):
            patches = jax.lax.conv_general_dilated_patches(x, filter_shape=(k, k), window_strides=(s, s), padding=((p, p), (p, p)), dimension_numbers=('NCHW', 'OIHW', 'NCHW'))
            B, D, Ho, Wo = patches.shape
            return patches.reshape(B, D, Ho * Wo).transpose(0, 2, 1)

        def _ln(x, g, b):
            mu = jnp.mean(x, -1, keepdims=True)
            var = jnp.var(x, -1, keepdims=True)
            return (x - mu) * jax.lax.rsqrt(var + 1e-05) * g + b

        def _prm_exp(x, w):
            xd = jnp.sum(x * x, -1, keepdims=True) * 0.5
            wtx = jnp.einsum('btd,md->btm', x, w)
            return jnp.exp(wtx - xd) / jnp.sqrt(jnp.float32(w.shape[0]))

        def _performer(x, n1g, n1b, kqvw, kqvb, projw, projb, n2g, n2b, w1, b1, w2, b2, wrand):
            h = _ln(x, n1g, n1b)
            kqv = h @ kqvw + kqvb
            k, q, v = (kqv[..., :EMB], kqv[..., EMB:2 * EMB], kqv[..., 2 * EMB:])
            kp, qp = (_prm_exp(k, wrand), _prm_exp(q, wrand))
            D = jnp.einsum('btm,bm->bt', qp, jnp.sum(kp, 1))[..., None]
            kptv = jnp.einsum('btd,btm->bdm', v, kp)
            y = jnp.einsum('btm,bdm->btd', qp, kptv) / (D + 1e-08)
            y = v + (y @ projw + projb)
            h2 = _ln(y, n2g, n2b)
            return y + (jax.nn.gelu(h2 @ w1 + b1, approximate=False) @ w2 + b2)

        def _forward(x, a1, a2, proj_w, proj_b):
            t = _unfold(x, 7, 4, 2)
            t = _performer(t, *a1)
            B, L, C = t.shape
            s = round(math.sqrt(L))
            t = t.transpose(0, 2, 1).reshape(B, C, s, s)
            t = _unfold(t, 3, 2, 1)
            t = _performer(t, *a2)
            B, L, C = t.shape
            s = round(math.sqrt(L))
            t = t.transpose(0, 2, 1).reshape(B, C, s, s)
            t = _unfold(t, 3, 2, 1)
            return t @ proj_w + proj_b
        a1 = (a1_n1g, a1_n1b, a1_kqvw, a1_kqvb, a1_projw, a1_projb, a1_n2g, a1_n2b, a1_w1, a1_b1, a1_w2, a1_b2, a1_w)
        a2 = (a2_n1g, a2_n1b, a2_kqvw, a2_kqvb, a2_projw, a2_projb, a2_n2g, a2_n2b, a2_w1, a2_b1, a2_w2, a2_b2, a2_w)
        return _forward(x, a1, a2, proj_w, proj_b)

    def _L0_attn_ref(x, qkv_w, qkv_b, proj_w, proj_b, temperature):
        import jax, jax.numpy as jnp
        import numpy as np
        DIM = 192
        NUM_HEADS = 12
        HEAD_DIM = DIM // NUM_HEADS
        SPARSITY_RATIO = 0.5
        B, N, C = x.shape
        scale = HEAD_DIM ** (-0.5)
        k_keep = max(1, int(N * SPARSITY_RATIO))
        qkv = (x @ qkv_w.T + qkv_b).reshape(B, N, 3, NUM_HEADS, HEAD_DIM)
        qkv = jnp.transpose(qkv, (2, 0, 3, 1, 4))
        q, k, v = (qkv[0], qkv[1], qkv[2])
        temp = jnp.clip(temperature, 0.01, None)
        q = q / temp
        scores = jnp.einsum('bhnd,bhmd->bhnm', q, k) * scale
        thresh = jax.lax.top_k(scores, k_keep)[0][..., -1:]
        scores = jnp.where(scores >= thresh, scores, -jnp.inf)
        probs = jax.nn.softmax(scores, axis=-1)
        out = jnp.einsum('bhnm,bhmd->bhnd', probs, v)
        out = jnp.transpose(out, (0, 2, 1, 3)).reshape(B, N, C)
        return out @ proj_w.T + proj_b

    def _L0_ffn_ref(x, W_qkv, b_qkv, W_gate, b_gate, A, B_lora, W_proj, b_proj):
        import jax, jax.numpy as jnp
        import numpy as np
        B_SZ, S, D = (8, 128, 192)
        H = 12
        N_EXP = 8
        RANK = 16
        ALPHA = 32
        TOP_K = 2
        b, s, d = x.shape
        n_exp, rank = (A.shape[0], A.shape[1])
        scaling = ALPHA / rank
        head_dim = d // H
        scale = head_dim ** (-0.5)
        t = b * s
        x_flat = x.reshape(t, d)
        qkv_base = x @ W_qkv.T + b_qkv
        logits = x_flat @ W_gate.T + b_gate
        router_probs = jax.nn.softmax(logits, axis=-1)
        top_k_weights, top_k_indices = jax.lax.top_k(router_probs, TOP_K)
        a_down = jnp.einsum('td,nrd->tnr', x_flat, A)
        expert_out = jnp.einsum('tnr,nor->tno', a_down, B_lora) * scaling
        dispatch = jnp.zeros((t, n_exp), x.dtype).at[jnp.arange(t)[:, None], top_k_indices].add(top_k_weights)
        sparse_out = jnp.einsum('tno,tn->to', expert_out, dispatch)
        qkv = qkv_base + sparse_out.reshape(b, s, 3 * d)
        qkv = qkv.reshape(b, s, 3, H, head_dim).transpose(2, 0, 3, 1, 4)
        q, k, v = (qkv[0], qkv[1], qkv[2])
        attn = jax.nn.softmax(jnp.einsum('bhqd,bhkd->bhqk', q, k) * scale, axis=-1)
        out = jnp.einsum('bhqk,bhkd->bhqd', attn, v)
        out = out.transpose(0, 2, 1, 3).reshape(b, s, d)
        return out @ W_proj.T + b_proj
    h = _L0_tok_ref(x, L0_tok_a1_n1g, L0_tok_a1_n1b, L0_tok_a1_kqvw, L0_tok_a1_kqvb, L0_tok_a1_projw, L0_tok_a1_projb, L0_tok_a1_n2g, L0_tok_a1_n2b, L0_tok_a1_w1, L0_tok_a1_b1, L0_tok_a1_w2, L0_tok_a1_b2, L0_tok_a1_w, L0_tok_a2_n1g, L0_tok_a2_n1b, L0_tok_a2_kqvw, L0_tok_a2_kqvb, L0_tok_a2_projw, L0_tok_a2_projb, L0_tok_a2_n2g, L0_tok_a2_n2b, L0_tok_a2_w1, L0_tok_a2_b1, L0_tok_a2_w2, L0_tok_a2_b2, L0_tok_a2_w, L0_tok_proj_w, L0_tok_proj_b)
    h = h + _L0_attn_ref(_layernorm(h, axis=-1), L0_attn_qkv_w, L0_attn_qkv_b, L0_attn_proj_w, L0_attn_proj_b, L0_attn_temperature)
    h = h + _L0_ffn_ref(_layernorm(h, axis=-1), L0_ffn_W_qkv, L0_ffn_b_qkv, L0_ffn_W_gate, L0_ffn_b_gate, L0_ffn_A, L0_ffn_B_lora, L0_ffn_W_proj, L0_ffn_b_proj)
    return h

_drawn_inputs = setup_inputs


def setup_inputs(seed=0):
    import zlib

    import numpy as np

    out = dict(_drawn_inputs(seed))
    spreads = {'L0_tok_a1_n1g': (1.0, 0.2),
     'L0_tok_a1_n1b': (0.0, 0.1),
     'L0_tok_a1_kqvb': (0.0, 0.1),
     'L0_tok_a1_projb': (0.0, 0.1),
     'L0_tok_a1_n2g': (1.0, 0.6),
     'L0_tok_a1_n2b': (0.0, 0.8),
     'L0_tok_a1_b1': (0.0, 0.1),
     'L0_tok_a1_b2': (0.0, 0.1),
     'L0_tok_a2_n1g': (1.0, 0.2),
     'L0_tok_a2_n1b': (0.0, 0.1),
     'L0_tok_a2_kqvb': (0.0, 0.1),
     'L0_tok_a2_projb': (0.0, 0.1),
     'L0_tok_a2_n2g': (1.0, 0.6),
     'L0_tok_a2_n2b': (0.0, 0.8),
     'L0_tok_a2_b1': (0.0, 0.4),
     'L0_tok_a2_b2': (0.0, 0.1),
     'L0_tok_proj_b': (0.0, 0.1),
     'L0_ffn_b_qkv': (0.0, 0.1),
     'L0_ffn_b_gate': (0.0, 0.8),
     'L0_ffn_b_proj': (0.0, 0.1)}
    factors = {'L0_tok_a1_w': 5.333, 'L0_ffn_W_gate': 8.0, 'L0_ffn_A': 8.0, 'L0_ffn_B_lora': 8.0}
    for name, (base, spread) in spreads.items():
        noise = np.random.default_rng([zlib.crc32(name.encode()), seed]).standard_normal(out[name].shape)
        drawn = base * np.exp(spread * noise) if base else spread * noise
        out[name] = jnp.asarray(drawn.astype(out[name].dtype))
    for name, factor in factors.items():
        out[name] = (out[name] * factor).astype(out[name].dtype)
    return out
```

```python
from contextlib import ExitStack

import numpy as np

import concourse.bass as bass
from concourse import mybir

F32 = mybir.dt.float32
ALU = mybir.AluOpType
ACT = mybir.ActivationFunctionType
AX_X = mybir.AxisListType.X

P = 128
B = 64
EMB, M = 64, 32
C3 = 3 * EMB
BLK = 4
GRID = 22
PIX = 3 * BLK * BLK
S1, S2, S3 = 21, 11, 6
T1, T2, T3 = S1 * S1, S2 * S2, S3 * S3
F1, F2 = 3 * 7 * 7, EMB * 9
NCH = 4
ROWS1 = 6
NT1 = ROWS1 * S1
XR = 25
NTAP = 5
TAPS = [((0, 0), (1, 0)), ((0, 1), (1, 1)), ((0, 2), (1, 2)), ((2, 0), (2, 1)), ((2, 2),)]
PAD1, PAD2 = S1 + 2, S2 + 2
MAP1, MAP2 = PAD1 * PAD1, PAD2 * PAD2
V0, ONE, WK, MEAN, SQ = 128, 192, 193, 257, 258
D = 192
HEADS, HD = 12, 16
GI, NG = 3, 22
GT = GI * T3
TRI = HEADS // 3
HALF = D // 2
NEXP, RANK, TOP_K, ALPHA = 8, 16, 2, 32
KEEP = T3 // 2
LANES = 2
EPS = 1e-5
HUGE = 3.0e38


class Part:
    pass


def performer_sizes():
    one = Part()
    one.name = 'a1'
    one.stage = 1
    one.nk = 2
    one.kp = 2 * PIX
    one.nt = NT1
    one.units = B
    one.shared_kv = True
    one.real = [NT1, NT1, NT1, T1 - 3 * NT1]
    one.features = F1
    one.mlp_units = B // 2
    one.columns = T1
    two = Part()
    two.name = 'a2'
    two.stage = 2
    two.nk = NTAP
    two.kp = P
    two.nt = T2
    two.units = B // NCH
    two.shared_kv = False
    two.real = [T2] * NCH
    two.features = F2
    two.mlp_units = B // NCH // 2
    two.columns = NCH * T2
    return one, two


def build(nc, a, out):
    with ExitStack() as ctx:
        def sb(name, shape):
            return ctx.enter_context(nc.sbuf_tensor(name, shape, F32))

        def sem(name):
            return ctx.enter_context(nc.semaphore(name))

        def sems(prefix, names):
            return {n: sem(prefix + n) for n in names.split()}

        psum = ctx.enter_context(nc.psum_tensor("psum", [P, 8, 512], F32))

        ident = sb("ident", [P, P])
        blockmean = sb("blockmean", [P, P])
        ones_sq = sb("ones_sq", [P, P])
        neg_half = sb("neg_half", [P, 2 * NCH])
        ln_m = sb("ln_m", [P, 1])
        scratch = sb("scratch", [P, 1])
        const_in = sem("const_in")
        const_set = sem("const_set")

        y_mem = sb("y_mem", [P, B // 2 * NCH * 2 * EMB])
        late = sb("late", [P, B // 2 * MAP1])
        y1_all = late[:, :].rearrange("p (n x) -> p n x", x=MAP1)
        y_out1 = y_mem[:, :].rearrange("p (n c i e) -> p n c i e", c=NCH, i=2, e=EMB)
        y_pair = y_mem[:, :].rearrange("p (n c e) -> p n c e", c=NCH, e=2 * EMB)
        n2 = B * EMB
        y_out2 = y_mem[:, 0:n2].rearrange("p (n c e) -> p n c e", c=NCH, e=EMB)
        y2_all = y_mem[:, n2:n2 + NG * GI // 2 * MAP2].rearrange("p (n x) -> p n x", x=MAP2)
        zeroed = sem("zeroed")

        def carver(mem, start=0):
            at = [start]

            def tile(rows, *dims):
                n = int(np.prod(dims))
                v = mem[0:rows, at[0]:at[0] + n]
                at[0] += n
                assert at[0] <= mem.shape[1], (at[0], mem.shape)
                if len(dims) == 1:
                    return v
                names = "abc"[:len(dims)]
                return v.rearrange(f"p ({' '.join(names)}) -> p {' '.join(names)}",
                                   **{m: d for m, d in zip(names, dims)})

            return tile

        early_tile = carver(y_mem)

        one, two = performer_sizes()
        for st in (one, two):
            n = st.name + "_"
            st.wraw = early_tile(st.kp, st.nk, C3)
            st.wcat = sb(n + "wcat", [st.kp, st.nk, MEAN + 1])
            st.gcol = sb(n + "gcol", [st.kp, st.nk])
            st.bcol = sb(n + "bcol", [st.kp, st.nk])
            st.inv = sb(n + "inv", [st.kp, st.nk])
            st.ninv = sb(n + "ninv", [st.kp, st.nk])
            st.kqvb = sb(n + "kqvb", [P, C3])
            st.bias = sb(n + "bias", [P, MEAN])
            st.pjb = sb(n + "pjb", [P, EMB])
            st.paug = sb(n + "paug", [EMB + 1, EMB + 1])
            st.wT = sb(n + "wT", [EMB, M])
            st.w1 = sb(n + "w1", [P, P])
            st.w1c = sb(n + "w1c", [P, P])
            st.w2 = sb(n + "w2", [P, P])
            st.cols = sb(n + "cols", [P, 4])
            st.b1c = sb(n + "b1c", [P, 1])
            st.w_in = sem(n + "w_in")
        w = sems("w_", "scaled summed centered wide biased bias_set turned turned_copied folded "
                       "folded_copied mlp_scaled mlp_summed mlp_set")
        x_made = sems("x_", "act dve")
        k = sems("k_", "xsq main stat square_mean var var_eps rstd z kqsq xd arg e vb kvq kvq_copied "
                       "mp mp_copied yp den rec yn y")
        m = sems("m_", "sq sum1 sum2 square_mean var var_eps rstd yn tr tr_copied w1 gelu w2 out")
        x_in = [sem(f"x_in{i}") for i in range(2)]
        m_in = [sem(f"m_in{i}") for i in range(2)]
        one.w0, two.w0 = 0, 1
        one.t0, two.t0 = 0, one.nk + 1
        one.k0, two.k0 = 1, 1 + one.units
        one.m0, two.m0 = 1, 1 + one.mlp_units
        one.y0, two.y0 = 0, 16 * one.mlp_units // 2
        wide = early_tile(P, NTAP, P)
        turned = early_tile(EMB, 2, P)

        xbuf = [sb(f"xbuf{i}", [P, NCH * NTAP * T2]) for i in range(2)]
        xsqbuf = [sb(f"xsqbuf{i}", [P, NCH * NTAP * T2]) for i in range(2)]
        z = [sb(f"z{i}", [P, NCH, MEAN]) for i in range(2)]
        e = [sb(f"e{i}", [P, NCH, 2, M]) for i in range(2)]
        vb = [sb(f"vb{i}", [P, NCH, EMB]) for i in range(2)]
        kqsq = sb("kqsq", [P, NCH, 2, EMB])
        xd = sb("xd", [P, NCH, 2])
        arg = sb("arg", [P, NCH, 2, M])
        stat = sb("stat", [P, NCH, 2])
        sqm = sb("sqm", [P, 2 * NCH])
        var = sb("var", [P, 2 * NCH])
        var_eps = sb("var_eps", [P, 2 * NCH])
        rstd = sb("rstd", [P, 2 * NCH])
        kv = sb("kv", [EMB + 1, NCH, M])
        qT = sb("qT", [M, NCH * NT1])
        mp = sb("mp", [M, NCH, EMB + 1])
        den = sb("den", [P, NCH])
        rec = sb("rec", [P, NCH])
        yn = sb("yn", [P, NCH, EMB])
        sum1 = sb("sum1", [P, 2 * NCH])
        sum2 = sb("sum2", [P, 2 * NCH])
        yfix = [x[:, 0:512].rearrange("p (c e) -> p c e", e=P) for x in xsqbuf]
        ysq = xsqbuf[0][:, 512:1024].rearrange("p (c e) -> p c e", e=EMB)
        ynm = xsqbuf[0][:, 1024:1536].rearrange("p (c e) -> p c e", e=P)
        ynT = xsqbuf[0][:, 1536:2048]
        gel = xsqbuf[1][:, 512:1024]

        X1 = [x[0:2 * PIX, 0:XR * S1] for x in xbuf]
        X1q = [x[0:2 * PIX, 0:XR * S1] for x in xsqbuf]

        def patches(st, x, c, kk):
            if st.stage == 1:
                return x[0:st.kp, NT1 * c + S1 * kk:NT1 * c + S1 * kk + NT1]
            at = (c * NTAP + kk) * T2
            return x[0:krows(st, kk), at:at + T2]

        def krows(st, kk):
            return st.kp if st.stage == 1 else EMB * len(TAPS[kk])

        late_tile = carver(late)
        tail_tile = carver(y_mem, n2 + NG * GI // 2 * MAP2)
        pw = tail_tile(P, NTAP, D)
        pb = tail_tile(P, D)
        wqkv, wproj = [], []
        for i in range(2):
            old_input = carver(xbuf[i])
            wqkv.append(old_input(HALF + 1, 2, 3 * D))
            wproj.append(old_input(3 * HD + 1, TRI, D))
        wrout = tail_tile(HALF + 1, 2, NEXP + P)
        blora = tail_tile(P, 3 * D)
        qscale = sb("qscale", [HALF, 4])
        kmask = sb("kmask", [HALF, 6])
        vmask = tail_tile(GT, D)
        thrice = tail_tile(GT, GI, GT)
        t_in = sem("t_in")
        clipped = sem("clipped")
        scale_set = sem("scale_set")
        lanes_set = sem("lanes_set")

        g_tile = late_tile(P, NTAP, LANES * GT)
        lanes = []
        for i in range(LANES):
            ln = Part()
            ln.i = i
            ln.h = late_tile(GT, D)
            ln.bn = late_tile(GT, 6)
            ln.mv = late_tile(GT, 2)
            ln.veps = late_tile(GT, 1)
            ln.r = late_tile(GT, 1)
            ln.hn = late_tile(GT, D)
            ln.hnT = late_tile(HALF + 1, 2, GT)
            ln.qx = late_tile(HALF, 2, GI * GT)
            ln.kT = late_tile(HALF, 2, GT)
            ln.kx = late_tile(HALF, 2, GI * 6 * T3)
            ln.vx = late_tile(GT, GI, D)
            ln.vt = late_tile(GT, D)
            ln.s0 = late_tile(GT, HEADS, T3)
            ln.s1 = late_tile(GT, HEADS, T3)
            ln.s2 = late_tile(GT, HEADS, T3)
            ln.keep = late_tile(GT, HEADS, T3)
            ln.top = [late_tile(GT, HEADS, 8) for _ in range(3)]
            ln.mx = late_tile(GT, HEADS)
            ln.sm = late_tile(GT, HEADS)
            ln.rs = late_tile(GT, HEADS)
            ln.pT = late_tile(GT, TRI * GT)
            ln.oT = late_tile(3 * HD + 1, TRI * GT)
            ln.res = late_tile(GT, D)
            ln.lg = late_tile(GT, 2 * NEXP)
            ln.lg2 = late_tile(GT, 2 * NEXP)
            ln.l8 = late_tile(GT, 8)
            ln.rep = late_tile(GT, 8)
            ln.sel = late_tile(GT, NEXP)
            ln.lm = late_tile(GT, NEXP)
            ln.le = late_tile(GT, NEXP)
            ln.ls = late_tile(GT, 1)
            ln.lr = late_tile(GT, 1)
            ln.lw = late_tile(GT, NEXP)
            ln.lw2 = late_tile(GT, NEXP)
            ln.aw = late_tile(GT, P)
            ln.aT = late_tile(P, GT)
            ln.res_ready = sem(f'res_ready{i}')
            ln.res_out = sem(f'res_out{i}')
            lanes.append(ln)
        t = sems("t_", "g hp h s0 top8 keep em rt lg l8 rep found sel lm le lr lw lw2 aw at aT")
        u = sems("u_", "bn mv veps r hn tr hnT qk v vt v3 q kT kx vx s mx sub exp sum rs p pt pT o oT pj h")

        block = ctx.enter_context(nc.Block())

        def nth(j, par):
            return j * 2 + par

        def peeled(j):
            return isinstance(j, int) and j == 0

        def load_x(sp, st, j, par):
            n = nth(j, par)
            if not peeled(j):
                sp.wait_ge(k["main"], NCH * (n + (st.k0 - 1)))
            src = a["x"][bass.ds(n, 1), :, :].rearrange("o p t -> (o p) t")
            sp.dma_start(X1[par][:, 0:GRID * S1], src).then_inc(x_in[par], 16)

        def load_y(sp, st, j, par):
            n = nth(j, par)
            if not peeled(j):
                sp.wait_ge(m["w2"], n + (st.m0 - 1))
            sp.dma_start(yfix[par][0:st.nt, :, :],
                         y_pair[0:st.nt, bass.ds(n, 1), :, :].rearrange("p o c e -> p (o c) e")
                         ).then_inc(m_in[par], 16)

        def store_group(sp, it, ln):
            sp.wait_ge(ln.res_ready, it + 2)
            sp.dma_start(out[bass.ds(it * (LANES * GT) + ln.i * GT, GT), :], ln.res).then_inc(ln.res_out, 16)

        @block.sync
        def _(sp):
            for name, s_ in (*k.items(), *m.items()):
                sp.sem_inc(s_, NCH if name in ("main", "z") else 1)
            for ln in lanes:
                sp.sem_inc(ln.res_ready, 1)
                sp.sem_inc(ln.res_out, 16)
            sp.sem_inc(t["hp"], 1)
            sp.dma_start(ident[:, :], a["ident"]).then_inc(const_in, 16)
            sp.dma_start(blockmean[:, :], a["blockmean"]).then_inc(const_in, 16)
            for st in (one, two):
                sp.dma_start(st.wraw, a[st.name + "_w"]).then_inc(st.w_in, 16)
                for dst, src in ((st.gcol, "g"), (st.bcol, "b"), (st.inv, "inv"), (st.ninv, "ninv"),
                                 (st.kqvb, "kqvb"), (st.pjb, "pjb"), (st.paug, "paug"), (st.wT, "wT"),
                                 (st.w1, "w1"), (st.w2, "w2"), (st.cols, "cols")):
                    sp.dma_start(dst[:, :], a[st.name + "_" + src]).then_inc(st.w_in, 16)
                if st.stage == 1:
                    sp.wait_ge(const_set, 1)
                    for par in range(2):
                        load_x(sp, one, 0, par)
            with sp.Fori(1, one.units // 2) as j:
                for par in range(2):
                    load_x(sp, one, j, par)

            sp.wait_ge(k["y"], two.k0)
            for par in range(2):
                load_y(sp, one, 0, par)
            with sp.Fori(1, one.mlp_units // 2) as j:
                for par in range(2):
                    load_y(sp, one, j, par)

            sp.wait_ge(k["y"], two.k0 + two.units)
            sp.dma_start(pw, a["pw"]).then_inc(t_in, 16)
            sp.dma_start(pb, a["pb"]).then_inc(t_in, 16)
            for i in range(2):
                sp.dma_start(wqkv[i], a[f"wqkv{i}"]).then_inc(t_in, 16)
                sp.dma_start(wproj[i], a[f"wproj{i}"]).then_inc(t_in, 16)
            sp.dma_start(wrout, a["wrout"]).then_inc(t_in, 16)
            sp.dma_start(blora, a["blora"]).then_inc(t_in, 16)
            sp.dma_start(qscale[:, 0:1], a["temp"]).then_inc(t_in, 16)
            sp.dma_start(kmask[:, :], a["kmask"]).then_inc(t_in, 16)
            sp.dma_start(vmask, a["vmask"]).then_inc(t_in, 16)
            sp.dma_start(thrice, a["thrice"]).then_inc(t_in, 16)
            for par in range(2):
                load_y(sp, two, 0, par)
            with sp.Fori(1, two.mlp_units // 2) as j:
                for par in range(2):
                    load_y(sp, two, j, par)

            with sp.Fori(0, NG // LANES - 1) as it:
                for ln in lanes:
                    store_group(sp, it, ln)
            for ln in lanes:
                store_group(sp, NG // LANES - 1, ln)
            for ln in lanes:
                sp.wait_ge(ln.res_out, 16 * (NG // LANES + 1))

        def rsqrt(pool, sems_, count, rows, cols):
            pool.wait_ge(sems_["var_eps"], count)
            nc.gpsimd.tensor_tensor(rstd[0:rows, 0:cols], var_eps[0:rows, 0:cols], neg_half[0:rows, 0:cols],
                                    ALU.pow).then_inc(sems_["rstd"], 1)

        def pool_squares(pool, st, j, par):
            n = nth(j, par)
            if st.stage == 1:
                pool.wait_ge(x_in[par], j * 16 + 16)
            else:
                pool.wait_ge(x_made["act"], n + 1)
                pool.wait_ge(x_made["dve"], n + 1)
            if not peeled(j):
                pool.wait_ge(k["main"], NCH * (n + (st.k0 - 1)))
            x, q = ((X1[par], X1q[par]) if st.stage == 1 else (xbuf[par][:, :], xsqbuf[par][:, :]))
            nc.gpsimd.tensor_tensor(q, x, x, ALU.mult).then_inc(k["xsq"], 1)

        def pool_front(pool, st, j, par):
            n = nth(j, par)
            rsqrt(pool, k, n + (st.k0 + 1), st.nt, NCH)
            pool.wait_ge(k["z"], NCH * (n + (st.k0 + 1)))
            pjb = st.pjb[0:st.nt, :].unsqueeze(1).broadcast_to([st.nt, NCH, EMB])
            nc.gpsimd.tensor_tensor(vb[par][0:st.nt, :, :], z[par][0:st.nt, :, V0:V0 + EMB], pjb,
                                    ALU.add).then_inc(k["vb"], 1)

        def pool_back(pool, st, j, par):
            n = nth(j, par)
            pool.wait_ge(k["yn"], n + (st.k0 + 1))
            pool.wait_ge(k["vb"], n + (st.k0 + 1))
            if st.stage == 1:
                dst = y_out1[0:st.nt, bass.ds(j, 1), :, par, :]
            else:
                dst = y_out2[0:st.nt, bass.ds(n, 1), :, :]
            nc.gpsimd.tensor_tensor(dst.rearrange("p o c e -> p (o c) e"), yn[0:st.nt, :, :],
                                    vb[par][0:st.nt, :, :], ALU.add).then_inc(k["y"], 1)

        def pool_performer(pool, st):
            last = st.units // 2 - 1
            pool_squares(pool, st, 0, 0)
            pool_squares(pool, st, 0, 1)
            pool_front(pool, st, 0, 0)
            with pool.Fori(0, last) as j:
                pool_squares(pool, st, j + 1, 0)
                pool_front(pool, st, j, 1)
                pool_back(pool, st, j, 0)
                pool_squares(pool, st, j + 1, 1)
                pool_front(pool, st, j + 1, 0)
                pool_back(pool, st, j, 1)
            pool_front(pool, st, last, 1)
            pool_back(pool, st, last, 0)
            pool_back(pool, st, last, 1)

        def pool_mlp(pool, st):
            with pool.Fori(0, st.mlp_units) as n:
                rsqrt(pool, m, n + (st.m0 + 1), st.nt, 2 * NCH)

        def per_head(x):
            return x.unsqueeze(2).broadcast_to([GT, HEADS, T3])

        @block.gpsimd
        def _(pool):
            for tile, value in ((ones_sq, 1.0), (neg_half, -0.5), (ln_m, -0.5 * float(np.log(M))),
                                (xbuf[0], 0.0), (xbuf[1], 0.0)):
                nc.gpsimd.memset(tile[:, :], value)
            for st in (one, two):
                nc.gpsimd.memset(st.wcat[:, :, ONE:ONE + 1], 0.0)
                nc.gpsimd.memset(st.bias[:, ONE:ONE + 1], 1.0)
            nc.gpsimd.memset(xsqbuf[0][:, 0:1], 0.0).then_inc(const_set, 1)
            nc.gpsimd.memset(late[:, :], 0.0).then_inc(zeroed, 1)
            pool.wait_ge(const_set, 1)
            for st in (one, two):
                pool.wait_ge(st.w_in, 16 * 12)
                pool.wait_ge(const_in, 32)

            pool_performer(pool, one)
            pool_mlp(pool, one)
            pool.wait_ge(m["out"], two.m0)
            nc.gpsimd.memset(y2_all, 0.0).then_inc(zeroed, 1)
            pool.wait_ge(zeroed, 2)
            pool_performer(pool, two)
            for ln in lanes:
                nc.gpsimd.memset(ln.qx, 0.0)
                nc.gpsimd.memset(ln.hnT, 1.0)
                nc.gpsimd.memset(ln.oT, 1.0)
                nc.gpsimd.memset(ln.lg[:, NEXP:2 * NEXP], -HUGE)
                last = nc.gpsimd.memset(ln.rep, -HUGE)
            last.then_inc(lanes_set, 1)
            pool.wait_ge(lanes_set, 1)
            pool_mlp(pool, two)
            pool.wait_ge(t_in, 16 * 12)

            with pool.Fori(0, NG // LANES) as it:
                for att in range(2):
                    for ln in lanes:
                        c = it * (2 * LANES) + (att * LANES + ln.i + 1)
                        pool.wait_ge(u["veps"], c)
                        nc.gpsimd.tensor_tensor(ln.r, ln.veps, neg_half[0:GT, 0:1], ALU.pow).then_inc(u["r"], 1)
                    for ln in lanes:
                        c = it * (2 * LANES) + (att * LANES + ln.i + 1)
                        pool.wait_ge(u["kT"], c)
                        for half in range(2):
                            keys = ln.kT[:, half, :].rearrange("p (i t) -> p i t", i=GI).unsqueeze(2)
                            kept = kmask[:, :].unsqueeze(1).unsqueeze(3)
                            last = nc.gpsimd.tensor_tensor(
                                ln.kx[:, half, :].rearrange("p (i h t) -> p i h t", i=GI, h=6),
                                keys.broadcast_to([HALF, GI, 6, T3]), kept.broadcast_to([HALF, GI, 6, T3]),
                                ALU.mult)
                        last.then_inc(u["kx"], 1)
                    for ln in lanes:
                        c = it * (2 * LANES) + (att * LANES + ln.i + 1)
                        pool.wait_ge(u["mx"], c)
                        nc.gpsimd.tensor_tensor(ln.s1, ln.s0, per_head(ln.mx), ALU.subtract).then_inc(u["sub"], 1)
                    for ln in lanes:
                        c = it * (2 * LANES) + (att * LANES + ln.i + 1)
                        pool.wait_ge(u["exp"], c)
                        if att == 0:
                            g = it * LANES + (ln.i + 1)
                            pool.wait_ge(t["keep"], g)
                            nc.gpsimd.tensor_tensor(ln.s2, ln.s2, ln.keep, ALU.mult).then_inc(t["em"], 1)
                    for ln in lanes:
                        c = it * (2 * LANES) + (att * LANES + ln.i + 1)
                        pool.wait_ge(u["rs"], c)
                        nc.gpsimd.tensor_tensor(ln.s0, ln.s2, per_head(ln.rs), ALU.mult).then_inc(u["p"], 1)

        def gather_ops(copy, dst, src, sides, i):
            for kk, taps in enumerate(TAPS):
                for upper, (kh, kw) in enumerate(taps):
                    end = 2 * sides - 1
                    last = copy(dst(EMB * upper, kk),
                                src[EMB * i:EMB * i + EMB, :, kh:kh + end:2, kw:kw + end:2])
            return last

        def gather_x(eng, copy, done, j, par, i):
            n = nth(j, par)
            if not peeled(j):
                eng.wait_ge(k["main"], NCH * (n + (two.k0 - 1)))
            src = y1_all[:, bass.ds(n * 2, 2), :].rearrange("p n (r c) -> p n r c", c=PAD1)
            x = xbuf[par][:, :].rearrange("p (n i k r c) -> p n i k r c", i=2, k=NTAP, c=S2, n=2)
            gather_ops(copy, lambda row, kk: x[row:row + EMB, :, i, kk, :, :], src, S2, i).then_inc(done, 1)

        def gather_g(copy, it, i):
            pairs = LANES * GI // 2
            src = y2_all[:, bass.ds(it * pairs, pairs), :].rearrange("p n (r c) -> p n r c", c=PAD2)
            x = g_tile.rearrange("p k (n i r c) -> p k n i r c", i=2, c=S3, n=pairs)
            return gather_ops(copy, lambda row, kk: x[row:row + EMB, kk, :, i, :, :], src, S3, i)

        def act_front(act, st, j, par):
            n = nth(j, par)
            act.wait_ge(k["z"], NCH * (n + (st.k0 + 1)))
            act.wait_ge(k["xd"], n + st.k0)
            nc.scalar.activation(kqsq[0:st.nt, :, :, :],
                                 z[par][0:st.nt, :, 0:V0].rearrange("p c (s e) -> p c s e", s=2),
                                 ACT.Square).then_inc(k["kqsq"], 1)
            act.wait_ge(k["arg"], n + (st.k0 + 1))
            if not peeled(j):
                act.wait_ge(k["kvq"], n + (st.k0 - 1))
            nc.scalar.activation(e[par][0:st.nt, :, :, :], arg[0:st.nt, :, :, :], ACT.Exp,
                                 bias=ln_m[0:st.nt, 0:1]).then_inc(k["e"], 1)

        def act_back(act, st, j, par):
            n = nth(j, par)
            act.wait_ge(k["kvq"], n + (st.k0 + 1))
            act.wait_ge(k["yp"], n + st.k0)
            nkv = 1 if st.shared_kv else NCH
            nc.scalar.activation(kv[:, 0:nkv, :], psum[0:EMB + 1, 4, 0:nkv * M].rearrange(
                "p (c m) -> p c m", m=M), ACT.Copy)
            nc.scalar.activation(qT[:, 0:NCH * st.nt], psum[0:M, 5, 0:NCH * st.nt], ACT.Copy
                                 ).then_inc(k["kvq_copied"], 1)
            act.wait_ge(k["mp"], n + (st.k0 + 1))
            nc.scalar.activation(mp[:, 0:nkv, :], psum[0:M, 4, P:P + nkv * (EMB + 1)].rearrange(
                "p (c m) -> p c m", m=EMB + 1), ACT.Copy).then_inc(k["mp_copied"], 1)

        def act_copy(dst, src):
            return nc.scalar.activation(dst, src, ACT.Copy)

        def act_gather(act, st, j, par):
            if st.stage == 2:
                gather_x(act, act_copy, x_made["act"], j, par, 0)

        def act_performer(act, st):
            last = st.units // 2 - 1
            for par in range(2):
                act_gather(act, st, 0, par)
            act_front(act, st, 0, 0)
            with act.Fori(0, last) as j:
                act_gather(act, st, j + 1, 0)
                act_back(act, st, j, 0)
                act_front(act, st, j, 1)
                act_gather(act, st, j + 1, 1)
                act_back(act, st, j, 1)
                act_front(act, st, j + 1, 0)
            act_back(act, st, last, 0)
            act_front(act, st, last, 1)
            act_back(act, st, last, 1)

        def act_square(act, st, j, par):
            n = nth(j, par)
            act.wait_ge(m_in[par], j * 16 + (st.y0 + 16))
            act.wait_ge(m["sum2"], n + st.m0)
            nc.scalar.activation(ysq[0:st.nt, :, :], yfix[par][0:st.nt, :, :].rearrange(
                "p c (i e) -> p (c i) e", i=2), ACT.Square).then_inc(m["sq"], 1)

        def act_turned(act, st, j, par):
            n = nth(j, par)
            act.wait_ge(m["tr"], n + (st.m0 + 1))
            act.wait_ge(m["w1"], n + st.m0)
            nc.scalar.activation(ynT[:, 0:st.columns], psum[:, par, 0:st.columns], ACT.Copy
                                 ).then_inc(m["tr_copied"], 1)

        def act_gelu(act, st, j, par):
            n = nth(j, par)
            act.wait_ge(m["w1"], n + (st.m0 + 1))
            act.wait_ge(m["w2"], n + st.m0)
            nc.scalar.activation(gel[:, 0:st.columns], psum[:, 2 + par, 0:st.columns], ACT.Gelu,
                                 bias=st.b1c[:, 0:1]).then_inc(m["gelu"], 1)

        def act_mlp(act, st):
            last = st.mlp_units // 2 - 1
            act.wait_ge(w["mlp_set"], st.w0 + 1)
            act_square(act, st, 0, 0)
            act_turned(act, st, 0, 0)
            with act.Fori(0, last) as j:
                act_square(act, st, j, 1)
                act_gelu(act, st, j, 0)
                act_turned(act, st, j, 1)
                act_square(act, st, j + 1, 0)
                act_gelu(act, st, j, 1)
                act_turned(act, st, j + 1, 0)
            act_square(act, st, last, 1)
            act_gelu(act, st, last, 0)
            act_turned(act, st, last, 1)
            act_gelu(act, st, last, 1)

        @block.scalar
        def _(act):
            act.wait_ge(const_set, 1)
            act_performer(act, one)
            act_mlp(act, one)
            act.wait_ge(m["out"], two.m0)
            act_performer(act, two)
            act_mlp(act, two)
            act.wait_ge(scale_set, 1)
            act.wait_ge(lanes_set, 1)
            act.wait_ge(m["out"], two.m0 + two.mlp_units)
            with act.Fori(0, NG // LANES) as it:
                act.wait_ge(t["hp"], it * LANES + 1)
                for i in range(2):
                    last = gather_g(act_copy, it, i)
                last.then_inc(t["g"], 1)
                for att in range(2):
                    for ln in lanes:
                        c = it * (2 * LANES) + (att * LANES + ln.i + 1)
                        act.wait_ge(u["tr"], c)
                        nc.scalar.activation(ln.hnT[0:HALF, :, :], psum[0:HALF, 4 * ln.i + 1, 0:2 * GT].rearrange(
                            "p (u t) -> p u t", u=2), ACT.Copy).then_inc(u["hnT"], 1)
                    if att == 1:
                        for ln in lanes:
                            g = it * LANES + (ln.i + 1)
                            act.wait_ge(t["lm"], g)
                            nc.scalar.activation(ln.le, ln.lm, ACT.Exp).then_inc(t["le"], 1)
                        for ln in lanes:
                            g = it * LANES + (ln.i + 1)
                            act.wait_ge(t["at"], g)
                            nc.scalar.activation(ln.aT, psum[:, 4 * ln.i + 1, 0:GT], ACT.Copy).then_inc(t["aT"], 1)
                    for ln in lanes:
                        c = it * (2 * LANES) + (att * LANES + ln.i + 1)
                        act.wait_ge(u["qk"], c)
                        blocks = bass.AP(ln.qx.tensor, ln.qx.offset, [list(ln.qx.ap[0]), [GI * GT, 2],
                                                                      [GT + T3, GI], [1, T3]])
                        nc.scalar.activation(blocks, psum[0:HALF, 4 * ln.i + 2, 0:2 * GT].rearrange(
                            "p (u i t) -> p u i t", u=2, i=GI), ACT.Copy, scale=qscale[:, 2 + att:3 + att])
                        nc.scalar.activation(ln.kT, psum[0:HALF, 4 * ln.i + 2, 2 * GT:4 * GT].rearrange(
                            "p (u t) -> p u t", u=2), ACT.Copy).then_inc(u["kT"], 1)
                    for ln in lanes:
                        c = it * (2 * LANES) + (att * LANES + ln.i + 1)
                        act.wait_ge(u["v"], c)
                        nc.scalar.activation(ln.vt, psum[0:GT, 4 * ln.i, 0:D], ACT.Copy).then_inc(u["vt"], 1)
                    for ln in lanes:
                        c = it * (2 * LANES) + (att * LANES + ln.i + 1)
                        act.wait_ge(u["s"], c)
                        nc.scalar.activation(ln.s0, psum[0:GT, 4 * ln.i + 1, 0:HEADS * T3].rearrange(
                            "p (h t) -> p h t", h=HEADS), ACT.Copy).then_inc(u["h"], 1)
                    for ln in lanes:
                        c = it * (2 * LANES) + (att * LANES + ln.i + 1)
                        act.wait_ge(u["sub"], c)
                        if att == 0:
                            act.wait_ge(t["keep"], it * LANES + (ln.i + 1))
                        nc.scalar.activation(ln.s2, ln.s1, ACT.Exp).then_inc(u["exp"], 1)
                    for ln in lanes:
                        c = it * (2 * LANES) + (att * LANES + ln.i + 1)
                        act.wait_ge(u["pt"], c)
                        nc.scalar.activation(ln.pT, psum[0:GT, 4 * ln.i + 3, 0:TRI * GT], ACT.Copy
                                             ).then_inc(u["pT"], 1)
                    for ln in lanes:
                        c = it * (2 * LANES) + (att * LANES + ln.i + 1)
                        act.wait_ge(u["o"], c)
                        nc.scalar.activation(ln.oT[0:3 * HD, :], psum[0:3 * HD, 4 * ln.i + 2, 0:TRI * GT], ACT.Copy
                                             ).then_inc(u["oT"], 1)

        def plain(dve):
            nc.vector.memset(scratch[0:1, 0:1], 0.0)

        def dve_prepare(dve, st):
            c0 = st.w0 + 1
            dve.wait_ge(st.w_in, 16 * 12)
            for c in range(st.nk):
                last = nc.vector.tensor_scalar(st.wcat[:, c, 0:C3], st.wraw[:, c, :], st.gcol[:, c:c + 1], None, ALU.mult)
                last = nc.vector.tensor_scalar(wide[0:st.kp, c, :], ones_sq[0:st.kp, :], st.bcol[:, c:c + 1], None, ALU.mult)
                last = nc.vector.tensor_copy(st.wcat[:, c, MEAN:MEAN + 1], st.inv[:, c:c + 1])
            last.then_inc(w["scaled"], 1)
            dve.wait_ge(w["summed"], c0)
            dve.wait_ge(w["scaled"], c0)
            for c in range(st.nk):
                last = nc.vector.scalar_tensor_tensor(out=st.wcat[:, c, 0:C3], in0=psum[0:st.kp, 0, 0:C3],
                                                      scalar=st.ninv[:, c:c + 1], in1=st.wcat[:, c, 0:C3],
                                                      op0=ALU.mult, op1=ALU.add)
            last.then_inc(w["centered"], 1)
            dve.wait_ge(w["biased"], c0)
            nc.vector.tensor_tensor(st.bias[:, 0:C3], psum[:, 1, 0:C3], st.kqvb[:, :], ALU.add).then_inc(w["bias_set"], 1)
            for c in range(st.nk + 1):
                rows = st.kp if c < st.nk else P
                step = st.t0 + c + 1
                dve.wait_ge(w["turned"], step)
                nc.vector.tensor_copy(turned[:, :, 0:rows], psum[0:EMB, 2, 0:2 * rows].rearrange(
                    "p (s r) -> p s r", s=2)).then_inc(w["turned_copied"], 1)
                dve.wait_ge(w["folded"], step)
                dst = st.wcat[:, c, WK:WK + 2 * M] if c < st.nk else st.bias[:, WK:WK + 2 * M]
                nc.vector.tensor_copy(dst, psum[0:rows, 3, 0:2 * M]).then_inc(w["folded_copied"], 1)
            nc.vector.tensor_scalar(st.w1c[:, :], st.w1[:, :], st.cols[:, 0:1], None, ALU.mult).then_inc(w["mlp_scaled"], 1)
            dve.wait_ge(w["mlp_summed"], c0)
            dve.wait_ge(w["mlp_scaled"], c0)
            nc.vector.tensor_tensor(st.w1c[:, :], st.w1c[:, :], psum[:, 0, 0:P], ALU.subtract)
            nc.vector.tensor_tensor(st.b1c[:, :], psum[:, 1, 0:1], st.cols[:, 2:3], ALU.add).then_inc(w["mlp_set"], 1)

        def dve_front(dve, st, j, par):
            n = nth(j, par)
            c = n + (st.k0 + 1)
            nt = st.nt
            dve.wait_ge(k["main"], NCH * c)
            nc.vector.tensor_copy(stat[0:nt, :, :], psum[0:nt, 0:NCH, MEAN:SQ + 1]).then_inc(k["stat"], 1)
            dve.wait_ge(k["stat"], c)
            nc.vector.tensor_tensor(sqm[0:nt, 0:NCH], stat[0:nt, :, 0], stat[0:nt, :, 0], ALU.mult
                                    ).then_inc(k["square_mean"], 1)
            dve.wait_ge(k["square_mean"], c)
            nc.vector.tensor_tensor(var[0:nt, 0:NCH], stat[0:nt, :, 1], sqm[0:nt, 0:NCH], ALU.subtract
                                    ).then_inc(k["var"], 1)
            dve.wait_ge(k["var"], c)
            nc.vector.tensor_scalar(var_eps[0:nt, 0:NCH], var[0:nt, 0:NCH], 0.0, EPS, ALU.max, ALU.add
                                    ).then_inc(k["var_eps"], 1)
            dve.wait_ge(k["rstd"], c)
            if not peeled(j):
                dve.wait_ge(k["kvq"], n + (st.k0 - 1))
                dve.wait_ge(k["vb"], n + (st.k0 - 1))
            for i in range(NCH):
                nc.vector.scalar_tensor_tensor(out=z[par][0:nt, i, :], in0=psum[0:nt, i, 0:MEAN],
                                               scalar=rstd[0:nt, i:i + 1], in1=st.bias[0:nt, :],
                                               op0=ALU.mult, op1=ALU.add).then_inc(k["z"], 1)
            dve.wait_ge(k["kqsq"], c)
            nc.vector.tensor_reduce(xd[0:nt, :, :], kqsq[0:nt, :, :, :], AX_X, ALU.add).then_inc(k["xd"], 1)
            dve.wait_ge(k["xd"], c)
            dve.wait_ge(k["e"], n + st.k0)
            nc.vector.scalar_tensor_tensor(out=arg[0:nt, :, :, :],
                                           in0=xd[0:nt, :, :].unsqueeze(3).broadcast_to([nt, NCH, 2, M]),
                                           scalar=-0.5, in1=z[par][0:nt, :, WK:WK + 2 * M].rearrange(
                                               "p c (s m) -> p c s m", s=2),
                                           op0=ALU.mult, op1=ALU.add).then_inc(k["arg"], 1)

        def dve_back(dve, st, j, par):
            n = nth(j, par)
            c = n + (st.k0 + 1)
            nt = st.nt
            yp = psum[0:nt, 6, 0:NCH * (EMB + 1)].rearrange("p (c e) -> p c e", c=NCH)
            dve.wait_ge(k["yp"], c)
            nc.vector.tensor_scalar(den[0:nt, :], yp[:, :, EMB], 1e-8, None, ALU.add).then_inc(k["den"], 1)
            dve.wait_ge(k["den"], c)
            nc.vector.reciprocal(rec[0:nt, :], den[0:nt, :]).then_inc(k["rec"], 1)
            dve.wait_ge(k["rec"], c)
            dve.wait_ge(k["y"], n + st.k0)
            nc.vector.tensor_tensor(yn[0:nt, :, :], yp[:, :, 0:EMB],
                                    rec[0:nt, :].unsqueeze(2).broadcast_to([nt, NCH, EMB]), ALU.mult
                                    ).then_inc(k["yn"], 1)

        def dve_gather(dve, st, j, par):
            if st.stage == 2:
                gather_x(dve, nc.vector.tensor_copy, x_made["dve"], j, par, 1)

        def dve_performer(dve, st):
            last = st.units // 2 - 1
            for par in range(2):
                dve_gather(dve, st, 0, par)
            dve_front(dve, st, 0, 0)
            with dve.Fori(0, last) as j:
                dve_gather(dve, st, j + 1, 0)
                dve_front(dve, st, j, 1)
                dve_back(dve, st, j, 0)
                dve_gather(dve, st, j + 1, 1)
                dve_front(dve, st, j + 1, 0)
                dve_back(dve, st, j, 1)
            dve_front(dve, st, last, 1)
            dve_back(dve, st, last, 0)
            dve_back(dve, st, last, 1)

        def dve_norm(dve, st, j, par):
            n = nth(j, par)
            c = n + (st.m0 + 1)
            nt = st.nt
            rows = yfix[par][0:nt, :, :].rearrange("p c (i e) -> p (c i) e", i=2)
            dve.wait_ge(m_in[par], j * 16 + (st.y0 + 16))
            nc.vector.tensor_reduce(sum1[0:nt, :], rows, AX_X, ALU.add).then_inc(m["sum1"], 1)
            dve.wait_ge(m["sq"], c)
            nc.vector.tensor_reduce(sum2[0:nt, :], ysq[0:nt, :, :], AX_X, ALU.add).then_inc(m["sum2"], 1)
            dve.wait_ge(m["sum1"], c)
            nc.vector.scalar_tensor_tensor(out=sqm[0:nt, :], in0=sum1[0:nt, :], scalar=1.0 / (EMB * EMB),
                                           in1=sum1[0:nt, :], op0=ALU.mult, op1=ALU.mult).then_inc(m["square_mean"], 1)
            dve.wait_ge(m["sum2"], c)
            dve.wait_ge(m["square_mean"], c)
            nc.vector.scalar_tensor_tensor(out=var[0:nt, :], in0=sum2[0:nt, :], scalar=1.0 / EMB,
                                           in1=sqm[0:nt, :], op0=ALU.mult, op1=ALU.subtract).then_inc(m["var"], 1)
            dve.wait_ge(m["var"], c)
            nc.vector.tensor_scalar(var_eps[0:nt, 0:2 * NCH], var[0:nt, 0:2 * NCH], 0.0, EPS, ALU.max, ALU.add
                                    ).then_inc(m["var_eps"], 1)
            dve.wait_ge(m["rstd"], c)
            dve.wait_ge(m["tr"], n + st.m0)
            nc.vector.tensor_tensor(ynm[0:nt, :, :].rearrange("p c (i e) -> p (c i) e", i=2), rows,
                                    rstd[0:nt, :].unsqueeze(2).broadcast_to([nt, 2 * NCH, EMB]), ALU.mult
                                    ).then_inc(m["yn"], 1)

        def dve_out(dve, st, j, par):
            n = nth(j, par)
            dve.wait_ge(m["w2"], n + (st.m0 + 1))
            src = psum[:, 4 + par, 0:st.columns]
            if st.stage == 1:
                dst = y1_all[:, bass.ds(n, 1), :].rearrange("p o (r c) -> p (o r) c", c=PAD1)[:, 1:1 + S1, 1:1 + S1]
                src = src.rearrange("p (r c) -> p r c", c=S1)
            else:
                dst = y2_all[:, bass.ds(n * NCH, NCH), :].rearrange("p n (r c) -> p n r c", c=PAD2
                                                                    )[:, :, 1:1 + S2, 1:1 + S2]
                src = src.rearrange("p (n r c) -> p n r c", n=NCH, c=S2)
            nc.vector.tensor_scalar(dst, src, st.cols[:, 3:4], None, ALU.add).then_inc(m["out"], 1)

        def dve_mlp(dve, st):
            last = st.mlp_units // 2 - 1
            dve_norm(dve, st, 0, 0)
            with dve.Fori(0, last) as j:
                dve_norm(dve, st, j, 1)
                dve_out(dve, st, j, 0)
                dve_norm(dve, st, j + 1, 0)
                dve_out(dve, st, j, 1)
            dve_norm(dve, st, last, 1)
            dve_out(dve, st, last, 0)
            dve_out(dve, st, last, 1)

        @block.vector
        def _(dve):
            dve.wait_ge(const_set, 1)
            dve_prepare(dve, one)
            dve_prepare(dve, two)
            dve_performer(dve, one)
            dve.wait_ge(zeroed, 1)
            dve_mlp(dve, one)
            dve.wait_ge(m["out"], two.m0)
            dve_performer(dve, two)
            dve.wait_ge(zeroed, 2)
            dve_mlp(dve, two)
            dve.wait_ge(t_in, 16 * 12)
            nc.vector.tensor_scalar(qscale[:, 1:2], qscale[:, 0:1], 0.01, None, ALU.max).then_inc(clipped, 1)
            dve.wait_ge(clipped, 1)
            nc.vector.reciprocal(qscale[:, 2:3], qscale[:, 1:2]).then_inc(clipped, 1)
            nc.vector.memset(qscale[:, 3:4], HD ** -0.5)
            dve.wait_ge(clipped, 2)
            nc.vector.tensor_scalar(qscale[:, 2:3], qscale[:, 2:3], HD ** -0.5, None, ALU.mult).then_inc(scale_set, 1)

            with dve.Fori(0, NG // LANES) as it:
                for ln in lanes:
                    g = it * LANES + (ln.i + 1)
                    dve.wait_ge(t["hp"], g + 1)
                    nc.vector.tensor_tensor(ln.h, psum[0:GT, 4 * ln.i, 0:D], pb[0:GT, :], ALU.add).then_inc(t["h"], 1)
                for att in range(2):
                    for ln in lanes:
                        c = it * (2 * LANES) + (att * LANES + ln.i + 1)
                        g = it * LANES + (ln.i + 1)
                        if att == 0:
                            dve.wait_ge(t["h"], g)
                        else:
                            dve.wait_ge(t["s0"], g)
                        nc.vector.bn_stats(ln.bn, ln.h).then_inc(u["bn"], 1)
                        dve.wait_ge(u["bn"], c)
                        plain(dve)
                        nc.vector.bn_aggr(ln.mv, ln.bn).then_inc(u["mv"], 1)
                        dve.wait_ge(u["mv"], c)
                        nc.vector.tensor_scalar(ln.veps, ln.mv[:, 1:2], 0.0, EPS, ALU.max, ALU.add
                                                ).then_inc(u["veps"], 1)
                    for ln in lanes:
                        c = it * (2 * LANES) + (att * LANES + ln.i + 1)
                        dve.wait_ge(u["r"], c)
                        nc.vector.tensor_scalar(ln.hn, ln.h, ln.mv[:, 0:1], ln.r, ALU.subtract, ALU.mult
                                                ).then_inc(u["hn"], 1)
                    if att == 1:
                        for ln in lanes:
                            g = it * LANES + (ln.i + 1)
                            rt = psum[0:GT, 4 * ln.i, D:D + NEXP + P]
                            dve.wait_ge(t["rt"], g)
                            nc.vector.tensor_copy(ln.lg[:, 0:NEXP], rt[:, 0:NEXP]).then_inc(t["lg"], 1)
                            dve.wait_ge(t["lg"], g)
                            plain(dve)
                            nc.vector.max(out=ln.l8, in_=ln.lg[:, 0:NEXP]).then_inc(t["l8"], 1)
                            dve.wait_ge(t["l8"], g)
                            nc.vector.tensor_copy(ln.rep[:, 0:TOP_K], ln.l8[:, 0:TOP_K]).then_inc(t["rep"], 1)
                            nc.vector.tensor_scalar(ln.lm, ln.lg[:, 0:NEXP], ln.l8[:, 0:1], None, ALU.subtract
                                                    ).then_inc(t["lm"], 1)
                            dve.wait_ge(t["rep"], g)
                            plain(dve)
                            nc.vector.match_replace(out=ln.lg2, in_to_replace=ln.rep, in_values=ln.lg,
                                                    imm_value=HUGE).then_inc(t["found"], 1)
                            dve.wait_ge(t["found"], g)
                            nc.vector.tensor_scalar(ln.sel, ln.lg2[:, 0:NEXP], HUGE, ALPHA / RANK, ALU.is_ge,
                                                    ALU.mult).then_inc(t["sel"], 1)
                        for ln in lanes:
                            g = it * LANES + (ln.i + 1)
                            rt = psum[0:GT, 4 * ln.i, D:D + NEXP + P]
                            dve.wait_ge(t["le"], g)
                            nc.vector.tensor_reduce(ln.ls, ln.le, AX_X, ALU.add).then_inc(t["lr"], 1)
                            dve.wait_ge(t["lr"], it * (2 * LANES) + (2 * ln.i + 1))
                            nc.vector.reciprocal(ln.lr, ln.ls).then_inc(t["lr"], 1)
                            dve.wait_ge(t["sel"], g)
                            nc.vector.tensor_tensor(ln.lw, ln.le, ln.sel, ALU.mult).then_inc(t["lw"], 1)
                            dve.wait_ge(t["lr"], it * (2 * LANES) + (2 * ln.i + 2))
                            dve.wait_ge(t["lw"], g)
                            nc.vector.tensor_scalar(ln.lw2, ln.lw, ln.lr, None, ALU.mult).then_inc(t["lw2"], 1)
                            dve.wait_ge(t["lw2"], g)
                            nc.vector.tensor_tensor(
                                ln.aw.rearrange("p (n r) -> p n r", r=RANK),
                                rt[:, NEXP:NEXP + P].rearrange("p (n r) -> p n r", r=RANK),
                                ln.lw2.unsqueeze(2).broadcast_to([GT, NEXP, RANK]), ALU.mult).then_inc(t["aw"], 1)
                    for ln in lanes:
                        c = it * (2 * LANES) + (att * LANES + ln.i + 1)
                        dve.wait_ge(u["v3"], c)
                        nc.vector.tensor_tensor(ln.vx[:, 0:2, :], psum[0:GT, 4 * ln.i + 3, 0:2 * D].rearrange(
                            "p (i f) -> p i f", i=2), vmask[:, :].unsqueeze(1).broadcast_to([GT, 2, D]), ALU.mult)
                        nc.vector.tensor_tensor(ln.vx[:, 2, :], psum[0:GT, 4 * ln.i, 0:D], vmask[:, :], ALU.mult
                                                ).then_inc(u["vx"], 1)
                    for ln in lanes:
                        c = it * (2 * LANES) + (att * LANES + ln.i + 1)
                        g = it * LANES + (ln.i + 1)
                        dve.wait_ge(u["h"], c)
                        if att == 1:
                            nc.vector.tensor_reduce(ln.mx, ln.s0, AX_X, ALU.max).then_inc(u["mx"], 1)
                            continue
                        plain(dve)
                        tops = it * (5 * LANES) + (5 * ln.i)
                        for hd in range(HEADS):
                            last = nc.vector.max(out=ln.top[0][:, hd, :], in_=ln.s0[:, hd, :])
                        last.then_inc(t["top8"], 1)
                        dve.wait_ge(t["top8"], tops + 1)
                        nc.vector.tensor_copy(ln.mx, ln.top[0][:, :, 0]).then_inc(u["mx"], 1)
                        for hd in range(HEADS):
                            last = nc.vector.match_replace(out=ln.s2[:, hd, :], in_to_replace=ln.top[0][:, hd, :],
                                                           in_values=ln.s0[:, hd, :], imm_value=-HUGE)
                        last.then_inc(t["top8"], 1)
                        dve.wait_ge(t["top8"], tops + 2)
                        plain(dve)
                        for hd in range(HEADS):
                            last = nc.vector.max(out=ln.top[1][:, hd, :], in_=ln.s2[:, hd, :])
                        last.then_inc(t["top8"], 1)
                        dve.wait_ge(t["top8"], tops + 3)
                        plain(dve)
                        for hd in range(HEADS):
                            last = nc.vector.match_replace(out=ln.keep[:, hd, :], in_to_replace=ln.top[1][:, hd, :],
                                                           in_values=ln.s2[:, hd, :], imm_value=-HUGE)
                        last.then_inc(t["top8"], 1)
                        dve.wait_ge(t["top8"], tops + 4)
                        plain(dve)
                        for hd in range(HEADS):
                            last = nc.vector.max(out=ln.top[2][:, hd, :], in_=ln.keep[:, hd, :])
                        last.then_inc(t["top8"], 1)
                        dve.wait_ge(t["top8"], tops + 5)
                        nc.vector.tensor_tensor(ln.keep, ln.s0, per_head(ln.top[2][:, :, KEEP - 17]), ALU.is_ge
                                                ).then_inc(t["keep"], 1)
                    for ln in lanes:
                        c = it * (2 * LANES) + (att * LANES + ln.i + 1)
                        if att == 0:
                            dve.wait_ge(t["em"], it * LANES + (ln.i + 1))
                        else:
                            dve.wait_ge(u["exp"], c)
                        nc.vector.tensor_reduce(ln.sm, ln.s2, AX_X, ALU.add).then_inc(u["sum"], 1)
                        dve.wait_ge(u["sum"], c)
                        nc.vector.reciprocal(ln.rs, ln.sm).then_inc(u["rs"], 1)
                    for ln in lanes:
                        c = it * (2 * LANES) + (att * LANES + ln.i + 1)
                        dve.wait_ge(u["pj"], c)
                        pj = psum[0:GT, 4 * ln.i, 0:D]
                        if att == 0:
                            nc.vector.tensor_tensor(ln.h, ln.h, pj, ALU.add).then_inc(t["s0"], 1)
                        else:
                            dve.wait_ge(ln.res_out, it * 16 + 16)
                            nc.vector.tensor_tensor(ln.res, ln.h, pj, ALU.add).then_inc(ln.res_ready, 1)

        def pe_prepare(pe, st):
            c0 = st.w0 + 1
            pe.wait_ge(w["scaled"], c0)
            if st.w0:
                pe.wait_ge(w["mlp_set"], st.w0)
            for c in range(st.nk):
                last = nc.tensor.matmul(psum[:, 0, 0:C3], ones_sq[0:st.kp, :], st.wcat[:, c, 0:C3],
                                        start=(c == 0), stop=(c == st.nk - 1))
            last.then_inc(w["summed"], 1)
            for c in range(st.nk):
                last = nc.tensor.matmul(psum[:, 1, 0:C3], wide[0:st.kp, c, :], st.wraw[:, c, :],
                                        start=(c == 0), stop=(c == st.nk - 1))
            last.then_inc(w["biased"], 1)
            pe.wait_ge(w["centered"], c0)
            pe.wait_ge(w["bias_set"], c0)
            for c in range(st.nk + 1):
                rows = st.kp if c < st.nk else P
                step = st.t0 + c
                src = st.wcat[:, c, :] if c < st.nk else st.bias[:, :]
                if step:
                    pe.wait_ge(w["folded_copied"], step)
                for s in range(2):
                    last = nc.tensor.transpose(psum[0:EMB, 2, s * rows:(s + 1) * rows],
                                               src[:, EMB * s:EMB * s + EMB], ident[0:rows, 0:rows])
                last.then_inc(w["turned"], 1)
                pe.wait_ge(w["turned_copied"], step + 1)
                for s in range(2):
                    last = nc.tensor.matmul(psum[0:rows, 3, M * s:M * s + M], turned[:, s, 0:rows], st.wT[:, :],
                                            start=True, stop=True)
                last.then_inc(w["folded"], 1)
            pe.wait_ge(w["mlp_scaled"], c0)
            nc.tensor.matmul(psum[:, 0, 0:P], blockmean[:, :], st.w1c[:, :], start=True, stop=True)
            nc.tensor.matmul(psum[:, 1, 0:1], st.w1[:, :], st.cols[:, 1:2], start=True, stop=True
                             ).then_inc(w["mlp_summed"], 1)

        def pe_main(pe, st, j, par, c):
            n = nth(j, par)
            if c == 0:
                pe.wait_ge(k["xsq"], n + (st.k0 + 1))
            pe.wait_ge(k["z"], NCH * (n + (st.k0 - 1)) + (c + 1))
            for kk in range(st.nk):
                rows = krows(st, kk)
                nc.tensor.matmul(psum[0:st.nt, c, 0:MEAN + 1], patches(st, xbuf[par], c, kk),
                                 st.wcat[0:rows, kk, :], start=(kk == 0), stop=(kk == st.nk - 1))
            for kk in range(st.nk):
                rows = krows(st, kk)
                last = nc.tensor.matmul(psum[0:st.nt, c, SQ:SQ + 1], patches(st, xsqbuf[par], c, kk),
                                        st.inv[0:rows, kk:kk + 1], start=(kk == 0), stop=(kk == st.nk - 1))
            last.then_inc(k["main"], 1)

        def pe_kvq(pe, st, j, par):
            n = nth(j, par)
            pe.wait_ge(k["e"], n + (st.k0 + 1))
            pe.wait_ge(k["mp_copied"], n + st.k0)
            for c in range(NCH):
                rows = st.real[c]
                kc = 0 if st.shared_kv else c
                nc.tensor.matmul(psum[0:EMB + 1, 4, M * kc:M * kc + M], z[par][0:rows, c, V0:ONE + 1],
                                 e[par][0:rows, c, 0, :], start=(c == 0 or not st.shared_kv),
                                 stop=(c == NCH - 1 or not st.shared_kv))
            for c in range(NCH):
                last = nc.tensor.transpose(psum[0:M, 5, st.nt * c:st.nt * c + st.nt], e[par][0:st.nt, c, 1, :],
                                           ident[0:st.nt, 0:st.nt])
            last.then_inc(k["kvq"], 1)

        def pe_mp(pe, st, j, par):
            n = nth(j, par)
            pe.wait_ge(k["kvq_copied"], n + (st.k0 + 1))
            for c in range(1 if st.shared_kv else NCH):
                last = nc.tensor.matmul(psum[0:M, 4, P + (EMB + 1) * c:P + (EMB + 1) * (c + 1)], kv[:, c, :],
                                        st.paug[:, :], start=True, stop=True)
            last.then_inc(k["mp"], 1)

        def pe_y(pe, st, j, par):
            n = nth(j, par)
            pe.wait_ge(k["mp_copied"], n + (st.k0 + 1))
            pe.wait_ge(k["yn"], n + st.k0)
            for c in range(NCH):
                last = nc.tensor.matmul(psum[0:st.nt, 6, (EMB + 1) * c:(EMB + 1) * (c + 1)],
                                        qT[:, st.nt * c:st.nt * c + st.nt], mp[:, 0 if st.shared_kv else c, :],
                                        start=True, stop=True)
            last.then_inc(k["yp"], 1)

        def pe_performer(pe, st):
            last = st.units // 2 - 1
            for par in range(2):
                for c in range(NCH):
                    pe_main(pe, st, 0, par, c)
            with pe.Fori(1, last + 1) as j:
                for par in range(2):
                    pe_main(pe, st, j, par, 0)
                    pe_kvq(pe, st, j - 1, par)
                    pe_main(pe, st, j, par, 1)
                    pe_mp(pe, st, j - 1, par)
                    pe_main(pe, st, j, par, 2)
                    pe_y(pe, st, j - 1, par)
                    pe_main(pe, st, j, par, 3)
            for par in range(2):
                pe_kvq(pe, st, last, par)
                pe_mp(pe, st, last, par)
                pe_y(pe, st, last, par)

        def pe_turn(pe, st, j, par):
            n = nth(j, par)
            pe.wait_ge(m["yn"], n + (st.m0 + 1))
            at = 0
            for c in range(NCH):
                rows = st.real[c]
                last = nc.tensor.transpose(psum[:, par, at:at + rows], ynm[0:rows, c, :], ident[0:rows, 0:rows])
                at += rows
            last.then_inc(m["tr"], 1)

        def pe_w1(pe, st, j, par):
            n = nth(j, par)
            pe.wait_ge(m["tr_copied"], n + (st.m0 + 1))
            nc.tensor.matmul(psum[:, 2 + par, 0:st.columns], st.w1c[:, :], ynT[:, 0:st.columns],
                             start=True, stop=True).then_inc(m["w1"], 1)

        def pe_w2(pe, st, j, par):
            n = nth(j, par)
            pe.wait_ge(m["gelu"], n + (st.m0 + 1))
            nc.tensor.matmul(psum[:, 4 + par, 0:st.columns], st.w2[:, :], gel[:, 0:st.columns],
                             start=True, stop=False)
            at = 0
            for c in range(NCH):
                rows = st.real[c]
                last = nc.tensor.matmul(psum[:, 4 + par, at:at + rows], yfix[par][0:rows, c, :],
                                        ident[0:rows, 0:rows], start=False, stop=(c == NCH - 1))
                at += rows
            last.then_inc(m["w2"], 1)

        def pe_mlp(pe, st):
            last = st.mlp_units // 2 - 1
            pe_turn(pe, st, 0, 0)
            with pe.Fori(0, last) as j:
                pe_w1(pe, st, j, 0)
                pe_turn(pe, st, j, 1)
                pe_w2(pe, st, j, 0)
                pe_w1(pe, st, j, 1)
                pe_turn(pe, st, j + 1, 0)
                pe_w2(pe, st, j, 1)
            pe_w1(pe, st, last, 0)
            pe_turn(pe, st, last, 1)
            pe_w2(pe, st, last, 0)
            pe_w1(pe, st, last, 1)
            pe_w2(pe, st, last, 1)

        @block.tensor
        def _(pe):
            pe.wait_ge(const_in, 32)
            pe.wait_ge(const_set, 1)
            pe_prepare(pe, one)
            pe_prepare(pe, two)
            pe.wait_ge(w["folded_copied"], one.nk + two.nk + 2)
            pe.wait_ge(w["mlp_set"], 2)
            pe_performer(pe, one)
            pe_mlp(pe, one)
            pe_performer(pe, two)
            pe_mlp(pe, two)
            pe.wait_ge(t_in, 16 * 12)
            pe.wait_ge(m["out"], two.m0 + two.mlp_units)

            with pe.Fori(0, NG // LANES) as it:
                for ln in lanes:
                    pe.wait_ge(t["g"], it + 1)
                    pe.wait_ge(ln.res_ready, it + 1)
                    for kk in range(NTAP):
                        rows = EMB * len(TAPS[kk])
                        last = nc.tensor.matmul(psum[0:GT, 4 * ln.i, 0:D], g_tile[0:rows, kk, GT * ln.i:GT * ln.i + GT],
                                                pw[0:rows, kk, :], start=(kk == 0), stop=(kk == NTAP - 1))
                    last.then_inc(t["hp"], 1)
                for att in range(2):
                    w_qkv, w_proj = wqkv[att], wproj[att]
                    for ln in lanes:
                        c = it * (2 * LANES) + (att * LANES + ln.i + 1)
                        pe.wait_ge(u["hn"], c)
                        for half in range(2):
                            last = nc.tensor.transpose(psum[0:HALF, 4 * ln.i + 1, GT * half:GT * half + GT],
                                                       ln.hn[:, HALF * half:HALF * half + HALF], ident[0:GT, 0:GT])
                        last.then_inc(u["tr"], 1)
                    if att == 1:
                        for ln in lanes:
                            c = it * (2 * LANES) + (att * LANES + ln.i + 1)
                            pe.wait_ge(u["hnT"], c)
                            dst = psum[0:GT, 4 * ln.i, D:D + NEXP + P]
                            nc.tensor.matmul(dst, ln.hnT[:, 0, :], wrout[:, 0, :], start=True, stop=False)
                            nc.tensor.matmul(dst, ln.hnT[0:HALF, 1, :], wrout[0:HALF, 1, :], start=False, stop=True
                                             ).then_inc(t["rt"], 1)
                    for ln in lanes:
                        c = it * (2 * LANES) + (att * LANES + ln.i + 1)
                        g = it * LANES + (ln.i + 1)
                        pe.wait_ge(u["hnT"], c)
                        if att == 1:
                            pe.wait_ge(t["aw"], g)
                            nc.tensor.transpose(psum[:, 4 * ln.i + 1, 0:GT], ln.aw, ident[0:GT, 0:GT]).then_inc(t["at"], 1)
                            pe.wait_ge(t["aT"], g)
                        for part in range(4):
                            dst = psum[0:HALF, 4 * ln.i + 2, GT * part:GT * part + GT]
                            cols = slice(HALF * part, HALF * part + HALF)
                            nc.tensor.matmul(dst, w_qkv[:, 0, cols], ln.hnT[:, 0, :], start=True, stop=False)
                            last = nc.tensor.matmul(dst, w_qkv[0:HALF, 1, cols], ln.hnT[0:HALF, 1, :],
                                                    start=False, stop=(att == 0))
                            if att == 1:
                                last = nc.tensor.matmul(dst, blora[:, cols], ln.aT, start=False, stop=True)
                        last.then_inc(u["qk"], 1)
                        dst = psum[0:GT, 4 * ln.i, 0:D]
                        cols = slice(2 * D, 3 * D)
                        nc.tensor.matmul(dst, ln.hnT[:, 0, :], w_qkv[:, 0, cols], start=True, stop=False)
                        last = nc.tensor.matmul(dst, ln.hnT[0:HALF, 1, :], w_qkv[0:HALF, 1, cols],
                                                start=False, stop=(att == 0))
                        if att == 1:
                            last = nc.tensor.matmul(dst, ln.aT, blora[:, cols], start=False, stop=True)
                        last.then_inc(u["v"], 1)
                    for ln in lanes:
                        c = it * (2 * LANES) + (att * LANES + ln.i + 1)
                        pe.wait_ge(u["vt"], c)
                        for i in range(GI):
                            dst = (psum[0:GT, 4 * ln.i + 3, D * i:D * i + D] if i < 2 else psum[0:GT, 4 * ln.i, 0:D])
                            last = nc.tensor.matmul(dst, thrice[:, i, :], ln.vt, start=True, stop=True)
                        last.then_inc(u["v3"], 1)
                    for ln in lanes:
                        c = it * (2 * LANES) + (att * LANES + ln.i + 1)
                        pe.wait_ge(u["kx"], c)
                        for half in range(2):
                            for i in range(GI):
                                last = nc.tensor.matmul(
                                    psum[0:GT, 4 * ln.i + 1, 216 * half:216 * half + 216],
                                    ln.qx[:, half, GT * i:GT * i + GT], ln.kx[:, half, 216 * i:216 * i + 216],
                                    start=(i == 0), stop=(i == GI - 1))
                        last.then_inc(u["s"], 1)
                    for ln in lanes:
                        c = it * (2 * LANES) + (att * LANES + ln.i + 1)
                        pe.wait_ge(u["p"], c)
                        pe.wait_ge(u["vx"], c)
                        for tri in range(TRI):
                            last = nc.tensor.transpose(
                                psum[0:GT, 4 * ln.i + 3, GT * tri:GT * tri + GT],
                                ln.s0[:, 3 * tri:3 * tri + 3, :].rearrange("p h t -> p (h t)"), ident[0:GT, 0:GT])
                        last.then_inc(u["pt"], 1)
                    for ln in lanes:
                        c = it * (2 * LANES) + (att * LANES + ln.i + 1)
                        pe.wait_ge(u["pT"], c)
                        for tri in range(TRI):
                            for i in range(GI):
                                at = GT * tri + T3 * i
                                last = nc.tensor.matmul(psum[0:3 * HD, 4 * ln.i + 2, at:at + T3],
                                                        ln.vx[:, i, 3 * HD * tri:3 * HD * tri + 3 * HD],
                                                        ln.pT[:, at:at + T3], start=True, stop=True)
                        last.then_inc(u["o"], 1)
                    for ln in lanes:
                        c = it * (2 * LANES) + (att * LANES + ln.i + 1)
                        pe.wait_ge(u["oT"], c)
                        for tri in range(TRI):
                            rows = 3 * HD + 1 if tri == 0 else 3 * HD
                            last = nc.tensor.matmul(psum[0:GT, 4 * ln.i, 0:D], ln.oT[0:rows, GT * tri:GT * tri + GT],
                                                    w_proj[0:rows, tri, :], start=(tri == 0), stop=(tri == TRI - 1))
                        last.then_inc(u["pj"], 1)


def layout(inp):
    f = np.float32
    a = {}
    x = np.asarray(inp["x"])
    pad = np.zeros((B, 3, GRID * BLK, GRID * BLK), f)
    pad[:, :, 2:86, 2:86] = x
    blocks = pad.reshape(B, 3, GRID, BLK, GRID, BLK).transpose(0, 1, 3, 5, 2, 4).reshape(B, PIX, GRID, GRID)
    a["x"] = np.concatenate([blocks[..., 0:S1], blocks[..., 1:GRID]], 1).reshape(B, 2 * PIX, GRID * S1)
    a["ident"] = np.eye(P, dtype=f)
    half = np.arange(P) // EMB
    a["blockmean"] = (half[:, None] == half[None, :]).astype(f) / f(EMB)

    def rows1(v):
        full = np.zeros((3, 8, 8, v.shape[1]), f)
        full[:, :7, :7] = v.reshape(3, 7, 7, -1)
        full = full.reshape(3, 2, BLK, 2, BLK, -1)
        return full.transpose(3, 0, 2, 4, 1, 5).reshape(2 * PIX, 2, -1)

    def rows2(v):
        v = v.reshape(EMB, 3, 3, -1)
        full = np.zeros((P, NTAP, v.shape[-1]), f)
        for kk, taps in enumerate(TAPS):
            for upper, (kh, kw) in enumerate(taps):
                full[EMB * upper:EMB * upper + EMB, kk] = v[:, kh, kw]
        return full

    def twice(v):
        out = np.zeros((P, P), f)
        out[0:EMB, 0:EMB] = v
        out[EMB:P, EMB:P] = v
        return out

    for name, rows, feats in (("a1", rows1, F1), ("a2", rows2, F2)):
        g = {key: np.asarray(inp[f"L0_tok_{name}_{key}"]) for key in
             ("n1g", "n1b", "kqvw", "kqvb", "projw", "projb", "n2g", "n2b", "w1", "b1", "w2", "b2", "w")}
        a[name + "_w"] = rows(g["kqvw"])
        a[name + "_g"] = rows(g["n1g"][:, None])[:, :, 0]
        a[name + "_b"] = rows(g["n1b"][:, None])[:, :, 0]
        real = rows(np.ones((feats, 1), f))[:, :, 0]
        a[name + "_inv"] = (real / f(feats)).astype(f)
        a[name + "_ninv"] = -a[name + "_inv"]
        a[name + "_kqvb"] = np.broadcast_to(g["kqvb"], (P, C3))
        a[name + "_pjb"] = np.broadcast_to(g["projb"], (P, EMB))
        paug = np.zeros((EMB + 1, EMB + 1), f)
        paug[0:EMB, 0:EMB] = g["projw"]
        paug[EMB, EMB] = 1.0
        a[name + "_paug"] = paug
        a[name + "_wT"] = g["w"].T
        a[name + "_w1"] = twice(g["w1"])
        a[name + "_w2"] = twice(g["w2"])
        a[name + "_cols"] = np.stack([np.concatenate([v, v]) for v in (g["n2g"], g["n2b"], g["b1"], g["b2"])], 1)
    a["pw"] = rows2(np.asarray(inp["L0_tok_proj_w"]))
    a["pb"] = np.broadcast_to(np.asarray(inp["L0_tok_proj_b"]), (P, D))

    def with_bias(w, b):
        full = np.zeros((HALF + 1, 2, w.shape[0]), f)
        full[0:HALF] = w.T.reshape(2, HALF, -1).transpose(1, 0, 2)
        full[HALF, 0] = b
        return full

    def by_triple(w, b):
        full = np.zeros((3 * HD + 1, TRI, D), f)
        full[0:3 * HD] = w.T.reshape(TRI, 3 * HD, D).transpose(1, 0, 2)
        full[3 * HD, 0] = b
        return full

    v = {key: np.asarray(inp["L0_" + key]) for key in
         ("attn_qkv_w", "attn_qkv_b", "attn_proj_w", "attn_proj_b", "attn_temperature", "ffn_W_qkv", "ffn_b_qkv",
          "ffn_W_gate", "ffn_b_gate", "ffn_A", "ffn_B_lora", "ffn_W_proj", "ffn_b_proj")}
    a["wqkv0"] = with_bias(v["attn_qkv_w"], v["attn_qkv_b"])
    a["wqkv1"] = with_bias(v["ffn_W_qkv"], v["ffn_b_qkv"])
    a["wproj0"] = by_triple(v["attn_proj_w"], v["attn_proj_b"])
    a["wproj1"] = by_triple(v["ffn_W_proj"], v["ffn_b_proj"])
    router = np.concatenate([v["ffn_W_gate"], v["ffn_A"].reshape(NEXP * RANK, D)], 0)
    a["wrout"] = with_bias(router, np.concatenate([v["ffn_b_gate"], np.zeros(P, f)]))
    a["blora"] = v["ffn_B_lora"].transpose(0, 2, 1).reshape(NEXP * RANK, 3 * D)
    a["temp"] = np.broadcast_to(v["attn_temperature"], (HALF, 1))
    a["kmask"] = (np.arange(HALF)[:, None] // HD == np.arange(6)[None, :]).astype(f)
    a["vmask"] = (np.arange(GT)[:, None] // T3 == np.arange(D)[None, :] // HD % 3).astype(f)
    tok = np.arange(GT)
    a["thrice"] = np.stack([(tok[:, None] == i * T3 + tok[None, :] % T3) for i in range(GI)], 1).astype(f)
    return a


def kernel(**inputs):
    import concourse.bacc as _bacc
    from concourse.bass_utils import run_bass_kernel_spmd as _run

    nc = _bacc.Bacc("TRN2", target_bir_lowering=False, num_devices=1)
    arrays, aps = {}, {}
    for name, v in layout(inputs).items():
        v = np.ascontiguousarray(v)
        arrays["in_" + name] = v
        aps[name] = nc.dram_tensor("in_" + name, v.shape, mybir.dt.from_np(v.dtype), kind="ExternalInput").ap()
    out = nc.dram_tensor("out_0", (NG * GT, D), F32, kind="ExternalOutput").ap()
    build(nc, aps, out)
    r = _run(nc, [arrays], core_ids=[0])
    return r.results[0]["out_0"][0:B * T3].reshape(B, T3, D)
```

```python
from contextlib import ExitStack

import numpy as np

import concourse.bass as bass
from concourse import mybir

F32 = mybir.dt.float32
ALU = mybir.AluOpType
ACT = mybir.ActivationFunctionType
AX_X = mybir.AxisListType.X

P = 128
B = 64
EMB, M = 64, 32
C3 = 3 * EMB
BLK = 4
GRID = 22
PIX = 3 * BLK * BLK
S1, S2, S3 = 21, 11, 6
T1, T2, T3 = S1 * S1, S2 * S2, S3 * S3
F1, F2 = 3 * 7 * 7, EMB * 9
NCH = 4
ROWS1 = 6
NT1 = ROWS1 * S1
XR = 25
NTAP = 5
TAPS = [((0, 0), (1, 0)), ((0, 1), (1, 1)), ((0, 2), (1, 2)), ((2, 0), (2, 1)), ((2, 2),)]
PAD1, PAD2 = S1 + 2, S2 + 2
MAP1, MAP2 = PAD1 * PAD1, PAD2 * PAD2
V0, ONE, WK, MEAN, SQ = 128, 192, 193, 257, 258
D = 192
HEADS, HD = 12, 16
GI, NG = 3, 22
GT = GI * T3
TRI = HEADS // 3
HALF = D // 2
NEXP, RANK, TOP_K, ALPHA = 8, 16, 2, 32
KEEP = T3 // 2
LANES = 2
EPS = 1e-5
MLP_DEPTH = 4
HUGE = 3.0e38


class Part:
    pass


def performer_sizes():
    one = Part()
    one.name = 'a1'
    one.stage = 1
    one.nk = 2
    one.kp = 2 * PIX
    one.nt = NT1
    one.units = B
    one.shared_kv = True
    one.real = [NT1, NT1, NT1, T1 - 3 * NT1]
    one.features = F1
    one.mlp_units = B // 2
    one.columns = T1
    two = Part()
    two.name = 'a2'
    two.stage = 2
    two.nk = NTAP
    two.kp = P
    two.nt = T2
    two.units = B // NCH
    two.shared_kv = False
    two.real = [T2] * NCH
    two.features = F2
    two.mlp_units = B // NCH // 2
    two.columns = NCH * T2
    return one, two


def build(nc, a, out):
    with ExitStack() as ctx:
        def sb(name, shape):
            return ctx.enter_context(nc.sbuf_tensor(name, shape, F32))

        def sem(name):
            return ctx.enter_context(nc.semaphore(name))

        def sems(prefix, names):
            return {n: sem(prefix + n) for n in names.split()}

        psum = ctx.enter_context(nc.psum_tensor("psum", [P, 8, 512], F32))

        ident = sb("ident", [P, P])
        blockmean = sb("blockmean", [P, P])
        ones_sq = sb("ones_sq", [P, P])
        neg_half = sb("neg_half", [P, 2 * NCH])
        ln_m = sb("ln_m", [P, 1])
        scratch = sb("scratch", [P, 1])
        const_in = sem("const_in")
        const_set = sem("const_set")

        y_mem = sb("y_mem", [P, B // 2 * NCH * 2 * EMB])
        late = sb("late", [P, B // 2 * MAP1])
        y1_all = late[:, :].rearrange("p (n x) -> p n x", x=MAP1)
        y_out1 = y_mem[:, :].rearrange("p (n c i e) -> p n c i e", c=NCH, i=2, e=EMB)
        y_pair = y_mem[:, :].rearrange("p (n c e) -> p n c e", c=NCH, e=2 * EMB)
        n2 = B * EMB
        y_out2 = y_mem[:, 0:n2].rearrange("p (n c e) -> p n c e", c=NCH, e=EMB)
        y2_all = y_mem[:, n2:n2 + NG * GI // 2 * MAP2].rearrange("p (n x) -> p n x", x=MAP2)
        zeroed = sem("zeroed")

        def carver(mem, start=0):
            at = [start]

            def tile(rows, *dims):
                n = int(np.prod(dims))
                v = mem[0:rows, at[0]:at[0] + n]
                at[0] += n
                assert at[0] <= mem.shape[1], (at[0], mem.shape)
                if len(dims) == 1:
                    return v
                names = "abc"[:len(dims)]
                return v.rearrange(f"p ({' '.join(names)}) -> p {' '.join(names)}",
                                   **{m: d for m, d in zip(names, dims)})

            return tile

        early_tile = carver(y_mem)

        one, two = performer_sizes()
        for st in (one, two):
            n = st.name + "_"
            st.wraw = early_tile(st.kp, st.nk, C3)
            st.wcat_all = sb(n + "wcat", [P, st.nk, SQ + 1])
            st.wcat = st.wcat_all[0:st.kp, :, :]
            st.gcol = sb(n + "gcol", [st.kp, st.nk])
            st.bcol = sb(n + "bcol", [st.kp, st.nk])
            st.inv = sb(n + "inv", [st.kp, st.nk])
            st.ninv = sb(n + "ninv", [st.kp, st.nk])
            st.kqvb = sb(n + "kqvb", [P, C3])
            st.bias = sb(n + "bias", [P, MEAN])
            st.pjb = sb(n + "pjb", [P, EMB])
            st.paug = sb(n + "paug", [EMB + 1, EMB + 1])
            st.wT = sb(n + "wT", [EMB, M])
            st.w1 = sb(n + "w1", [P, P])
            st.w1c = sb(n + "w1c", [P, P])
            st.w2 = sb(n + "w2", [P, P])
            st.cols = sb(n + "cols", [P, 4])
            st.b1c = sb(n + "b1c", [P, 1])
            st.w_in = sem(n + "w_in")
        sq_weights = sb("sq_weights", [P, 2])
        channels = sb("channels", [2 * PIX, 2 * BLK * BLK])
        w = sems("w_", "scaled summed centered wide biased bias_set turned turned_copied folded "
                       "folded_copied mlp_scaled mlp_summed mlp_set")
        x_made = sems("x_", "act dve zero")
        k = sems("k_", "xsq chan taps main stat square_mean var var_eps rstd z kqsq xd arg e vb kvq kvq_copied "
                       "mp mp_copied yp den rec yn y")
        m = sems("m_", "sq sum1 sum2 square_mean var var_eps rstd yn tr tr_copied w1 gelu w2 out")
        m_in = [sem(f"m_in{i}") for i in range(2)]
        x_in = [sem(f"x_in{i}") for i in range(2)]
        one.w0, two.w0 = 0, 1
        one.t0, two.t0 = 0, one.nk + 1
        one.k0, two.k0 = 1, 1 + one.units
        one.m0, two.m0 = 1, 1 + one.mlp_units
        one.y0, two.y0 = 0, 16 * one.mlp_units // 2
        wide = early_tile(P, NTAP, P)
        turned = early_tile(EMB, 2, P)

        xbuf = [sb(f"xbuf{i}", [P, NCH * NTAP * T2]) for i in range(2)]
        xsqbuf = sb("xsqbuf", [P, NCH * NTAP * T2])
        tapsum = [sb(f"tapsum{i}", [P, NCH * P]) for i in range(2)]
        z = [sb(f"z{i}", [P, NCH, MEAN]) for i in range(2)]
        e = [sb(f"e{i}", [P, NCH, 2, M]) for i in range(2)]
        vb = [sb(f"vb{i}", [P, NCH, EMB]) for i in range(2)]
        kqsq = sb("kqsq", [P, NCH, 2, EMB])
        xd = sb("xd", [P, NCH, 2])
        arg = sb("arg", [P, NCH, 2, M])
        stat = sb("stat", [P, NCH, 2])
        sqm = sb("sqm", [P, 2 * NCH])
        var = sb("var", [P, 2 * NCH])
        var_eps = sb("var_eps", [P, NCH])
        rstd = sb("rstd", [P, NCH])
        var_eps_m = [sb(f"var_eps_m{i}", [P, 2 * NCH]) for i in range(2)]
        rstd_m = [sb(f"rstd_m{i}", [P, 2 * NCH]) for i in range(2)]
        kv = sb("kv", [EMB + 1, NCH, M])
        qT = sb("qT", [M, NCH * NT1])
        mp = sb("mp", [M, NCH, EMB + 1])
        den = sb("den", [P, NCH])
        rec = sb("rec", [P, NCH])
        yn = sb("yn", [P, NCH, EMB])
        sum1 = sb("sum1", [P, 2 * NCH])
        sum2 = sb("sum2", [P, 2 * NCH])
        square_tile = carver(xsqbuf)
        ysq = [square_tile(P, 2 * NCH, EMB) for _ in range(2)]
        ynm = [square_tile(P, NCH, P) for _ in range(2)]
        z_flat = [z_[:, :, :].rearrange("p c e -> p (c e)") for z_ in z]
        ynT = [z_[:, 0:NCH * P] for z_ in z_flat]
        yres = [z_[:, NCH * P:2 * NCH * P].rearrange("p (c e) -> p c e", e=P) for z_ in z_flat]
        gel = tapsum

        X1 = [x[0:2 * PIX, 0:GRID * S1] for x in xbuf]
        X1sum = [x[2 * PIX:P, 0:GRID * S1] for x in xbuf]
        X1q = xsqbuf[0:2 * PIX, 0:GRID * S1]

        def patches(st, x, c, kk):
            if st.stage == 1:
                return x[:, NT1 * c + S1 * kk:NT1 * c + S1 * kk + NT1]
            at = (c * NTAP + kk) * T2
            return x[0:krows(st, kk), at:at + T2]

        def krows(st, kk):
            return P if st.stage == 1 else EMB * len(TAPS[kk])

        late_tile = carver(late)
        tail_tile = carver(y_mem, n2 + NG * GI // 2 * MAP2)
        pw = tail_tile(P, NTAP, D)
        pb = tail_tile(P, D)
        wqkv, wproj = [], []
        for i in range(2):
            old_input = carver(xbuf[i])
            wqkv.append(old_input(HALF + 1, 2, 3 * D))
            wproj.append(old_input(3 * HD + 1, TRI, D))
        wrout = tail_tile(HALF + 1, 2, NEXP + P)
        blora = tail_tile(P, 3 * D)
        qscale = sb("qscale", [HALF, 4])
        kmask = sb("kmask", [HALF, 6])
        vmask = tail_tile(GT, D)
        thrice = tail_tile(GT, GI, GT)
        t_in = sem("t_in")
        clipped = sem("clipped")
        scale_set = sem("scale_set")
        lanes_set = sem("lanes_set")

        g_tile = late_tile(P, NTAP, LANES * GT)
        lanes = []
        for i in range(LANES):
            ln = Part()
            ln.i = i
            ln.h = late_tile(GT, D)
            ln.bn = late_tile(GT, 6)
            ln.mv = late_tile(GT, 2)
            ln.veps = late_tile(GT, 1)
            ln.r = late_tile(GT, 1)
            ln.hn = late_tile(GT, D)
            ln.hnT = late_tile(HALF + 1, 2, GT)
            ln.qx = late_tile(HALF, 2, GI * GT)
            ln.kT = late_tile(HALF, 2, GT)
            ln.kx = late_tile(HALF, 2, GI * 6 * T3)
            ln.vx = late_tile(GT, GI, D)
            ln.vt = late_tile(GT, D)
            ln.s0 = late_tile(GT, HEADS, T3)
            ln.s1 = late_tile(GT, HEADS, T3)
            ln.s2 = late_tile(GT, HEADS, T3)
            ln.keep = late_tile(GT, HEADS, T3)
            ln.top = [late_tile(GT, HEADS, 8) for _ in range(3)]
            ln.mx = late_tile(GT, HEADS)
            ln.sm = late_tile(GT, HEADS)
            ln.rs = late_tile(GT, HEADS)
            ln.pT = late_tile(GT, TRI * GT)
            ln.oT = late_tile(3 * HD + 1, TRI * GT)
            ln.res = late_tile(GT, D)
            ln.lg = late_tile(GT, 2 * NEXP)
            ln.lg2 = late_tile(GT, 2 * NEXP)
            ln.l8 = late_tile(GT, 8)
            ln.rep = late_tile(GT, 8)
            ln.sel = late_tile(GT, NEXP)
            ln.lm = late_tile(GT, NEXP)
            ln.le = late_tile(GT, NEXP)
            ln.ls = late_tile(GT, 1)
            ln.lr = late_tile(GT, 1)
            ln.lw = late_tile(GT, NEXP)
            ln.lw2 = late_tile(GT, NEXP)
            ln.aw = late_tile(GT, P)
            ln.aT = late_tile(P, GT)
            ln.res_ready = sem(f'res_ready{i}')
            ln.res_out = sem(f'res_out{i}')
            lanes.append(ln)
        t = sems("t_", "g hp h s0 top8 keep em rt lg l8 rep found sel lm le lr lw lw2 aw at aT")
        u = sems("u_", "bn mv veps r hn tr hnT qk v vt v3 q kT kx vx s mx sub exp sum rs p pt pT o oT pj h")

        block = ctx.enter_context(nc.Block())

        def nth(j, par):
            return j * 2 + par

        def peeled(j):
            return isinstance(j, int) and j == 0

        def before(j, par, back):
            return j + (par - back) // 2, (par - back) % 2

        def performer_periods(eng, st, period):
            last = st.units // 2 - 1
            for par in range(2):
                period(0, par, lambda back: par >= back)
            with eng.Fori(1, last) as j_:
                for par in range(2):
                    period(j_, par, lambda back: True)
            for n in range(2 * last, 2 * last + 4):
                period(n // 2, n % 2, lambda back: n - back < st.units)

        def mlp_periods(eng, st, period):
            edge = MLP_DEPTH // 2
            for j in range(edge):
                for par in range(2):
                    period(j, par, lambda back: 2 * j + par >= back)
            with eng.Fori(edge, st.mlp_units // 2) as j_:
                for par in range(2):
                    period(j_, par, lambda back: True)
            for n in range(st.mlp_units, st.mlp_units + MLP_DEPTH - 1):
                period(n // 2, n % 2, lambda back: n - back < st.mlp_units)

        def mlp_rows(st, j, par):
            return y_pair[0:st.nt, bass.ds(nth(j, par), 1), :, :].rearrange("p o c e -> p (o c) e")

        def load_x(sp, st, j, par):
            n = nth(j, par)
            if not peeled(j):
                sp.wait_ge(k["main"], NCH * (n + (st.k0 - 1)))
            src = a["x"][bass.ds(n, 1), :, :].rearrange("o p t -> (o p) t")
            sp.dma_start(X1[par][:, 0:GRID * S1], src).then_inc(x_in[par], 16)

        def load_y(sp, st, j, par):
            n = nth(j, par)
            if not peeled(j):
                sp.wait_ge(m["w2"], n + (st.m0 - 1))
            sp.dma_start(yres[par][0:st.nt, :, :], mlp_rows(st, j, par)).then_inc(m_in[par], 16)

        def load_ys(sp, st):
            sp.wait_ge(k["y"], st.k0 + st.units)
            for par in range(2):
                load_y(sp, st, 0, par)
            with sp.Fori(1, st.mlp_units // 2) as j:
                for par in range(2):
                    load_y(sp, st, j, par)

        def store_group(sp, it, ln):
            sp.wait_ge(ln.res_ready, it + 2)
            sp.dma_start(out[bass.ds(it * (LANES * GT) + ln.i * GT, GT), :], ln.res).then_inc(ln.res_out, 16)

        @block.sync
        def _(sp):
            for name, s_ in (*k.items(), *m.items()):
                sp.sem_inc(s_, NCH if name in ("main", "z") else 1)
            for name in ("stat", "square_mean", "var", "var_eps", "rstd"):
                sp.sem_inc(k[name], 1)
            for ln in lanes:
                sp.sem_inc(ln.res_ready, 1)
                sp.sem_inc(ln.res_out, 16)
            sp.sem_inc(t["hp"], 1)
            sp.dma_start(ident[:, :], a["ident"]).then_inc(const_in, 16)
            sp.dma_start(blockmean[:, :], a["blockmean"]).then_inc(const_in, 16)
            sp.dma_start(sq_weights[:, :], a["sq_weights"]).then_inc(const_in, 16)
            sp.dma_start(channels[:, :], a["channels"]).then_inc(const_in, 16)
            for st in (one, two):
                sp.dma_start(st.wraw, a[st.name + "_w"]).then_inc(st.w_in, 16)
                for dst, src in ((st.gcol, "g"), (st.bcol, "b"), (st.inv, "inv"), (st.ninv, "ninv"),
                                 (st.kqvb, "kqvb"), (st.pjb, "pjb"), (st.paug, "paug"), (st.wT, "wT"),
                                 (st.w1, "w1"), (st.w2, "w2"), (st.cols, "cols")):
                    sp.dma_start(dst[:, :], a[st.name + "_" + src]).then_inc(st.w_in, 16)
                if st.stage == 1:
                    sp.wait_ge(const_set, 1)
                    for par in range(2):
                        load_x(sp, one, 0, par)
            with sp.Fori(1, one.units // 2) as j:
                for par in range(2):
                    load_x(sp, one, j, par)

            load_ys(sp, one)

            sp.wait_ge(k["y"], two.k0 + two.units)
            sp.dma_start(pw, a["pw"]).then_inc(t_in, 16)
            sp.dma_start(pb, a["pb"]).then_inc(t_in, 16)
            for i in range(2):
                sp.dma_start(wqkv[i], a[f"wqkv{i}"]).then_inc(t_in, 16)
                sp.dma_start(wproj[i], a[f"wproj{i}"]).then_inc(t_in, 16)
            sp.dma_start(wrout, a["wrout"]).then_inc(t_in, 16)
            sp.dma_start(blora, a["blora"]).then_inc(t_in, 16)
            sp.dma_start(qscale[:, 0:1], a["temp"]).then_inc(t_in, 16)
            sp.dma_start(kmask[:, :], a["kmask"]).then_inc(t_in, 16)
            sp.dma_start(vmask, a["vmask"]).then_inc(t_in, 16)
            sp.dma_start(thrice, a["thrice"]).then_inc(t_in, 16)
            load_ys(sp, two)

            with sp.Fori(0, NG // LANES - 1) as it:
                for ln in lanes:
                    store_group(sp, it, ln)
            for ln in lanes:
                store_group(sp, NG // LANES - 1, ln)
            for ln in lanes:
                sp.wait_ge(ln.res_out, 16 * (NG // LANES + 1))

        def pool_rstd(pool, st, j, par, half):
            n = nth(j, par)
            two_chunks = slice(2 * half, 2 * half + 2)
            pool.wait_ge(k["var_eps"], n * 2 + (2 * st.k0 + half + 1))
            nc.gpsimd.tensor_tensor(rstd[0:st.nt, two_chunks], var_eps[0:st.nt, two_chunks],
                                    neg_half[0:st.nt, two_chunks], ALU.pow).then_inc(k["rstd"], 1)

        def pool_residual(pool, st, j, par):
            n = nth(j, par)
            pool.wait_ge(k["z"], NCH * (n + (st.k0 + 1)))
            if not peeled(j):
                pool.wait_ge(k["y"], n + (st.k0 - 1))
            pjb = st.pjb[0:st.nt, :].unsqueeze(1).broadcast_to([st.nt, NCH, EMB])
            nc.gpsimd.tensor_tensor(vb[par][0:st.nt, :, :], z[par][0:st.nt, :, V0:V0 + EMB], pjb,
                                    ALU.add).then_inc(k["vb"], 1)

        def pool_back(pool, st, j, par):
            n = nth(j, par)
            pool.wait_ge(k["yn"], n + (st.k0 + 1))
            pool.wait_ge(k["vb"], n + (st.k0 + 1))
            if st.stage == 1:
                dst = y_out1[0:st.nt, bass.ds(j, 1), :, par, :]
            else:
                dst = y_out2[0:st.nt, bass.ds(n, 1), :, :]
            nc.gpsimd.tensor_tensor(dst.rearrange("p o c e -> p (o c) e"), yn[0:st.nt, :, :],
                                    vb[par][0:st.nt, :, :], ALU.add).then_inc(k["y"], 1)

        def pool_performer(pool, st):
            def period(j, par, live=lambda back: True):
                if live(0):
                    pool_rstd(pool, st, j, par, 0)
                if live(1):
                    pool_residual(pool, st, *before(j, par, 1))
                if live(0):
                    pool_rstd(pool, st, j, par, 1)
                if live(2):
                    pool_back(pool, st, j - 1, par)

            performer_periods(pool, st, period)

        def pool_mlp(pool, st):
            with pool.Fori(0, st.mlp_units // 2) as j:
                for par in range(2):
                    pool.wait_ge(m["var_eps"], nth(j, par) + (st.m0 + 1))
                    nc.gpsimd.tensor_tensor(rstd_m[par][0:st.nt, :], var_eps_m[par][0:st.nt, :], neg_half[0:st.nt, :],
                                            ALU.pow).then_inc(m["rstd"], 1)

        def per_head(x):
            return x.unsqueeze(2).broadcast_to([GT, HEADS, T3])

        @block.gpsimd
        def _(pool):
            for tile, value in ((ones_sq, 1.0), (neg_half, -0.5), (ln_m, -0.5 * float(np.log(M))),
                                (xbuf[0], 0.0), (xbuf[1], 0.0)):
                nc.gpsimd.memset(tile[:, :], value)
            for st in (one, two):
                nc.gpsimd.memset(st.wcat_all[:, :, :], 0.0)
                nc.gpsimd.memset(st.bias[:, ONE:ONE + 1], 1.0)
            nc.gpsimd.memset(xsqbuf[:, 0:1], 0.0).then_inc(const_set, 1)
            nc.gpsimd.memset(late[:, :], 0.0).then_inc(zeroed, 1)
            pool.wait_ge(const_set, 1)
            for st in (one, two):
                pool.wait_ge(st.w_in, 16 * 12)
                pool.wait_ge(const_in, 64)

            pool_performer(pool, one)
            pool_mlp(pool, one)
            pool.wait_ge(m["out"], two.m0)
            nc.gpsimd.memset(y2_all, 0.0).then_inc(zeroed, 1)
            pool.wait_ge(zeroed, 2)
            pool_performer(pool, two)
            for ln in lanes:
                nc.gpsimd.memset(ln.qx, 0.0)
                nc.gpsimd.memset(ln.hnT, 1.0)
                nc.gpsimd.memset(ln.oT, 1.0)
                nc.gpsimd.memset(ln.lg[:, NEXP:2 * NEXP], -HUGE)
                last = nc.gpsimd.memset(ln.rep, -HUGE)
            last.then_inc(lanes_set, 1)
            pool.wait_ge(lanes_set, 1)
            pool_mlp(pool, two)
            pool.wait_ge(t_in, 16 * 12)

            with pool.Fori(0, NG // LANES) as it:
                for att in range(2):
                    for ln in lanes:
                        c = it * (2 * LANES) + (att * LANES + ln.i + 1)
                        pool.wait_ge(u["veps"], c)
                        nc.gpsimd.tensor_tensor(ln.r, ln.veps, neg_half[0:GT, 0:1], ALU.pow).then_inc(u["r"], 1)
                    for ln in lanes:
                        c = it * (2 * LANES) + (att * LANES + ln.i + 1)
                        pool.wait_ge(u["kT"], c)
                        for half in range(2):
                            keys = ln.kT[:, half, :].rearrange("p (i t) -> p i t", i=GI).unsqueeze(2)
                            kept = kmask[:, :].unsqueeze(1).unsqueeze(3)
                            last = nc.gpsimd.tensor_tensor(
                                ln.kx[:, half, :].rearrange("p (i h t) -> p i h t", i=GI, h=6),
                                keys.broadcast_to([HALF, GI, 6, T3]), kept.broadcast_to([HALF, GI, 6, T3]),
                                ALU.mult)
                        last.then_inc(u["kx"], 1)
                    for ln in lanes:
                        c = it * (2 * LANES) + (att * LANES + ln.i + 1)
                        pool.wait_ge(u["mx"], c)
                        nc.gpsimd.tensor_tensor(ln.s1, ln.s0, per_head(ln.mx), ALU.subtract).then_inc(u["sub"], 1)
                    for ln in lanes:
                        c = it * (2 * LANES) + (att * LANES + ln.i + 1)
                        pool.wait_ge(u["exp"], c)
                        if att == 0:
                            g = it * LANES + (ln.i + 1)
                            pool.wait_ge(t["keep"], g)
                            nc.gpsimd.tensor_tensor(ln.s2, ln.s2, ln.keep, ALU.mult).then_inc(t["em"], 1)
                    for ln in lanes:
                        c = it * (2 * LANES) + (att * LANES + ln.i + 1)
                        pool.wait_ge(u["rs"], c)
                        nc.gpsimd.tensor_tensor(ln.s0, ln.s2, per_head(ln.rs), ALU.mult).then_inc(u["p"], 1)

        def gather_ops(copy, dst, src, sides, i):
            for kk, taps in enumerate(TAPS):
                for upper, (kh, kw) in enumerate(taps):
                    end = 2 * sides - 1
                    last = copy(dst(EMB * upper, kk),
                                src[EMB * i:EMB * i + EMB, :, kh:kh + end:2, kw:kw + end:2])
            return last

        def gather_x(eng, copy, done, j, par, i):
            n = nth(j, par)
            if not peeled(j):
                eng.wait_ge(k["main"], NCH * (n + (two.k0 - 1)))
            src = y1_all[:, bass.ds(n * 2, 2), :].rearrange("p n (r c) -> p n r c", c=PAD1)
            x = xbuf[par][:, :].rearrange("p (n i k r c) -> p n i k r c", i=2, k=NTAP, c=S2, n=2)
            gather_ops(copy, lambda row, kk: x[row:row + EMB, :, i, kk, :, :], src, S2, i).then_inc(done, 1)

        def gather_g(copy, it, i):
            pairs = LANES * GI // 2
            src = y2_all[:, bass.ds(it * pairs, pairs), :].rearrange("p n (r c) -> p n r c", c=PAD2)
            x = g_tile.rearrange("p k (n i r c) -> p k n i r c", i=2, c=S3, n=pairs)
            return gather_ops(copy, lambda row, kk: x[row:row + EMB, kk, :, i, :, :], src, S3, i)

        def act_squares(act, st, j, par):
            n = nth(j, par)
            act.wait_ge(k["z"], NCH * (n + (st.k0 + 1)))
            act.wait_ge(k["xd"], n + st.k0)
            nc.scalar.activation(kqsq[0:st.nt, :, :, :],
                                 z[par][0:st.nt, :, 0:V0].rearrange("p c (s e) -> p c s e", s=2),
                                 ACT.Square).then_inc(k["kqsq"], 1)

        def act_exp(act, st, j, par):
            n = nth(j, par)
            act.wait_ge(k["arg"], n + (st.k0 + 1))
            if not peeled(j):
                act.wait_ge(k["kvq"], n + (st.k0 - 1))
            nc.scalar.activation(e[par][0:st.nt, :, :, :], arg[0:st.nt, :, :, :], ACT.Exp,
                                 bias=ln_m[0:st.nt, 0:1]).then_inc(k["e"], 1)

        def act_kvq(act, st, j, par):
            n = nth(j, par)
            act.wait_ge(k["kvq"], n + (st.k0 + 1))
            act.wait_ge(k["yp"], n + st.k0)
            nkv = 1 if st.shared_kv else NCH
            nc.scalar.activation(kv[:, 0:nkv, :], psum[0:EMB + 1, 4, 0:nkv * M].rearrange(
                "p (c m) -> p c m", m=M), ACT.Copy)
            nc.scalar.activation(qT[:, 0:NCH * st.nt], psum[0:M, 5, 0:NCH * st.nt], ACT.Copy
                                 ).then_inc(k["kvq_copied"], 1)

        def act_mp(act, st, j, par):
            n = nth(j, par)
            nkv = 1 if st.shared_kv else NCH
            act.wait_ge(k["mp"], n + (st.k0 + 1))
            nc.scalar.activation(mp[:, 0:nkv, :], psum[0:M, 4, P:P + nkv * (EMB + 1)].rearrange(
                "p (c m) -> p c m", m=EMB + 1), ACT.Copy).then_inc(k["mp_copied"], 1)

        def act_channels(act, st, j, par):
            if st.stage == 1:
                n = nth(j, par)
                act.wait_ge(k["chan"], n + (st.k0 + 1))
                if not peeled(j):
                    act.wait_ge(k["main"], NCH * (n + (st.k0 - 1)))
                nc.scalar.activation(X1sum[par], psum[0:2 * BLK * BLK, 7, 0:GRID * S1], ACT.Copy).then_inc(k["taps"], 1)

        def act_copy(dst, src):
            return nc.scalar.activation(dst, src, ACT.Copy)

        def act_patches(act, st, j, par):
            if st.stage == 2:
                gather_x(act, act_copy, x_made["act"], j, par, 0)
                n = nth(j, par)
                act.wait_ge(x_made["act"], n + 1)
                act.wait_ge(x_made["dve"], n + 1)
                act.wait_ge(x_made["zero"], 1)
                act.wait_ge(k["taps"], n + st.k0)
                nc.scalar.activation(xsqbuf[:, :], xbuf[par][:, :], ACT.Square).then_inc(k["xsq"], 1)
            else:
                n = nth(j, par)
                act.wait_ge(x_in[par], j * 16 + 16)
                act.wait_ge(k["chan"], n + st.k0)
                nc.scalar.activation(X1q, X1[par], ACT.Square).then_inc(k["xsq"], 1)

        def act_performer(act, st):
            act_patches(act, st, 0, 0)
            act_channels(act, st, 0, 0)

            def period(j, par, live):
                if live(-1) and st.stage == 2:
                    act_patches(act, st, *before(j, par, -1))
                if live(2):
                    act_kvq(act, st, j - 1, par)
                if live(1):
                    act_squares(act, st, *before(j, par, 1))
                if live(-1) and st.stage == 1:
                    act_patches(act, st, *before(j, par, -1))
                if live(2):
                    act_mp(act, st, j - 1, par)
                if live(-1):
                    act_channels(act, st, *before(j, par, -1))
                if live(1):
                    act_exp(act, st, *before(j, par, 1))

            performer_periods(act, st, period)

        def act_square(act, st, j, par):
            n = nth(j, par)
            if not peeled(j):
                act.wait_ge(m["sum2"], n + (st.m0 - 1))
            nc.scalar.activation(ysq[par][0:st.nt, :, :], mlp_rows(st, j, par).rearrange(
                "p c (i e) -> p (c i) e", i=2), ACT.Square).then_inc(m["sq"], 1)

        def act_turned(act, st, j, par):
            n = nth(j, par)
            act.wait_ge(m["tr"], n + (st.m0 + 1))
            nc.scalar.activation(ynT[par][:, 0:st.columns], psum[:, par, 0:st.columns], ACT.Copy
                                 ).then_inc(m["tr_copied"], 1)

        def act_gelu(act, st, j, par):
            n = nth(j, par)
            if not peeled(j):
                act.wait_ge(m["w2"], n + (st.m0 - 1))
            act.wait_ge(m["w1"], n + (st.m0 + 1))
            nc.scalar.activation(gel[par][:, 0:st.columns], psum[:, 2 + par, 0:st.columns], ACT.Gelu,
                                 bias=st.b1c[:, 0:1]).then_inc(m["gelu"], 1)

        def act_mlp(act, st):
            act.wait_ge(w["mlp_set"], st.w0 + 1)
            act.wait_ge(k["y"], st.k0 + st.units)

            def period(j, par, live):
                if live(0):
                    act_square(act, st, j, par)
                if live(2):
                    act_gelu(act, st, *before(j, par, 2))
                if live(1):
                    act_turned(act, st, *before(j, par, 1))

            mlp_periods(act, st, period)

        @block.scalar
        def _(act):
            act.wait_ge(const_set, 1)
            act_performer(act, one)
            act_mlp(act, one)
            act.wait_ge(m["out"], two.m0)
            act_performer(act, two)
            act_mlp(act, two)
            act.wait_ge(scale_set, 1)
            act.wait_ge(lanes_set, 1)
            act.wait_ge(m["out"], two.m0 + two.mlp_units)
            with act.Fori(0, NG // LANES) as it:
                act.wait_ge(t["hp"], it * LANES + 1)
                for i in range(2):
                    last = gather_g(act_copy, it, i)
                last.then_inc(t["g"], 1)
                for att in range(2):
                    for ln in lanes:
                        c = it * (2 * LANES) + (att * LANES + ln.i + 1)
                        act.wait_ge(u["tr"], c)
                        nc.scalar.activation(ln.hnT[0:HALF, :, :], psum[0:HALF, 4 * ln.i + 1, 0:2 * GT].rearrange(
                            "p (u t) -> p u t", u=2), ACT.Copy).then_inc(u["hnT"], 1)
                    if att == 1:
                        for ln in lanes:
                            g = it * LANES + (ln.i + 1)
                            act.wait_ge(t["lm"], g)
                            nc.scalar.activation(ln.le, ln.lm, ACT.Exp).then_inc(t["le"], 1)
                        for ln in lanes:
                            g = it * LANES + (ln.i + 1)
                            act.wait_ge(t["at"], g)
                            nc.scalar.activation(ln.aT, psum[:, 4 * ln.i + 1, 0:GT], ACT.Copy).then_inc(t["aT"], 1)
                    for ln in lanes:
                        c = it * (2 * LANES) + (att * LANES + ln.i + 1)
                        act.wait_ge(u["qk"], c)
                        blocks = bass.AP(ln.qx.tensor, ln.qx.offset, [list(ln.qx.ap[0]), [GI * GT, 2],
                                                                      [GT + T3, GI], [1, T3]])
                        nc.scalar.activation(blocks, psum[0:HALF, 4 * ln.i + 2, 0:2 * GT].rearrange(
                            "p (u i t) -> p u i t", u=2, i=GI), ACT.Copy, scale=qscale[:, 2 + att:3 + att])
                        nc.scalar.activation(ln.kT, psum[0:HALF, 4 * ln.i + 2, 2 * GT:4 * GT].rearrange(
                            "p (u t) -> p u t", u=2), ACT.Copy).then_inc(u["kT"], 1)
                    for ln in lanes:
                        c = it * (2 * LANES) + (att * LANES + ln.i + 1)
                        act.wait_ge(u["v"], c)
                        nc.scalar.activation(ln.vt, psum[0:GT, 4 * ln.i, 0:D], ACT.Copy).then_inc(u["vt"], 1)
                    for ln in lanes:
                        c = it * (2 * LANES) + (att * LANES + ln.i + 1)
                        act.wait_ge(u["s"], c)
                        nc.scalar.activation(ln.s0, psum[0:GT, 4 * ln.i + 1, 0:HEADS * T3].rearrange(
                            "p (h t) -> p h t", h=HEADS), ACT.Copy).then_inc(u["h"], 1)
                    for ln in lanes:
                        c = it * (2 * LANES) + (att * LANES + ln.i + 1)
                        act.wait_ge(u["sub"], c)
                        if att == 0:
                            act.wait_ge(t["keep"], it * LANES + (ln.i + 1))
                        nc.scalar.activation(ln.s2, ln.s1, ACT.Exp).then_inc(u["exp"], 1)
                    for ln in lanes:
                        c = it * (2 * LANES) + (att * LANES + ln.i + 1)
                        act.wait_ge(u["pt"], c)
                        nc.scalar.activation(ln.pT, psum[0:GT, 4 * ln.i + 3, 0:TRI * GT], ACT.Copy
                                             ).then_inc(u["pT"], 1)
                    for ln in lanes:
                        c = it * (2 * LANES) + (att * LANES + ln.i + 1)
                        act.wait_ge(u["o"], c)
                        nc.scalar.activation(ln.oT[0:3 * HD, :], psum[0:3 * HD, 4 * ln.i + 2, 0:TRI * GT], ACT.Copy
                                             ).then_inc(u["oT"], 1)

        def plain(dve):
            nc.vector.memset(scratch[0:1, 0:1], 0.0)

        def dve_prepare(dve, st):
            c0 = st.w0 + 1
            dve.wait_ge(st.w_in, 16 * 12)
            if st.stage == 1:
                dve.wait_ge(const_in, 64)
                nc.vector.tensor_copy(st.wcat_all[:, :, SQ], sq_weights[:, :])
            for c in range(st.nk):
                last = nc.vector.tensor_scalar(st.wcat[:, c, 0:C3], st.wraw[:, c, :], st.gcol[:, c:c + 1], None, ALU.mult)
                last = nc.vector.tensor_scalar(wide[0:st.kp, c, :], ones_sq[0:st.kp, :], st.bcol[:, c:c + 1], None, ALU.mult)
                last = nc.vector.tensor_copy(st.wcat[:, c, MEAN:MEAN + 1], st.inv[:, c:c + 1])
            last.then_inc(w["scaled"], 1)
            dve.wait_ge(w["summed"], c0)
            dve.wait_ge(w["scaled"], c0)
            for c in range(st.nk):
                last = nc.vector.scalar_tensor_tensor(out=st.wcat[:, c, 0:C3], in0=psum[0:st.kp, 0, 0:C3],
                                                      scalar=st.ninv[:, c:c + 1], in1=st.wcat[:, c, 0:C3],
                                                      op0=ALU.mult, op1=ALU.add)
            last.then_inc(w["centered"], 1)
            dve.wait_ge(w["biased"], c0)
            nc.vector.tensor_tensor(st.bias[:, 0:C3], psum[:, 1, 0:C3], st.kqvb[:, :], ALU.add).then_inc(w["bias_set"], 1)
            for c in range(st.nk + 1):
                rows = st.kp if c < st.nk else P
                step = st.t0 + c + 1
                dve.wait_ge(w["turned"], step)
                nc.vector.tensor_copy(turned[:, :, 0:rows], psum[0:EMB, 2, 0:2 * rows].rearrange(
                    "p (s r) -> p s r", s=2)).then_inc(w["turned_copied"], 1)
                dve.wait_ge(w["folded"], step)
                dst = st.wcat[:, c, WK:WK + 2 * M] if c < st.nk else st.bias[:, WK:WK + 2 * M]
                nc.vector.tensor_copy(dst, psum[0:rows, 3, 0:2 * M]).then_inc(w["folded_copied"], 1)
            nc.vector.tensor_scalar(st.w1c[:, :], st.w1[:, :], st.cols[:, 0:1], None, ALU.mult).then_inc(w["mlp_scaled"], 1)
            dve.wait_ge(w["mlp_summed"], c0)
            dve.wait_ge(w["mlp_scaled"], c0)
            nc.vector.tensor_tensor(st.w1c[:, :], st.w1c[:, :], psum[:, 0, 0:P], ALU.subtract)
            nc.vector.tensor_tensor(st.b1c[:, :], psum[:, 1, 0:1], st.cols[:, 2:3], ALU.add).then_inc(w["mlp_set"], 1)

        def dve_var(dve, st, j, par, half):
            n = nth(j, par)
            c = n * 2 + (2 * st.k0 + half + 1)
            nt = st.nt
            two_chunks = slice(2 * half, 2 * half + 2)
            dve.wait_ge(k["main"], NCH * n + (NCH * st.k0 + 2 * half + 2))
            nc.vector.tensor_copy(stat[0:nt, two_chunks, :], psum[0:nt, two_chunks, MEAN:SQ + 1]).then_inc(k["stat"], 1)
            dve.wait_ge(k["stat"], c)
            nc.vector.tensor_tensor(sqm[0:nt, two_chunks], stat[0:nt, two_chunks, 0], stat[0:nt, two_chunks, 0], ALU.mult
                                    ).then_inc(k["square_mean"], 1)
            dve.wait_ge(k["square_mean"], c)
            nc.vector.tensor_tensor(var[0:nt, two_chunks], stat[0:nt, two_chunks, 1], sqm[0:nt, two_chunks], ALU.subtract
                                    ).then_inc(k["var"], 1)
            dve.wait_ge(k["var"], c)
            nc.vector.tensor_scalar(var_eps[0:nt, two_chunks], var[0:nt, two_chunks], 0.0, EPS, ALU.max, ALU.add
                                    ).then_inc(k["var_eps"], 1)

        def dve_z(dve, st, j, par, half):
            n = nth(j, par)
            nt = st.nt
            if not peeled(j):
                dve.wait_ge(k["kvq"], n + (st.k0 - 1))
                dve.wait_ge(k["vb"], n + (st.k0 - 1))
            dve.wait_ge(k["rstd"], n * 2 + (2 * st.k0 + half + 1))
            for i in (2 * half, 2 * half + 1):
                nc.vector.scalar_tensor_tensor(out=z[par][0:nt, i, :], in0=psum[0:nt, i, 0:MEAN],
                                               scalar=rstd[0:nt, i:i + 1], in1=st.bias[0:nt, :],
                                               op0=ALU.mult, op1=ALU.add).then_inc(k["z"], 1)

        def dve_taps(dve, st, j, par):
            if st.stage == 1:
                return
            n = nth(j, par)
            dve.wait_ge(k["xsq"], n + (st.k0 + 1))
            if not peeled(j):
                dve.wait_ge(k["main"], NCH * (n + (st.k0 - 1)))
            nc.vector.tensor_reduce(
                tapsum[par][:, 0:NCH * T2].rearrange("p (c t) -> p c t", c=NCH),
                xsqbuf[:, :].rearrange("p (c k t) -> p c t k", c=NCH, k=NTAP), AX_X, ALU.add).then_inc(k["taps"], 1)

        def dve_xd(dve, st, j, par):
            n = nth(j, par)
            c = n + (st.k0 + 1)
            nt = st.nt
            dve.wait_ge(k["kqsq"], c)
            nc.vector.tensor_reduce(xd[0:nt, :, :], kqsq[0:nt, :, :, :], AX_X, ALU.add).then_inc(k["xd"], 1)

        def dve_arg(dve, st, j, par):
            n = nth(j, par)
            c = n + (st.k0 + 1)
            nt = st.nt
            dve.wait_ge(k["xd"], c)
            dve.wait_ge(k["e"], n + st.k0)
            nc.vector.scalar_tensor_tensor(out=arg[0:nt, :, :, :],
                                           in0=xd[0:nt, :, :].unsqueeze(3).broadcast_to([nt, NCH, 2, M]),
                                           scalar=-0.5, in1=z[par][0:nt, :, WK:WK + 2 * M].rearrange(
                                               "p c (s m) -> p c s m", s=2),
                                           op0=ALU.mult, op1=ALU.add).then_inc(k["arg"], 1)

        def dve_back(dve, st, j, par):
            n = nth(j, par)
            c = n + (st.k0 + 1)
            nt = st.nt
            yp = psum[0:nt, 6, 0:NCH * (EMB + 1)].rearrange("p (c e) -> p c e", c=NCH)
            dve.wait_ge(k["yp"], c)
            nc.vector.tensor_scalar(den[0:nt, :], yp[:, :, EMB], 1e-8, None, ALU.add).then_inc(k["den"], 1)
            dve.wait_ge(k["den"], c)
            nc.vector.reciprocal(rec[0:nt, :], den[0:nt, :]).then_inc(k["rec"], 1)
            dve.wait_ge(k["rec"], c)
            dve.wait_ge(k["y"], n + st.k0)
            nc.vector.tensor_tensor(yn[0:nt, :, :], yp[:, :, 0:EMB],
                                    rec[0:nt, :].unsqueeze(2).broadcast_to([nt, NCH, EMB]), ALU.mult
                                    ).then_inc(k["yn"], 1)

        def dve_gather(dve, st, j, par):
            if st.stage == 2:
                gather_x(dve, nc.vector.tensor_copy, x_made["dve"], j, par, 1)

        def dve_performer(dve, st):
            dve_gather(dve, st, 0, 0)
            dve_taps(dve, st, 0, 0)

            def period(j, par, live):
                if live(-1):
                    dve_gather(dve, st, *before(j, par, -1))
                if live(0):
                    dve_var(dve, st, j, par, 0)
                if live(1):
                    dve_xd(dve, st, *before(j, par, 1))
                if live(0):
                    dve_z(dve, st, j, par, 0)
                if live(-1):
                    dve_taps(dve, st, *before(j, par, -1))
                if live(1):
                    dve_arg(dve, st, *before(j, par, 1))
                if live(0):
                    dve_var(dve, st, j, par, 1)
                if live(2):
                    dve_back(dve, st, j - 1, par)
                if live(0):
                    dve_z(dve, st, j, par, 1)

            performer_periods(dve, st, period)

        def dve_sums(dve, st, j, par):
            n = nth(j, par)
            c = n + (st.m0 + 1)
            nt = st.nt
            rows = mlp_rows(st, j, par).rearrange("p c (i e) -> p (c i) e", i=2)
            nc.vector.tensor_reduce(sum1[0:nt, :], rows, AX_X, ALU.add).then_inc(m["sum1"], 1)
            dve.wait_ge(m["sq"], c)
            nc.vector.tensor_reduce(sum2[0:nt, :], ysq[par][0:nt, :, :], AX_X, ALU.add).then_inc(m["sum2"], 1)
            dve.wait_ge(m["sum1"], c)
            nc.vector.scalar_tensor_tensor(out=sqm[0:nt, :], in0=sum1[0:nt, :], scalar=1.0 / (EMB * EMB),
                                           in1=sum1[0:nt, :], op0=ALU.mult, op1=ALU.mult).then_inc(m["square_mean"], 1)
            dve.wait_ge(m["sum2"], c)
            dve.wait_ge(m["square_mean"], c)
            nc.vector.scalar_tensor_tensor(out=var[0:nt, :], in0=sum2[0:nt, :], scalar=1.0 / EMB,
                                           in1=sqm[0:nt, :], op0=ALU.mult, op1=ALU.subtract).then_inc(m["var"], 1)
            dve.wait_ge(m["var"], c)
            nc.vector.tensor_scalar(var_eps_m[par][0:nt, :], var[0:nt, 0:2 * NCH], 0.0, EPS, ALU.max, ALU.add
                                    ).then_inc(m["var_eps"], 1)

        def dve_scaled(dve, st, j, par):
            n = nth(j, par)
            nt = st.nt
            dve.wait_ge(m["rstd"], n + (st.m0 + 1))
            if not peeled(j):
                dve.wait_ge(m["tr"], n + (st.m0 - 1))
            nc.vector.tensor_tensor(ynm[par][0:nt, :, :].rearrange("p c (i e) -> p (c i) e", i=2),
                                    mlp_rows(st, j, par).rearrange("p c (i e) -> p (c i) e", i=2),
                                    rstd_m[par][0:nt, :].unsqueeze(2).broadcast_to([nt, 2 * NCH, EMB]), ALU.mult
                                    ).then_inc(m["yn"], 1)

        def dve_out(dve, st, j, par):
            n = nth(j, par)
            dve.wait_ge(m["w2"], n + (st.m0 + 1))
            src = psum[:, 4 + par, 0:st.columns]
            if st.stage == 1:
                dst = y1_all[:, bass.ds(n, 1), :].rearrange("p o (r c) -> p (o r) c", c=PAD1)[:, 1:1 + S1, 1:1 + S1]
                src = src.rearrange("p (r c) -> p r c", c=S1)
            else:
                dst = y2_all[:, bass.ds(n * NCH, NCH), :].rearrange("p n (r c) -> p n r c", c=PAD2
                                                                    )[:, :, 1:1 + S2, 1:1 + S2]
                src = src.rearrange("p (n r c) -> p n r c", n=NCH, c=S2)
            nc.vector.tensor_scalar(dst, src, st.cols[:, 3:4], None, ALU.add).then_inc(m["out"], 1)

        def dve_mlp(dve, st):
            dve.wait_ge(k["y"], st.k0 + st.units)

            def period(j, par, live):
                if live(0):
                    dve_sums(dve, st, j, par)
                if live(1):
                    dve_scaled(dve, st, *before(j, par, 1))
                if live(3):
                    dve_out(dve, st, *before(j, par, 3))

            mlp_periods(dve, st, period)

        @block.vector
        def _(dve):
            dve.wait_ge(const_set, 1)
            dve_prepare(dve, one)
            dve_prepare(dve, two)
            dve_performer(dve, one)
            dve.wait_ge(zeroed, 1)
            dve_mlp(dve, one)
            dve.wait_ge(m["out"], two.m0)
            for x in xbuf:
                last = nc.vector.memset(x[EMB:P, :].rearrange("p (c k t) -> p c k t", c=NCH, k=NTAP)[:, :, NTAP - 1, :], 0.0)
            last.then_inc(x_made["zero"], 1)
            dve_performer(dve, two)
            dve.wait_ge(zeroed, 2)
            dve_mlp(dve, two)
            dve.wait_ge(t_in, 16 * 12)
            nc.vector.tensor_scalar(qscale[:, 1:2], qscale[:, 0:1], 0.01, None, ALU.max).then_inc(clipped, 1)
            dve.wait_ge(clipped, 1)
            nc.vector.reciprocal(qscale[:, 2:3], qscale[:, 1:2]).then_inc(clipped, 1)
            nc.vector.memset(qscale[:, 3:4], HD ** -0.5)
            dve.wait_ge(clipped, 2)
            nc.vector.tensor_scalar(qscale[:, 2:3], qscale[:, 2:3], HD ** -0.5, None, ALU.mult).then_inc(scale_set, 1)

            with dve.Fori(0, NG // LANES) as it:
                for ln in lanes:
                    g = it * LANES + (ln.i + 1)
                    dve.wait_ge(t["hp"], g + 1)
                    nc.vector.tensor_tensor(ln.h, psum[0:GT, 4 * ln.i, 0:D], pb[0:GT, :], ALU.add).then_inc(t["h"], 1)
                for att in range(2):
                    for ln in lanes:
                        c = it * (2 * LANES) + (att * LANES + ln.i + 1)
                        g = it * LANES + (ln.i + 1)
                        if att == 0:
                            dve.wait_ge(t["h"], g)
                        else:
                            dve.wait_ge(t["s0"], g)
                        nc.vector.bn_stats(ln.bn, ln.h).then_inc(u["bn"], 1)
                        dve.wait_ge(u["bn"], c)
                        plain(dve)
                        nc.vector.bn_aggr(ln.mv, ln.bn).then_inc(u["mv"], 1)
                        dve.wait_ge(u["mv"], c)
                        nc.vector.tensor_scalar(ln.veps, ln.mv[:, 1:2], 0.0, EPS, ALU.max, ALU.add
                                                ).then_inc(u["veps"], 1)
                    for ln in lanes:
                        c = it * (2 * LANES) + (att * LANES + ln.i + 1)
                        dve.wait_ge(u["r"], c)
                        nc.vector.tensor_scalar(ln.hn, ln.h, ln.mv[:, 0:1], ln.r, ALU.subtract, ALU.mult
                                                ).then_inc(u["hn"], 1)
                    if att == 1:
                        for ln in lanes:
                            g = it * LANES + (ln.i + 1)
                            rt = psum[0:GT, 4 * ln.i, D:D + NEXP + P]
                            dve.wait_ge(t["rt"], g)
                            nc.vector.tensor_copy(ln.lg[:, 0:NEXP], rt[:, 0:NEXP]).then_inc(t["lg"], 1)
                            dve.wait_ge(t["lg"], g)
                            plain(dve)
                            nc.vector.max(out=ln.l8, in_=ln.lg[:, 0:NEXP]).then_inc(t["l8"], 1)
                            dve.wait_ge(t["l8"], g)
                            nc.vector.tensor_copy(ln.rep[:, 0:TOP_K], ln.l8[:, 0:TOP_K]).then_inc(t["rep"], 1)
                            nc.vector.tensor_scalar(ln.lm, ln.lg[:, 0:NEXP], ln.l8[:, 0:1], None, ALU.subtract
                                                    ).then_inc(t["lm"], 1)
                            dve.wait_ge(t["rep"], g)
                            plain(dve)
                            nc.vector.match_replace(out=ln.lg2, in_to_replace=ln.rep, in_values=ln.lg,
                                                    imm_value=HUGE).then_inc(t["found"], 1)
                            dve.wait_ge(t["found"], g)
                            nc.vector.tensor_scalar(ln.sel, ln.lg2[:, 0:NEXP], HUGE, ALPHA / RANK, ALU.is_ge,
                                                    ALU.mult).then_inc(t["sel"], 1)
                        for ln in lanes:
                            g = it * LANES + (ln.i + 1)
                            rt = psum[0:GT, 4 * ln.i, D:D + NEXP + P]
                            dve.wait_ge(t["le"], g)
                            nc.vector.tensor_reduce(ln.ls, ln.le, AX_X, ALU.add).then_inc(t["lr"], 1)
                            dve.wait_ge(t["lr"], it * (2 * LANES) + (2 * ln.i + 1))
                            nc.vector.reciprocal(ln.lr, ln.ls).then_inc(t["lr"], 1)
                            dve.wait_ge(t["sel"], g)
                            nc.vector.tensor_tensor(ln.lw, ln.le, ln.sel, ALU.mult).then_inc(t["lw"], 1)
                            dve.wait_ge(t["lr"], it * (2 * LANES) + (2 * ln.i + 2))
                            dve.wait_ge(t["lw"], g)
                            nc.vector.tensor_scalar(ln.lw2, ln.lw, ln.lr, None, ALU.mult).then_inc(t["lw2"], 1)
                            dve.wait_ge(t["lw2"], g)
                            nc.vector.tensor_tensor(
                                ln.aw.rearrange("p (n r) -> p n r", r=RANK),
                                rt[:, NEXP:NEXP + P].rearrange("p (n r) -> p n r", r=RANK),
                                ln.lw2.unsqueeze(2).broadcast_to([GT, NEXP, RANK]), ALU.mult).then_inc(t["aw"], 1)
                    for ln in lanes:
                        c = it * (2 * LANES) + (att * LANES + ln.i + 1)
                        dve.wait_ge(u["v3"], c)
                        nc.vector.tensor_tensor(ln.vx[:, 0:2, :], psum[0:GT, 4 * ln.i + 3, 0:2 * D].rearrange(
                            "p (i f) -> p i f", i=2), vmask[:, :].unsqueeze(1).broadcast_to([GT, 2, D]), ALU.mult)
                        nc.vector.tensor_tensor(ln.vx[:, 2, :], psum[0:GT, 4 * ln.i, 0:D], vmask[:, :], ALU.mult
                                                ).then_inc(u["vx"], 1)
                    for ln in lanes:
                        c = it * (2 * LANES) + (att * LANES + ln.i + 1)
                        g = it * LANES + (ln.i + 1)
                        dve.wait_ge(u["h"], c)
                        if att == 1:
                            nc.vector.tensor_reduce(ln.mx, ln.s0, AX_X, ALU.max).then_inc(u["mx"], 1)
                            continue
                        plain(dve)
                        tops = it * (5 * LANES) + (5 * ln.i)
                        for hd in range(HEADS):
                            last = nc.vector.max(out=ln.top[0][:, hd, :], in_=ln.s0[:, hd, :])
                        last.then_inc(t["top8"], 1)
                        dve.wait_ge(t["top8"], tops + 1)
                        nc.vector.tensor_copy(ln.mx, ln.top[0][:, :, 0]).then_inc(u["mx"], 1)
                        for hd in range(HEADS):
                            last = nc.vector.match_replace(out=ln.s2[:, hd, :], in_to_replace=ln.top[0][:, hd, :],
                                                           in_values=ln.s0[:, hd, :], imm_value=-HUGE)
                        last.then_inc(t["top8"], 1)
                        dve.wait_ge(t["top8"], tops + 2)
                        plain(dve)
                        for hd in range(HEADS):
                            last = nc.vector.max(out=ln.top[1][:, hd, :], in_=ln.s2[:, hd, :])
                        last.then_inc(t["top8"], 1)
                        dve.wait_ge(t["top8"], tops + 3)
                        plain(dve)
                        for hd in range(HEADS):
                            last = nc.vector.match_replace(out=ln.keep[:, hd, :], in_to_replace=ln.top[1][:, hd, :],
                                                           in_values=ln.s2[:, hd, :], imm_value=-HUGE)
                        last.then_inc(t["top8"], 1)
                        dve.wait_ge(t["top8"], tops + 4)
                        plain(dve)
                        for hd in range(HEADS):
                            last = nc.vector.max(out=ln.top[2][:, hd, :], in_=ln.keep[:, hd, :])
                        last.then_inc(t["top8"], 1)
                        dve.wait_ge(t["top8"], tops + 5)
                        nc.vector.tensor_tensor(ln.keep, ln.s0, per_head(ln.top[2][:, :, KEEP - 17]), ALU.is_ge
                                                ).then_inc(t["keep"], 1)
                    for ln in lanes:
                        c = it * (2 * LANES) + (att * LANES + ln.i + 1)
                        if att == 0:
                            dve.wait_ge(t["em"], it * LANES + (ln.i + 1))
                        else:
                            dve.wait_ge(u["exp"], c)
                        nc.vector.tensor_reduce(ln.sm, ln.s2, AX_X, ALU.add).then_inc(u["sum"], 1)
                        dve.wait_ge(u["sum"], c)
                        nc.vector.reciprocal(ln.rs, ln.sm).then_inc(u["rs"], 1)
                    for ln in lanes:
                        c = it * (2 * LANES) + (att * LANES + ln.i + 1)
                        dve.wait_ge(u["pj"], c)
                        pj = psum[0:GT, 4 * ln.i, 0:D]
                        if att == 0:
                            nc.vector.tensor_tensor(ln.h, ln.h, pj, ALU.add).then_inc(t["s0"], 1)
                        else:
                            dve.wait_ge(ln.res_out, it * 16 + 16)
                            nc.vector.tensor_tensor(ln.res, ln.h, pj, ALU.add).then_inc(ln.res_ready, 1)

        def pe_prepare(pe, st):
            c0 = st.w0 + 1
            pe.wait_ge(w["scaled"], c0)
            if st.w0:
                pe.wait_ge(w["mlp_set"], st.w0)
            for c in range(st.nk):
                last = nc.tensor.matmul(psum[:, 0, 0:C3], ones_sq[0:st.kp, :], st.wcat[:, c, 0:C3],
                                        start=(c == 0), stop=(c == st.nk - 1))
            last.then_inc(w["summed"], 1)
            for c in range(st.nk):
                last = nc.tensor.matmul(psum[:, 1, 0:C3], wide[0:st.kp, c, :], st.wraw[:, c, :],
                                        start=(c == 0), stop=(c == st.nk - 1))
            last.then_inc(w["biased"], 1)
            pe.wait_ge(w["centered"], c0)
            pe.wait_ge(w["bias_set"], c0)
            for c in range(st.nk + 1):
                rows = st.kp if c < st.nk else P
                step = st.t0 + c
                src = st.wcat[:, c, :] if c < st.nk else st.bias[:, :]
                if step:
                    pe.wait_ge(w["folded_copied"], step)
                for s in range(2):
                    last = nc.tensor.transpose(psum[0:EMB, 2, s * rows:(s + 1) * rows],
                                               src[:, EMB * s:EMB * s + EMB], ident[0:rows, 0:rows])
                last.then_inc(w["turned"], 1)
                pe.wait_ge(w["turned_copied"], step + 1)
                for s in range(2):
                    last = nc.tensor.matmul(psum[0:rows, 3, M * s:M * s + M], turned[:, s, 0:rows], st.wT[:, :],
                                            start=True, stop=True)
                last.then_inc(w["folded"], 1)
            pe.wait_ge(w["mlp_scaled"], c0)
            nc.tensor.matmul(psum[:, 0, 0:P], blockmean[:, :], st.w1c[:, :], start=True, stop=True)
            nc.tensor.matmul(psum[:, 1, 0:1], st.w1[:, :], st.cols[:, 1:2], start=True, stop=True
                             ).then_inc(w["mlp_summed"], 1)

        def pe_main(pe, st, j, par, c):
            n = nth(j, par)
            if c == 0:
                pe.wait_ge(k["taps"], n + (st.k0 + 1))
            pe.wait_ge(k["z"], NCH * (n + (st.k0 - 1)) + (c + 1))
            for kk in range(st.nk):
                rows = krows(st, kk)
                columns = SQ + 1 if st.stage == 1 else MEAN + 1
                last = nc.tensor.matmul(psum[0:st.nt, c, 0:columns], patches(st, xbuf[par], c, kk),
                                        st.wcat_all[0:rows, kk, 0:columns], start=(kk == 0), stop=(kk == st.nk - 1))
            if st.stage == 1:
                last.then_inc(k["main"], 1)
                return
            nc.tensor.matmul(psum[0:st.nt, c, SQ:SQ + 1], tapsum[par][0:st.kp, st.nt * c:st.nt * c + st.nt],
                             st.inv[:, 0:1], start=True, stop=True).then_inc(k["main"], 1)

        def pe_channels(pe, st, j, par):
            if st.stage == 2:
                return
            n = nth(j, par)
            pe.wait_ge(k["xsq"], n + (st.k0 + 1))
            nc.tensor.matmul(psum[0:2 * BLK * BLK, 7, 0:GRID * S1], channels[:, :], X1q,
                             start=True, stop=True).then_inc(k["chan"], 1)

        def pe_kvq(pe, st, j, par):
            n = nth(j, par)
            pe.wait_ge(k["e"], n + (st.k0 + 1))
            pe.wait_ge(k["mp_copied"], n + st.k0)
            for c in range(NCH):
                rows = st.real[c]
                kc = 0 if st.shared_kv else c
                nc.tensor.matmul(psum[0:EMB + 1, 4, M * kc:M * kc + M], z[par][0:rows, c, V0:ONE + 1],
                                 e[par][0:rows, c, 0, :], start=(c == 0 or not st.shared_kv),
                                 stop=(c == NCH - 1 or not st.shared_kv))
            for c in range(NCH):
                last = nc.tensor.transpose(psum[0:M, 5, st.nt * c:st.nt * c + st.nt], e[par][0:st.nt, c, 1, :],
                                           ident[0:st.nt, 0:st.nt])
            last.then_inc(k["kvq"], 1)

        def pe_mp(pe, st, j, par):
            n = nth(j, par)
            pe.wait_ge(k["kvq_copied"], n + (st.k0 + 1))
            for c in range(1 if st.shared_kv else NCH):
                last = nc.tensor.matmul(psum[0:M, 4, P + (EMB + 1) * c:P + (EMB + 1) * (c + 1)], kv[:, c, :],
                                        st.paug[:, :], start=True, stop=True)
            last.then_inc(k["mp"], 1)

        def pe_y(pe, st, j, par):
            n = nth(j, par)
            pe.wait_ge(k["mp_copied"], n + (st.k0 + 1))
            pe.wait_ge(k["yn"], n + st.k0)
            for c in range(NCH):
                last = nc.tensor.matmul(psum[0:st.nt, 6, (EMB + 1) * c:(EMB + 1) * (c + 1)],
                                        qT[:, st.nt * c:st.nt * c + st.nt], mp[:, 0 if st.shared_kv else c, :],
                                        start=True, stop=True)
            last.then_inc(k["yp"], 1)

        def pe_performer(pe, st):
            pe_channels(pe, st, 0, 0)

            def period(j, par, live):
                for c in range(NCH):
                    if live(0):
                        pe_main(pe, st, j, par, c)
                    if live(2) and c == 0:
                        pe_kvq(pe, st, j - 1, par)
                    if live(2) and c == 1:
                        pe_mp(pe, st, j - 1, par)
                    if live(-1) and c == 2:
                        pe_channels(pe, st, *before(j, par, -1))
                    if live(2) and c == 2:
                        pe_y(pe, st, j - 1, par)

            performer_periods(pe, st, period)

        def pe_turn(pe, st, j, par):
            n = nth(j, par)
            pe.wait_ge(m["yn"], n + (st.m0 + 1))
            at = 0
            for c in range(NCH):
                rows = st.real[c]
                last = nc.tensor.transpose(psum[:, par, at:at + rows], ynm[par][0:rows, c, :], ident[0:rows, 0:rows])
                at += rows
            last.then_inc(m["tr"], 1)

        def pe_w1(pe, st, j, par):
            n = nth(j, par)
            pe.wait_ge(m["tr_copied"], n + (st.m0 + 1))
            nc.tensor.matmul(psum[:, 2 + par, 0:st.columns], st.w1c[:, :], ynT[par][:, 0:st.columns],
                             start=True, stop=True).then_inc(m["w1"], 1)

        def pe_w2(pe, st, j, par):
            n = nth(j, par)
            pe.wait_ge(m["gelu"], n + (st.m0 + 1))
            pe.wait_ge(m_in[par], j * 16 + (st.y0 + 16))
            if not peeled(j):
                pe.wait_ge(m["out"], n + (st.m0 - 1))
            nc.tensor.matmul(psum[:, 4 + par, 0:st.columns], st.w2[:, :], gel[par][:, 0:st.columns],
                             start=True, stop=False)
            at = 0
            for c in range(NCH):
                rows = st.real[c]
                last = nc.tensor.matmul(psum[:, 4 + par, at:at + rows], yres[par][0:rows, c, :],
                                        ident[0:rows, 0:rows], start=False, stop=(c == NCH - 1))
                at += rows
            last.then_inc(m["w2"], 1)

        def pe_mlp(pe, st):
            def period(j, par, live):
                if live(3):
                    pe_w2(pe, st, *before(j, par, 3))
                if live(2):
                    pe_w1(pe, st, *before(j, par, 2))
                if live(1):
                    pe_turn(pe, st, *before(j, par, 1))

            mlp_periods(pe, st, period)

        @block.tensor
        def _(pe):
            pe.wait_ge(const_in, 64)
            pe.wait_ge(const_set, 1)
            pe_prepare(pe, one)
            pe_prepare(pe, two)
            pe.wait_ge(w["folded_copied"], one.nk + two.nk + 2)
            pe.wait_ge(w["mlp_set"], 2)
            pe_performer(pe, one)
            pe_mlp(pe, one)
            pe_performer(pe, two)
            pe_mlp(pe, two)
            pe.wait_ge(t_in, 16 * 12)
            pe.wait_ge(m["out"], two.m0 + two.mlp_units)

            with pe.Fori(0, NG // LANES) as it:
                for ln in lanes:
                    pe.wait_ge(t["g"], it + 1)
                    pe.wait_ge(ln.res_ready, it + 1)
                    for kk in range(NTAP):
                        rows = EMB * len(TAPS[kk])
                        last = nc.tensor.matmul(psum[0:GT, 4 * ln.i, 0:D], g_tile[0:rows, kk, GT * ln.i:GT * ln.i + GT],
                                                pw[0:rows, kk, :], start=(kk == 0), stop=(kk == NTAP - 1))
                    last.then_inc(t["hp"], 1)
                for att in range(2):
                    w_qkv, w_proj = wqkv[att], wproj[att]
                    for ln in lanes:
                        c = it * (2 * LANES) + (att * LANES + ln.i + 1)
                        pe.wait_ge(u["hn"], c)
                        for half in range(2):
                            last = nc.tensor.transpose(psum[0:HALF, 4 * ln.i + 1, GT * half:GT * half + GT],
                                                       ln.hn[:, HALF * half:HALF * half + HALF], ident[0:GT, 0:GT])
                        last.then_inc(u["tr"], 1)
                    if att == 1:
                        for ln in lanes:
                            c = it * (2 * LANES) + (att * LANES + ln.i + 1)
                            pe.wait_ge(u["hnT"], c)
                            dst = psum[0:GT, 4 * ln.i, D:D + NEXP + P]
                            nc.tensor.matmul(dst, ln.hnT[:, 0, :], wrout[:, 0, :], start=True, stop=False)
                            nc.tensor.matmul(dst, ln.hnT[0:HALF, 1, :], wrout[0:HALF, 1, :], start=False, stop=True
                                             ).then_inc(t["rt"], 1)
                    for ln in lanes:
                        c = it * (2 * LANES) + (att * LANES + ln.i + 1)
                        g = it * LANES + (ln.i + 1)
                        pe.wait_ge(u["hnT"], c)
                        if att == 1:
                            pe.wait_ge(t["aw"], g)
                            nc.tensor.transpose(psum[:, 4 * ln.i + 1, 0:GT], ln.aw, ident[0:GT, 0:GT]).then_inc(t["at"], 1)
                            pe.wait_ge(t["aT"], g)
                        for part in range(4):
                            dst = psum[0:HALF, 4 * ln.i + 2, GT * part:GT * part + GT]
                            cols = slice(HALF * part, HALF * part + HALF)
                            nc.tensor.matmul(dst, w_qkv[:, 0, cols], ln.hnT[:, 0, :], start=True, stop=False)
                            last = nc.tensor.matmul(dst, w_qkv[0:HALF, 1, cols], ln.hnT[0:HALF, 1, :],
                                                    start=False, stop=(att == 0))
                            if att == 1:
                                last = nc.tensor.matmul(dst, blora[:, cols], ln.aT, start=False, stop=True)
                        last.then_inc(u["qk"], 1)
                        dst = psum[0:GT, 4 * ln.i, 0:D]
                        cols = slice(2 * D, 3 * D)
                        nc.tensor.matmul(dst, ln.hnT[:, 0, :], w_qkv[:, 0, cols], start=True, stop=False)
                        last = nc.tensor.matmul(dst, ln.hnT[0:HALF, 1, :], w_qkv[0:HALF, 1, cols],
                                                start=False, stop=(att == 0))
                        if att == 1:
                            last = nc.tensor.matmul(dst, ln.aT, blora[:, cols], start=False, stop=True)
                        last.then_inc(u["v"], 1)
                    for ln in lanes:
                        c = it * (2 * LANES) + (att * LANES + ln.i + 1)
                        pe.wait_ge(u["vt"], c)
                        for i in range(GI):
                            dst = (psum[0:GT, 4 * ln.i + 3, D * i:D * i + D] if i < 2 else psum[0:GT, 4 * ln.i, 0:D])
                            last = nc.tensor.matmul(dst, thrice[:, i, :], ln.vt, start=True, stop=True)
                        last.then_inc(u["v3"], 1)
                    for ln in lanes:
                        c = it * (2 * LANES) + (att * LANES + ln.i + 1)
                        pe.wait_ge(u["kx"], c)
                        for half in range(2):
                            for i in range(GI):
                                last = nc.tensor.matmul(
                                    psum[0:GT, 4 * ln.i + 1, 216 * half:216 * half + 216],
                                    ln.qx[:, half, GT * i:GT * i + GT], ln.kx[:, half, 216 * i:216 * i + 216],
                                    start=(i == 0), stop=(i == GI - 1))
                        last.then_inc(u["s"], 1)
                    for ln in lanes:
                        c = it * (2 * LANES) + (att * LANES + ln.i + 1)
                        pe.wait_ge(u["p"], c)
                        pe.wait_ge(u["vx"], c)
                        for tri in range(TRI):
                            last = nc.tensor.transpose(
                                psum[0:GT, 4 * ln.i + 3, GT * tri:GT * tri + GT],
                                ln.s0[:, 3 * tri:3 * tri + 3, :].rearrange("p h t -> p (h t)"), ident[0:GT, 0:GT])
                        last.then_inc(u["pt"], 1)
                    for ln in lanes:
                        c = it * (2 * LANES) + (att * LANES + ln.i + 1)
                        pe.wait_ge(u["pT"], c)
                        for tri in range(TRI):
                            for i in range(GI):
                                at = GT * tri + T3 * i
                                last = nc.tensor.matmul(psum[0:3 * HD, 4 * ln.i + 2, at:at + T3],
                                                        ln.vx[:, i, 3 * HD * tri:3 * HD * tri + 3 * HD],
                                                        ln.pT[:, at:at + T3], start=True, stop=True)
                        last.then_inc(u["o"], 1)
                    for ln in lanes:
                        c = it * (2 * LANES) + (att * LANES + ln.i + 1)
                        pe.wait_ge(u["oT"], c)
                        for tri in range(TRI):
                            rows = 3 * HD + 1 if tri == 0 else 3 * HD
                            last = nc.tensor.matmul(psum[0:GT, 4 * ln.i, 0:D], ln.oT[0:rows, GT * tri:GT * tri + GT],
                                                    w_proj[0:rows, tri, :], start=(tri == 0), stop=(tri == TRI - 1))
                        last.then_inc(u["pj"], 1)


def layout(inp):
    f = np.float32
    a = {}
    x = np.asarray(inp["x"])
    pad = np.zeros((B, 3, GRID * BLK, GRID * BLK), f)
    pad[:, :, 2:86, 2:86] = x
    blocks = pad.reshape(B, 3, GRID, BLK, GRID, BLK).transpose(0, 1, 3, 5, 2, 4).reshape(B, PIX, GRID, GRID)
    a["x"] = np.concatenate([blocks[..., 0:S1], blocks[..., 1:GRID]], 1).reshape(B, 2 * PIX, GRID * S1)
    a["ident"] = np.eye(P, dtype=f)
    half = np.arange(P) // EMB
    a["blockmean"] = (half[:, None] == half[None, :]).astype(f) / f(EMB)

    def rows1(v):
        full = np.zeros((3, 8, 8, v.shape[1]), f)
        full[:, :7, :7] = v.reshape(3, 7, 7, -1)
        full = full.reshape(3, 2, BLK, 2, BLK, -1)
        return full.transpose(3, 0, 2, 4, 1, 5).reshape(2 * PIX, 2, -1)

    def rows2(v):
        v = v.reshape(EMB, 3, 3, -1)
        full = np.zeros((P, NTAP, v.shape[-1]), f)
        for kk, taps in enumerate(TAPS):
            for upper, (kh, kw) in enumerate(taps):
                full[EMB * upper:EMB * upper + EMB, kk] = v[:, kh, kw]
        return full

    def twice(v):
        out = np.zeros((P, P), f)
        out[0:EMB, 0:EMB] = v
        out[EMB:P, EMB:P] = v
        return out

    for name, rows, feats in (("a1", rows1, F1), ("a2", rows2, F2)):
        g = {key: np.asarray(inp[f"L0_tok_{name}_{key}"]) for key in
             ("n1g", "n1b", "kqvw", "kqvb", "projw", "projb", "n2g", "n2b", "w1", "b1", "w2", "b2", "w")}
        a[name + "_w"] = rows(g["kqvw"])
        a[name + "_g"] = rows(g["n1g"][:, None])[:, :, 0]
        a[name + "_b"] = rows(g["n1b"][:, None])[:, :, 0]
        real = rows(np.ones((feats, 1), f))[:, :, 0]
        a[name + "_inv"] = (real / f(feats)).astype(f)
        if name == "a1":
            sq = np.zeros((P, 2), f)
            sq[2 * PIX:P] = (real / f(feats)).reshape(2, 3, BLK * BLK, 2)[:, 0].reshape(2 * BLK * BLK, 2)
            a["sq_weights"] = sq
            a["channels"] = np.kron(np.eye(2), np.kron(np.ones((3, 1)), np.eye(BLK * BLK))).astype(f)
        a[name + "_ninv"] = -a[name + "_inv"]
        a[name + "_kqvb"] = np.broadcast_to(g["kqvb"], (P, C3))
        a[name + "_pjb"] = np.broadcast_to(g["projb"], (P, EMB))
        paug = np.zeros((EMB + 1, EMB + 1), f)
        paug[0:EMB, 0:EMB] = g["projw"]
        paug[EMB, EMB] = 1.0
        a[name + "_paug"] = paug
        a[name + "_wT"] = g["w"].T
        a[name + "_w1"] = twice(g["w1"])
        a[name + "_w2"] = twice(g["w2"])
        a[name + "_cols"] = np.stack([np.concatenate([v, v]) for v in (g["n2g"], g["n2b"], g["b1"], g["b2"])], 1)
    a["pw"] = rows2(np.asarray(inp["L0_tok_proj_w"]))
    a["pb"] = np.broadcast_to(np.asarray(inp["L0_tok_proj_b"]), (P, D))

    def with_bias(w, b):
        full = np.zeros((HALF + 1, 2, w.shape[0]), f)
        full[0:HALF] = w.T.reshape(2, HALF, -1).transpose(1, 0, 2)
        full[HALF, 0] = b
        return full

    def by_triple(w, b):
        full = np.zeros((3 * HD + 1, TRI, D), f)
        full[0:3 * HD] = w.T.reshape(TRI, 3 * HD, D).transpose(1, 0, 2)
        full[3 * HD, 0] = b
        return full

    v = {key: np.asarray(inp["L0_" + key]) for key in
         ("attn_qkv_w", "attn_qkv_b", "attn_proj_w", "attn_proj_b", "attn_temperature", "ffn_W_qkv", "ffn_b_qkv",
          "ffn_W_gate", "ffn_b_gate", "ffn_A", "ffn_B_lora", "ffn_W_proj", "ffn_b_proj")}
    a["wqkv0"] = with_bias(v["attn_qkv_w"], v["attn_qkv_b"])
    a["wqkv1"] = with_bias(v["ffn_W_qkv"], v["ffn_b_qkv"])
    a["wproj0"] = by_triple(v["attn_proj_w"], v["attn_proj_b"])
    a["wproj1"] = by_triple(v["ffn_W_proj"], v["ffn_b_proj"])
    router = np.concatenate([v["ffn_W_gate"], v["ffn_A"].reshape(NEXP * RANK, D)], 0)
    a["wrout"] = with_bias(router, np.concatenate([v["ffn_b_gate"], np.zeros(P, f)]))
    a["blora"] = v["ffn_B_lora"].transpose(0, 2, 1).reshape(NEXP * RANK, 3 * D)
    a["temp"] = np.broadcast_to(v["attn_temperature"], (HALF, 1))
    a["kmask"] = (np.arange(HALF)[:, None] // HD == np.arange(6)[None, :]).astype(f)
    a["vmask"] = (np.arange(GT)[:, None] // T3 == np.arange(D)[None, :] // HD % 3).astype(f)
    tok = np.arange(GT)
    a["thrice"] = np.stack([(tok[:, None] == i * T3 + tok[None, :] % T3) for i in range(GI)], 1).astype(f)
    return a


def kernel(**inputs):
    import concourse.bacc as _bacc
    from concourse.bass_utils import run_bass_kernel_spmd as _run

    nc = _bacc.Bacc("TRN2", target_bir_lowering=False, num_devices=1)
    arrays, aps = {}, {}
    for name, v in layout(inputs).items():
        v = np.ascontiguousarray(v)
        arrays["in_" + name] = v
        aps[name] = nc.dram_tensor("in_" + name, v.shape, mybir.dt.from_np(v.dtype), kind="ExternalInput").ap()
    out = nc.dram_tensor("out_0", (NG * GT, D), F32, kind="ExternalOutput").ap()
    build(nc, aps, out)
    r = _run(nc, [arrays], core_ids=[0])
    return r.results[0]["out_0"][0:B * T3].reshape(B, T3, D)
```

```python
from contextlib import ExitStack

import numpy as np

import concourse.bass as bass
from concourse import mybir

F32 = mybir.dt.float32
ALU = mybir.AluOpType
ACT = mybir.ActivationFunctionType
AX_X = mybir.AxisListType.X

P = 128
B = 64
EMB, M = 64, 32
C3 = 3 * EMB
BLK = 4
GRID = 22
PIX = 3 * BLK * BLK
S1, S2, S3 = 21, 11, 6
T1, T2, T3 = S1 * S1, S2 * S2, S3 * S3
F1, F2 = 3 * 7 * 7, EMB * 9
NCH = 4
ROWS1 = 6
NT1 = ROWS1 * S1
XR = 25
NTAP = 5
TAPS = [((0, 0), (1, 0)), ((0, 1), (1, 1)), ((0, 2), (1, 2)), ((2, 0), (2, 1)), ((2, 2),)]
PAD1, PAD2 = S1 + 2, S2 + 2
MAP1, MAP2 = PAD1 * PAD1, PAD2 * PAD2
V0, ONE, WK, MEAN, SQ = 128, 192, 193, 257, 258
D = 192
HEADS, HD = 12, 16
GI, NG = 3, 22
GT = GI * T3
TRI = HEADS // 3
PAIR = 64 + 3 * HD
HALF = D // 2
NEXP, RANK, TOP_K, ALPHA = 8, 16, 2, 32
KEEP = T3 // 2
DEPTH = 5
EPS = 1e-5
MLP_DEPTH = 5
HUGE = 3.0e38


class Part:
    pass


def performer_sizes():
    one = Part()
    one.name = 'a1'
    one.stage = 1
    one.nk = 2
    one.kp = 2 * PIX
    one.nt = NT1
    one.units = B
    one.shared_kv = True
    one.real = [NT1, NT1, NT1, T1 - 3 * NT1]
    one.features = F1
    one.mlp_units = B // 2
    one.columns = T1
    two = Part()
    two.name = 'a2'
    two.stage = 2
    two.nk = NTAP
    two.kp = P
    two.nt = T2
    two.units = B // NCH
    two.shared_kv = False
    two.real = [T2] * NCH
    two.features = F2
    two.mlp_units = B // NCH // 2
    two.columns = NCH * T2
    return one, two


def build(nc, a, out):
    with ExitStack() as ctx:
        def sb(name, shape):
            return ctx.enter_context(nc.sbuf_tensor(name, shape, F32))

        def sem(name):
            return ctx.enter_context(nc.semaphore(name))

        def sems(prefix, names):
            return {n: sem(prefix + n) for n in names.split()}

        psum = ctx.enter_context(nc.psum_tensor("psum", [P, 8, 512], F32))

        ident = sb("ident", [P, P])
        blockmean = sb("blockmean", [P, P])
        ones_sq = sb("ones_sq", [P, P])
        neg_half = sb("neg_half", [P, 2 * NCH])
        ln_m = sb("ln_m", [P, 1])
        scratch = sb("scratch", [P, 1])
        const_in = sem("const_in")
        const_set = sem("const_set")

        y_mem = sb("y_mem", [P, B // 2 * NCH * 2 * EMB])
        late = sb("late", [P, B // 2 * MAP1])
        y1_all = late[:, :].rearrange("p (n x) -> p n x", x=MAP1)
        y_out1 = y_mem[:, :].rearrange("p (n c i e) -> p n c i e", c=NCH, i=2, e=EMB)
        y_pair = y_mem[:, :].rearrange("p (n c e) -> p n c e", c=NCH, e=2 * EMB)
        n2 = B * EMB
        y_out2 = y_mem[:, 0:n2].rearrange("p (n c e) -> p n c e", c=NCH, e=EMB)
        y2_all = y_mem[:, n2:n2 + NG * GI // 2 * MAP2].rearrange("p (n x) -> p n x", x=MAP2)
        zeroed = sem("zeroed")

        def carver(mem, start=0):
            at = [start]

            def tile(rows, *dims):
                n = int(np.prod(dims))
                v = mem[0:rows, at[0]:at[0] + n]
                at[0] += n
                assert at[0] <= mem.shape[1], (at[0], mem.shape)
                if len(dims) == 1:
                    return v
                names = "abc"[:len(dims)]
                return v.rearrange(f"p ({' '.join(names)}) -> p {' '.join(names)}",
                                   **{m: d for m, d in zip(names, dims)})

            return tile

        early_tile = carver(y_mem)

        one, two = performer_sizes()
        for st in (one, two):
            n = st.name + "_"
            st.wraw = early_tile(st.kp, st.nk, C3)
            st.wcat_all = sb(n + "wcat", [P, st.nk, SQ + 1])
            st.wcat = st.wcat_all[0:st.kp, :, :]
            st.gcol = sb(n + "gcol", [st.kp, st.nk])
            st.bcol = sb(n + "bcol", [st.kp, st.nk])
            st.inv = sb(n + "inv", [st.kp, st.nk])
            st.ninv = sb(n + "ninv", [st.kp, st.nk])
            st.kqvb = sb(n + "kqvb", [P, C3])
            st.bias = sb(n + "bias", [P, MEAN])
            st.pjb = sb(n + "pjb", [P, EMB])
            st.paug = sb(n + "paug", [EMB + 1, EMB + 1])
            st.wT = sb(n + "wT", [EMB, M])
            st.w1 = sb(n + "w1", [P, P])
            st.w1c = sb(n + "w1c", [P, P])
            st.w2 = sb(n + "w2", [P, P])
            st.cols = sb(n + "cols", [P, 4])
            st.b1c = sb(n + "b1c", [P, 1])
            st.w_in = sem(n + "w_in")
        sq_weights = sb("sq_weights", [P, 2])
        channels = sb("channels", [2 * PIX, 2 * BLK * BLK])
        w = sems("w_", "scaled summed centered wide biased bias_set turned turned_copied folded "
                       "folded_copied mlp_scaled mlp_summed mlp_set")
        x_made = sems("x_", "act dve zero")
        k = sems("k_", "xsq chan taps main stat square_mean var var_eps rstd z kqsq xd arg e vb kvq kvq_copied "
                       "mp mp_copied yp den rec yn y")
        m = sems("m_", "sq sum1 sum2 square_mean var var_eps rstd yn tr tr_copied w1 gelu w2 out")
        m_in = [sem(f"m_in{i}") for i in range(2)]
        x_in = [sem(f"x_in{i}") for i in range(2)]
        one.w0, two.w0 = 0, 1
        one.t0, two.t0 = 0, one.nk + 1
        one.k0, two.k0 = 1, 1 + one.units
        one.m0, two.m0 = 1, 1 + one.mlp_units
        one.y0, two.y0 = 0, 16 * one.mlp_units // 2
        wide = early_tile(P, NTAP, P)
        turned = early_tile(EMB, NTAP + 1, 2 * P)

        xbuf = [sb(f"xbuf{i}", [P, NCH * NTAP * T2]) for i in range(2)]
        xsqbuf = sb("xsqbuf", [P, NCH * NTAP * T2])
        tapsum = [sb(f"tapsum{i}", [P, NCH * P]) for i in range(2)]
        z = [sb(f"z{i}", [P, NCH, MEAN]) for i in range(2)]
        e = [sb(f"e{i}", [P, 2, NCH, M]) for i in range(2)]
        vb = [sb(f"vb{i}", [P, NCH, EMB]) for i in range(2)]
        kqsq = sb("kqsq", [P, NCH, 2, EMB])
        xd = sb("xd", [P, NCH, 2])
        arg = sb("arg", [P, NCH, 2, M])
        stat = sb("stat", [P, NCH, 2])
        sqm = sb("sqm", [P, 2 * NCH])
        var = sb("var", [P, 2 * NCH])
        var_eps = sb("var_eps", [P, NCH])
        rstd = sb("rstd", [P, NCH])
        var_eps_m = [sb(f"var_eps_m{i}", [P, 2 * NCH]) for i in range(2)]
        rstd_m = [sb(f"rstd_m{i}", [P, 2 * NCH]) for i in range(2)]
        kv = sb("kv", [EMB + 1, NCH, M])
        qT = sb("qT", [P, NT1])
        mp = sb("mp", [P, NCH, EMB + 1])
        den = sb("den", [P, NCH])
        rec = sb("rec", [P, NCH])
        yn = sb("yn", [P, NCH, EMB])
        sum1 = sb("sum1", [P, 2 * NCH])
        sum2 = sb("sum2", [P, 2 * NCH])
        square_tile = carver(xsqbuf)
        ysq = [square_tile(P, 2 * NCH, EMB) for _ in range(2)]
        ynm = [square_tile(P, NCH, P) for _ in range(2)]
        z_flat = [z_[:, :, :].rearrange("p c e -> p (c e)") for z_ in z]
        ynT = [z_[:, 0:NCH * P] for z_ in z_flat]
        yres = [z_[:, NCH * P:2 * NCH * P].rearrange("p (c e) -> p c e", e=P) for z_ in z_flat]
        gel = tapsum

        X1 = [x[0:2 * PIX, 0:GRID * S1] for x in xbuf]
        X1sum = [x[2 * PIX:P, 0:GRID * S1] for x in xbuf]
        X1q = xsqbuf[0:2 * PIX, 0:GRID * S1]

        def patches(st, x, c, kk):
            if st.stage == 1:
                return x[:, NT1 * c + S1 * kk:NT1 * c + S1 * kk + NT1]
            at = (c * NTAP + kk) * T2
            return x[0:krows(st, kk), at:at + T2]

        def krows(st, kk):
            return P if st.stage == 1 else EMB * len(TAPS[kk])

        late_tile = carver(late)
        tail_tile = carver(y_mem, n2 + NG * GI // 2 * MAP2)
        pw = tail_tile(P, NTAP, D)
        pb = tail_tile(P, D)
        wqkv, wproj = [], []
        for i in range(2):
            old_input = carver(xbuf[i])
            wqkv.append(old_input(HALF + 1, 2, 3 * D))
            wproj.append(old_input(PAIR, TRI // 2, D))
        wrout = tail_tile(HALF + 1, 2, NEXP + P)
        blora = tail_tile(P, 3 * D)
        qscale = sb("qscale", [HALF, 4])
        kmask = sb("kmask", [HALF, 6])
        vmask = tail_tile(GT, D)
        thrice = tail_tile(GT, GI, GT)
        t_in = sem("t_in")
        clipped = sem("clipped")
        scale_set = sem("scale_set")
        blocks_set = sem("blocks_set")

        g_tile = late_tile(P, NTAP, 2 * GT)
        h_in = late_tile(GT, D)
        fronts, backs = [], []
        for i in range(2):
            fr = Part()
            fr.att = i
            fr.h = [late_tile(GT, D) for _ in range(2)]
            fr.bn = late_tile(GT, 6)
            fr.mv = late_tile(GT, 2)
            fr.veps = late_tile(GT, 1)
            fr.r = late_tile(GT, 1)
            fr.hn = late_tile(GT, D)
            fr.hnT = late_tile(HALF + 1, 2, GT)
            fr.qx = late_tile(HALF, 2, GI * GT)
            fr.kT = late_tile(HALF, 2, GT)
            fr.kx = late_tile(HALF, 2, GI * 6 * T3)
            fr.vt = late_tile(GT, D)
            fr.vx = [late_tile(GT, GI, D) for _ in range(2)]
            fr.s = [late_tile(GT, HEADS, T3) for _ in range(2)]
            fr.wide, fr.narrow = 2 * i, 2 * i + 1
            fr.sems = sems(f"f{i}_", "bn mv veps r hn tr hnT qk v vt v3 kT kx vx s scores")
            fronts.append(fr)
            bk = Part()
            bk.att = i
            bk.s1 = late_tile(GT, HEADS, T3)
            if i == 0:
                bk.s2 = late_tile(GT, HEADS, T3)
            bk.mx = late_tile(GT, HEADS)
            bk.sm = late_tile(GT, HEADS)
            bk.rs = late_tile(GT, HEADS)
            bk.pT = late_tile(GT, TRI * GT)
            bk.oT = late_tile(PAIR, TRI // 2 * GT)
            bk.bank = 5 + i
            bk.sems = sems(f"b{i}_", "mx sub exp sum rs p pt pT o oT pj h")
            backs.append(bk)
        third_bank, in_bank = 4, 7
        keep = late_tile(GT, HEADS, T3)
        top = [late_tile(GT, HEADS, 8) for _ in range(3)]
        res = [late_tile(GT, D) for _ in range(2)]
        lg = late_tile(GT, 2 * NEXP)
        lg2 = late_tile(GT, 2 * NEXP)
        l8 = late_tile(GT, 8)
        rep = late_tile(GT, 8)
        sel = late_tile(GT, NEXP)
        lm = late_tile(GT, NEXP)
        le = late_tile(GT, NEXP)
        ls = late_tile(GT, 1)
        lr = late_tile(GT, 1)
        lw = late_tile(GT, NEXP)
        lw2 = late_tile(GT, NEXP)
        aw = late_tile(GT, P)
        aT = late_tile(P, GT)
        res_ready = [sem(f"res_ready{i}") for i in range(2)]
        res_out = [sem(f"res_out{i}") for i in range(2)]
        t = sems("t_", "g hp h h0 top8 keep em rt lg l8 rep found sel lm le lr lw lw2 aw at aT")

        block = ctx.enter_context(nc.Block())

        def nth(j, par):
            return j * 2 + par

        def peeled(j):
            return isinstance(j, int) and j == 0

        def before(j, par, back):
            return j + (par - back) // 2, (par - back) % 2

        def periods(eng, units, depth, period):
            edge = depth // 2
            for j in range(edge):
                for par in range(2):
                    period(j, par, lambda back: 2 * j + par >= back)
            with eng.Fori(edge, units // 2 - 1) as j_:
                for par in range(2):
                    period(j_, par, lambda back: True)
            for n in range(units - 2, units + depth - 1):
                period(n // 2, n % 2, lambda back: n - back < units)

        def mlp_rows(st, j, par):
            return y_pair[0:st.nt, bass.ds(nth(j, par), 1), :, :].rearrange("p o c e -> p (o c) e")

        def load_x(sp, st, j, par):
            n = nth(j, par)
            if not peeled(j):
                sp.wait_ge(k["main"], NCH * (n + (st.k0 - 1)))
            src = a["x"][bass.ds(n, 1), :, :].rearrange("o p t -> (o p) t")
            sp.dma_start(X1[par][:, 0:GRID * S1], src).then_inc(x_in[par], 16)

        def load_y(sp, st, j, par):
            n = nth(j, par)
            if not peeled(j):
                sp.wait_ge(m["w2"], n + (st.m0 - 1))
            sp.dma_start(yres[par][0:st.nt, :, :], mlp_rows(st, j, par)).then_inc(m_in[par], 16)

        def load_ys(sp, st):
            sp.wait_ge(k["y"], st.k0 + st.units)
            for par in range(2):
                load_y(sp, st, 0, par)
            with sp.Fori(1, st.mlp_units // 2) as j:
                for par in range(2):
                    load_y(sp, st, j, par)

        def store_group(sp, j, par):
            sp.wait_ge(res_ready[par], j + 1)
            sp.dma_start(out[bass.ds(nth(j, par) * GT, GT), :], res[par]).then_inc(res_out[par], 16)

        @block.sync
        def _(sp):
            for name, s_ in (*k.items(), *m.items()):
                sp.sem_inc(s_, NCH if name in ("main", "z") else 1)
            for name in ("stat", "square_mean", "var", "var_eps", "rstd"):
                sp.sem_inc(k[name], 1)
            for s_ in res_out:
                sp.sem_inc(s_, 16)
            sp.dma_start(ident[:, :], a["ident"]).then_inc(const_in, 16)
            sp.dma_start(blockmean[:, :], a["blockmean"]).then_inc(const_in, 16)
            sp.dma_start(sq_weights[:, :], a["sq_weights"]).then_inc(const_in, 16)
            sp.dma_start(channels[:, :], a["channels"]).then_inc(const_in, 16)
            for st in (one, two):
                sp.dma_start(st.wraw, a[st.name + "_w"]).then_inc(st.w_in, 16)
                for dst, src in ((st.gcol, "g"), (st.bcol, "b"), (st.inv, "inv"), (st.ninv, "ninv"),
                                 (st.kqvb, "kqvb"), (st.pjb, "pjb"), (st.paug, "paug"), (st.wT, "wT"),
                                 (st.w1, "w1"), (st.w2, "w2"), (st.cols, "cols")):
                    sp.dma_start(dst[:, :], a[st.name + "_" + src]).then_inc(st.w_in, 16)
                if st.stage == 1:
                    sp.wait_ge(const_set, 1)
                    for par in range(2):
                        load_x(sp, one, 0, par)
            with sp.Fori(1, one.units // 2) as j:
                for par in range(2):
                    load_x(sp, one, j, par)

            load_ys(sp, one)

            sp.wait_ge(k["y"], two.k0 + two.units)
            sp.dma_start(pw, a["pw"]).then_inc(t_in, 16)
            sp.dma_start(pb, a["pb"]).then_inc(t_in, 16)
            for i in range(2):
                sp.dma_start(wqkv[i], a[f"wqkv{i}"]).then_inc(t_in, 16)
                sp.dma_start(wproj[i], a[f"wproj{i}"]).then_inc(t_in, 16)
            sp.dma_start(wrout, a["wrout"]).then_inc(t_in, 16)
            sp.dma_start(blora, a["blora"]).then_inc(t_in, 16)
            sp.dma_start(qscale[:, 0:1], a["temp"]).then_inc(t_in, 16)
            sp.dma_start(kmask[:, :], a["kmask"]).then_inc(t_in, 16)
            sp.dma_start(vmask, a["vmask"]).then_inc(t_in, 16)
            sp.dma_start(thrice, a["thrice"]).then_inc(t_in, 16)
            load_ys(sp, two)

            with sp.Fori(0, NG // 2) as j:
                for par in range(2):
                    store_group(sp, j, par)
            for par in range(2):
                sp.wait_ge(res_out[par], 16 * (NG // 2 + 1))

        def pool_rstd(pool, st, j, par, half):
            n = nth(j, par)
            two_chunks = slice(2 * half, 2 * half + 2)
            pool.wait_ge(k["var_eps"], n * 2 + (2 * st.k0 + half + 1))
            nc.gpsimd.tensor_tensor(rstd[0:st.nt, two_chunks], var_eps[0:st.nt, two_chunks],
                                    neg_half[0:st.nt, two_chunks], ALU.pow).then_inc(k["rstd"], 1)

        def pool_residual(pool, st, j, par):
            n = nth(j, par)
            pool.wait_ge(k["z"], NCH * (n + (st.k0 + 1)))
            if not peeled(j):
                pool.wait_ge(k["y"], n + (st.k0 - 1))
            pjb = st.pjb[0:st.nt, :].unsqueeze(1).broadcast_to([st.nt, NCH, EMB])
            nc.gpsimd.tensor_tensor(vb[par][0:st.nt, :, :], z[par][0:st.nt, :, V0:V0 + EMB], pjb,
                                    ALU.add).then_inc(k["vb"], 1)

        def pool_back(pool, st, j, par):
            n = nth(j, par)
            pool.wait_ge(k["yn"], n + (st.k0 + 1))
            pool.wait_ge(k["vb"], n + (st.k0 + 1))
            if st.stage == 1:
                dst = y_out1[0:st.nt, bass.ds(j, 1), :, par, :]
            else:
                dst = y_out2[0:st.nt, bass.ds(n, 1), :, :]
            nc.gpsimd.tensor_tensor(dst.rearrange("p o c e -> p (o c) e"), yn[0:st.nt, :, :],
                                    vb[par][0:st.nt, :, :], ALU.add).then_inc(k["y"], 1)

        def pool_performer(pool, st):
            def period(j, par, live=lambda back: True):
                if live(0):
                    pool_rstd(pool, st, j, par, 0)
                if live(1):
                    pool_residual(pool, st, *before(j, par, 1))
                if live(0):
                    pool_rstd(pool, st, j, par, 1)
                if live(2):
                    pool_back(pool, st, j - 1, par)

            periods(pool, st.units, 3, period)

        def pool_mlp(pool, st):
            with pool.Fori(0, st.mlp_units // 2) as j:
                for par in range(2):
                    pool.wait_ge(m["var_eps"], nth(j, par) + (st.m0 + 1))
                    nc.gpsimd.tensor_tensor(rstd_m[par][0:st.nt, :], var_eps_m[par][0:st.nt, :], neg_half[0:st.nt, :],
                                            ALU.pow).then_inc(m["rstd"], 1)

        def per_head(x):
            return x.unsqueeze(2).broadcast_to([GT, HEADS, T3])

        @block.gpsimd
        def _(pool):
            for tile, value in ((ones_sq, 1.0), (neg_half, -0.5), (ln_m, -0.5 * float(np.log(M))),
                                (xbuf[0], 0.0), (xbuf[1], 0.0), (mp, 0.0)):
                nc.gpsimd.memset(tile[:], value)
            for st in (one, two):
                nc.gpsimd.memset(st.wcat_all[:, :, :], 0.0)
                nc.gpsimd.memset(st.bias[:, ONE:ONE + 1], 1.0)
            nc.gpsimd.memset(xsqbuf[:, 0:1], 0.0).then_inc(const_set, 1)
            nc.gpsimd.memset(late[:, :], 0.0).then_inc(zeroed, 1)
            pool.wait_ge(const_set, 1)
            for st in (one, two):
                pool.wait_ge(st.w_in, 16 * 12)
                pool.wait_ge(const_in, 64)

            pool_performer(pool, one)
            pool_mlp(pool, one)
            pool.wait_ge(m["out"], two.m0)
            nc.gpsimd.memset(y2_all, 0.0).then_inc(zeroed, 1)
            pool.wait_ge(zeroed, 2)
            pool_performer(pool, two)
            for fr, bk in zip(fronts, backs):
                nc.gpsimd.memset(fr.qx, 0.0)
                nc.gpsimd.memset(fr.hnT, 1.0)
                nc.gpsimd.memset(bk.oT, 1.0)
            nc.gpsimd.memset(lg[:, NEXP:2 * NEXP], -HUGE)
            nc.gpsimd.memset(rep, -HUGE).then_inc(blocks_set, 1)
            pool.wait_ge(blocks_set, 1)
            pool_mlp(pool, two)
            pool.wait_ge(t_in, 16 * 12)

            def r(fr, g):
                c = nth(*g) + 1
                pool.wait_ge(fr.sems["veps"], c)
                nc.gpsimd.tensor_tensor(fr.r, fr.veps, neg_half[0:GT, 0:1], ALU.pow).then_inc(fr.sems["r"], 1)

            def kx(fr, g, half):
                pool.wait_ge(fr.sems["kT"], nth(*g) + 1)
                keys = fr.kT[:, half, :].rearrange("p (i t) -> p i t", i=GI).unsqueeze(2)
                kept = kmask[:, :].unsqueeze(1).unsqueeze(3)
                nc.gpsimd.tensor_tensor(
                    fr.kx[:, half, :].rearrange("p (i h t) -> p i h t", i=GI, h=6),
                    keys.broadcast_to([HALF, GI, 6, T3]), kept.broadcast_to([HALF, GI, 6, T3]), ALU.mult
                    ).then_inc(fr.sems["kx"], 1)

            def minus_max(bk, g):
                pool.wait_ge(bk.sems["mx"], nth(*g) + 1)
                nc.gpsimd.tensor_tensor(bk.s1, fronts[bk.att].s[g[1]], per_head(bk.mx), ALU.subtract
                                        ).then_inc(bk.sems["sub"], 1)

            def over_sum(bk, g):
                pool.wait_ge(bk.sems["rs"], nth(*g) + 1)
                nc.gpsimd.tensor_tensor(fronts[bk.att].s[g[1]], bk.s1, per_head(bk.rs), ALU.mult
                                        ).then_inc(bk.sems["p"], 1)

            def period(j, par, live):
                g = [before(j, par, back) for back in range(DEPTH)]
                if live(3):
                    r(fronts[1], g[3])
                if live(4):
                    minus_max(backs[1], g[4])
                if live(1):
                    kx(fronts[0], g[1], 0)
                    kx(fronts[0], g[1], 1)
                if live(4):
                    over_sum(backs[1], g[4])
                if live(2):
                    minus_max(backs[0], g[2])
                if live(3):
                    kx(fronts[1], g[3], 0)
                if live(0):
                    r(fronts[0], g[0])
                if live(3):
                    kx(fronts[1], g[3], 1)

            periods(pool, NG, DEPTH, period)

        def gather_ops(copy, dst, src, sides, i):
            for kk, taps in enumerate(TAPS):
                for upper, (kh, kw) in enumerate(taps):
                    end = 2 * sides - 1
                    last = copy(dst(EMB * upper, kk),
                                src[EMB * i:EMB * i + EMB, :, kh:kh + end:2, kw:kw + end:2])
            return last

        def gather_x(eng, copy, done, j, par, i):
            n = nth(j, par)
            if not peeled(j):
                eng.wait_ge(k["main"], NCH * (n + (two.k0 - 1)))
            src = y1_all[:, bass.ds(n * 2, 2), :].rearrange("p n (r c) -> p n r c", c=PAD1)
            x = xbuf[par][:, :].rearrange("p (n i k r c) -> p n i k r c", i=2, k=NTAP, c=S2, n=2)
            gather_ops(copy, lambda row, kk: x[row:row + EMB, :, i, kk, :, :], src, S2, i).then_inc(done, 1)

        def gather_g(copy, it, i):
            pairs = GI
            src = y2_all[:, bass.ds(it * pairs, pairs), :].rearrange("p n (r c) -> p n r c", c=PAD2)
            x = g_tile.rearrange("p k (n i r c) -> p k n i r c", i=2, c=S3, n=pairs)
            return gather_ops(copy, lambda row, kk: x[row:row + EMB, kk, :, i, :, :], src, S3, i)

        def act_squares(act, st, j, par):
            n = nth(j, par)
            act.wait_ge(k["z"], NCH * (n + (st.k0 + 1)))
            act.wait_ge(k["xd"], n + st.k0)
            nc.scalar.activation(kqsq[0:st.nt, :, :, :],
                                 z[par][0:st.nt, :, 0:V0].rearrange("p c (s e) -> p c s e", s=2),
                                 ACT.Square).then_inc(k["kqsq"], 1)

        def act_exp(act, st, j, par):
            n = nth(j, par)
            act.wait_ge(k["arg"], n + (st.k0 + 1))
            if not peeled(j):
                act.wait_ge(k["kvq"], n + (st.k0 - 1))
            nc.scalar.activation(e[par][0:st.nt, :, :, :].rearrange("p s c m -> p c s m"), arg[0:st.nt, :, :, :], ACT.Exp,
                                 bias=ln_m[0:st.nt, 0:1]).then_inc(k["e"], 1)

        def act_kvq(act, st, j, par):
            n = nth(j, par)
            act.wait_ge(k["kvq"], n + (st.k0 + 1))
            act.wait_ge(k["yp"], n + st.k0)
            sums = (psum[0:EMB + 1, 4, 0:M].unsqueeze(1).broadcast_to([EMB + 1, NCH, M]) if st.shared_kv else
                    psum[0:EMB + 1, 4, 0:NCH * M].rearrange("p (c m) -> p c m", m=M))
            nc.scalar.activation(kv[:, :, :], sums, ACT.Copy)
            nc.scalar.activation(qT[:, 0:st.nt], psum[:, 5, 0:st.nt], ACT.Copy).then_inc(k["kvq_copied"], 1)

        def act_mp(act, st, j, par):
            n = nth(j, par)
            act.wait_ge(k["mp"], n + (st.k0 + 1))
            for c in range(NCH):
                rows = slice(M * c, M * c + M)
                last = nc.scalar.activation(mp[rows, c, :], psum[rows, 4, P:P + EMB + 1], ACT.Copy)
            last.then_inc(k["mp_copied"], 1)

        def act_channels(act, st, j, par):
            if st.stage == 1:
                n = nth(j, par)
                act.wait_ge(k["chan"], n + (st.k0 + 1))
                if not peeled(j):
                    act.wait_ge(k["main"], NCH * (n + (st.k0 - 1)))
                nc.scalar.activation(X1sum[par], psum[0:2 * BLK * BLK, 7, 0:GRID * S1], ACT.Copy).then_inc(k["taps"], 1)

        def act_copy(dst, src):
            return nc.scalar.activation(dst, src, ACT.Copy)

        def act_gather(act, st, j, par):
            if st.stage == 2:
                gather_x(act, act_copy, x_made["act"], j, par, 0)

        def act_patches(act, st, j, par):
            if st.stage == 2:
                n = nth(j, par)
                act.wait_ge(x_made["act"], n + 1)
                act.wait_ge(x_made["dve"], n + 1)
                act.wait_ge(x_made["zero"], 1)
                act.wait_ge(k["taps"], n + st.k0)
                nc.scalar.activation(xsqbuf[:, :], xbuf[par][:, :], ACT.Square).then_inc(k["xsq"], 1)
            else:
                n = nth(j, par)
                act.wait_ge(x_in[par], j * 16 + 16)
                act.wait_ge(k["chan"], n + st.k0)
                nc.scalar.activation(X1q, X1[par], ACT.Square).then_inc(k["xsq"], 1)

        def act_performer(act, st):
            act_gather(act, st, 0, 0)
            act_patches(act, st, 0, 0)
            act_channels(act, st, 0, 0)

            def period(j, par, live):
                if live(-1):
                    act_gather(act, st, *before(j, par, -1))
                if live(2):
                    act_kvq(act, st, j - 1, par)
                if live(2) and st.stage == 1:
                    act_mp(act, st, j - 1, par)
                if live(1) and st.stage == 2:
                    act_squares(act, st, *before(j, par, 1))
                if live(-1):
                    act_patches(act, st, *before(j, par, -1))
                if live(1) and st.stage == 1:
                    act_squares(act, st, *before(j, par, 1))
                if live(2) and st.stage == 2:
                    act_mp(act, st, j - 1, par)
                if live(-1):
                    act_channels(act, st, *before(j, par, -1))
                if live(1):
                    act_exp(act, st, *before(j, par, 1))

            periods(act, st.units, 3, period)

        def act_square(act, st, j, par):
            n = nth(j, par)
            if not peeled(j):
                act.wait_ge(m["sum2"], n + (st.m0 - 1))
            nc.scalar.activation(ysq[par][0:st.nt, :, :], mlp_rows(st, j, par).rearrange(
                "p c (i e) -> p (c i) e", i=2), ACT.Square).then_inc(m["sq"], 1)

        def act_turned(act, st, j, par):
            n = nth(j, par)
            act.wait_ge(m["tr"], n + (st.m0 + 1))
            nc.scalar.activation(ynT[par][:, 0:st.columns], psum[:, par, 0:st.columns], ACT.Copy
                                 ).then_inc(m["tr_copied"], 1)

        def act_gelu(act, st, j, par):
            n = nth(j, par)
            if not peeled(j):
                act.wait_ge(m["w2"], n + (st.m0 - 1))
            act.wait_ge(m["w1"], n + (st.m0 + 1))
            nc.scalar.activation(gel[par][:, 0:st.columns], psum[:, 2 + par, 0:st.columns], ACT.Gelu,
                                 bias=st.b1c[:, 0:1]).then_inc(m["gelu"], 1)

        def act_mlp(act, st):
            act.wait_ge(w["mlp_set"], st.w0 + 1)
            act.wait_ge(k["y"], st.k0 + st.units)

            act_square(act, st, 0, 0)

            def period(j, par, live):
                if live(-1):
                    act_square(act, st, *before(j, par, -1))
                if live(2):
                    act_gelu(act, st, *before(j, par, 2))
                if live(1):
                    act_turned(act, st, *before(j, par, 1))

            periods(act, st.mlp_units, MLP_DEPTH, period)

        @block.scalar
        def _(act):
            act.wait_ge(const_set, 1)
            act_performer(act, one)
            act_mlp(act, one)
            act.wait_ge(m["out"], two.m0)
            act_performer(act, two)
            act_mlp(act, two)
            act.wait_ge(scale_set, 1)
            act.wait_ge(blocks_set, 1)
            act.wait_ge(m["out"], two.m0 + two.mlp_units)

            def gather(j, i):
                last = gather_g(act_copy, j, i)
                if i == 1:
                    last.then_inc(t["g"], 1)

            def keep_h(g):
                act.wait_ge(t["h"], nth(*g) + 1)
                if not peeled(g[0]):
                    act.wait_ge(backs[0].sems["h"], nth(*g) - 1)
                nc.scalar.activation(fronts[0].h[g[1]], h_in, ACT.Copy).then_inc(t["h0"], 1)

            def turned_h(fr, g):
                act.wait_ge(fr.sems["tr"], nth(*g) + 1)
                nc.scalar.activation(fr.hnT[0:HALF, :, :], psum[0:HALF, fr.narrow, 0:2 * GT].rearrange(
                    "p (u t) -> p u t", u=2), ACT.Copy).then_inc(fr.sems["hnT"], 1)

            def queries_keys(fr, g):
                act.wait_ge(fr.sems["qk"], nth(*g) + 1)
                blocks = bass.AP(fr.qx.tensor, fr.qx.offset, [list(fr.qx.ap[0]), [GI * GT, 2],
                                                              [GT + T3, GI], [1, T3]])
                nc.scalar.activation(blocks, psum[0:HALF, fr.narrow, 0:2 * GT].rearrange(
                    "p (u i t) -> p u i t", u=2, i=GI), ACT.Copy, scale=qscale[:, 2 + fr.att:3 + fr.att])
                nc.scalar.activation(fr.kT, psum[0:HALF, fr.narrow, 2 * GT:4 * GT].rearrange(
                    "p (u t) -> p u t", u=2), ACT.Copy).then_inc(fr.sems["kT"], 1)

            def values(fr, g):
                act.wait_ge(fr.sems["v"], nth(*g) + 1)
                nc.scalar.activation(fr.vt, psum[0:GT, fr.wide, 0:D], ACT.Copy).then_inc(fr.sems["vt"], 1)

            def spread_values(fr, g):
                images = fr.vx[g[1]].rearrange("p i (r c d) -> p i r c d", c=3, d=HD)
                third = D * fr.att
                firsts = psum[0:GT, fr.wide, 0:2 * D].rearrange("p (i r c d) -> p i r c d", i=2, c=3, d=HD)
                last_one = psum[0:GT, third_bank, third:third + D].rearrange("p (r c d) -> p r c d", c=3, d=HD)
                act.wait_ge(fr.sems["v3"], nth(*g) + 1)
                for c in range(3):
                    mask = vmask[:, HD * c:HD * c + 1]
                    nc.scalar.activation(images[:, 0:2, :, c, :], firsts[:, :, :, c, :], ACT.Copy, scale=mask)
                    last = nc.scalar.activation(images[:, 2, :, c, :], last_one[:, :, c, :], ACT.Copy, scale=mask)
                last.then_inc(fr.sems["vx"], 1)

            def scores(fr, g):
                act.wait_ge(fr.sems["s"], nth(*g) + 1)
                nc.scalar.activation(fr.s[g[1]], psum[0:GT, fr.narrow, 0:HEADS * T3].rearrange(
                    "p (h t) -> p h t", h=HEADS), ACT.Copy).then_inc(fr.sems["scores"], 1)

            def router_exp(g):
                act.wait_ge(t["lm"], nth(*g) + 1)
                nc.scalar.activation(le, lm, ACT.Exp).then_inc(t["le"], 1)

            def turned_factors(g):
                act.wait_ge(t["at"], nth(*g) + 1)
                nc.scalar.activation(aT, psum[:, fronts[1].narrow, 0:GT], ACT.Copy).then_inc(t["aT"], 1)

            def exponentials(bk, g):
                act.wait_ge(bk.sems["sub"], nth(*g) + 1)
                nc.scalar.activation(bk.s1, bk.s1, ACT.Exp).then_inc(bk.sems["exp"], 1)

            def turned_p(bk, g):
                act.wait_ge(bk.sems["pt"], nth(*g) + 1)
                nc.scalar.activation(bk.pT, psum[0:GT, bk.bank, 0:TRI * GT], ACT.Copy).then_inc(bk.sems["pT"], 1)

            def outputs(bk, g):
                act.wait_ge(bk.sems["o"], nth(*g) + 1)
                for row in (0, 64):
                    last = nc.scalar.activation(bk.oT[row:row + 3 * HD, :],
                                                psum[row:row + 3 * HD, bk.bank, 0:TRI // 2 * GT], ACT.Copy)
                last.then_inc(bk.sems["oT"], 1)

            def period(j, par, live):
                g = [before(j, par, back) for back in range(DEPTH)]
                if live(1):
                    keep_h(g[1])
                    queries_keys(fronts[0], g[1])
                    values(fronts[0], g[1])
                if live(3):
                    turned_h(fronts[1], g[3])
                if live(4):
                    exponentials(backs[1], g[4])
                if live(1):
                    spread_values(fronts[0], g[1])
                if live(3):
                    router_exp(g[3])
                if live(1):
                    scores(fronts[0], g[1])
                if live(4):
                    turned_p(backs[1], g[4])
                if live(3):
                    turned_factors(g[3])
                if live(2):
                    exponentials(backs[0], g[2])
                if live(4):
                    outputs(backs[1], g[4])
                if par == 1 and live(-1):
                    act.wait_ge(t["hp"], nth(*g[0]) + 1)
                    gather(j + 1, 0)
                if live(3):
                    queries_keys(fronts[1], g[3])
                if live(3):
                    values(fronts[1], g[3])
                if live(2):
                    turned_p(backs[0], g[2])
                if live(2):
                    outputs(backs[0], g[2])
                if live(0):
                    turned_h(fronts[0], g[0])
                if par == 1 and live(-1):
                    gather(j + 1, 1)
                if live(3):
                    scores(fronts[1], g[3])

            for i in range(2):
                gather(0, i)
            periods(act, NG, DEPTH, period)

        def plain(dve):
            nc.vector.memset(scratch[0:1, 0:1], 0.0)

        def turned_bank(c, columns):
            return psum[0:EMB, 2 + c // 2, 2 * P * (c % 2):2 * P * (c % 2) + columns]

        def dve_prepare(dve, st):
            c0 = st.w0 + 1
            dve.wait_ge(st.w_in, 16 * 12)
            if st.stage == 1:
                dve.wait_ge(const_in, 64)
                nc.vector.tensor_copy(st.wcat_all[:, :, SQ], sq_weights[:, :])
            for c in range(st.nk):
                last = nc.vector.tensor_scalar(st.wcat[:, c, 0:C3], st.wraw[:, c, :], st.gcol[:, c:c + 1], None, ALU.mult)
                last = nc.vector.tensor_scalar(wide[0:st.kp, c, :], ones_sq[0:st.kp, :], st.bcol[:, c:c + 1], None, ALU.mult)
                last = nc.vector.tensor_copy(st.wcat[:, c, MEAN:MEAN + 1], st.inv[:, c:c + 1])
            last.then_inc(w["scaled"], 1)
            dve.wait_ge(w["summed"], c0)
            dve.wait_ge(w["scaled"], c0)
            for c in range(st.nk):
                last = nc.vector.scalar_tensor_tensor(out=st.wcat[:, c, 0:C3], in0=psum[0:st.kp, 0, 0:C3],
                                                      scalar=st.ninv[:, c:c + 1], in1=st.wcat[:, c, 0:C3],
                                                      op0=ALU.mult, op1=ALU.add)
            last.then_inc(w["centered"], 1)
            dve.wait_ge(w["biased"], c0)
            nc.vector.tensor_tensor(st.bias[:, 0:C3], psum[:, 1, 0:C3], st.kqvb[:, :], ALU.add).then_inc(w["bias_set"], 1)
            for c in range(st.nk + 1):
                rows = st.kp if c < st.nk else P
                dve.wait_ge(w["turned"], st.t0 + st.nk + 1)
                nc.vector.tensor_copy(turned[:, c, 0:2 * rows], turned_bank(c, 2 * rows)).then_inc(w["turned_copied"], 1)
            for c in range(st.nk + 1):
                rows = st.kp if c < st.nk else P
                dve.wait_ge(w["folded"], st.t0 + st.nk + 1)
                dst = st.wcat[:, c, WK:WK + 2 * M] if c < st.nk else st.bias[:, WK:WK + 2 * M]
                nc.vector.tensor_copy(dst, psum[0:rows, 5, 2 * M * c:2 * M * (c + 1)]).then_inc(w["folded_copied"], 1)
            nc.vector.tensor_scalar(st.w1c[:, :], st.w1[:, :], st.cols[:, 0:1], None, ALU.mult).then_inc(w["mlp_scaled"], 1)
            dve.wait_ge(w["mlp_summed"], c0)
            dve.wait_ge(w["mlp_scaled"], c0)
            nc.vector.tensor_tensor(st.w1c[:, :], st.w1c[:, :], psum[:, 0, 0:P], ALU.subtract)
            nc.vector.tensor_tensor(st.b1c[:, :], psum[:, 1, 0:1], st.cols[:, 2:3], ALU.add).then_inc(w["mlp_set"], 1)

        def dve_var(dve, st, j, par, half):
            n = nth(j, par)
            c = n * 2 + (2 * st.k0 + half + 1)
            nt = st.nt
            two_chunks = slice(2 * half, 2 * half + 2)
            dve.wait_ge(k["main"], NCH * n + (NCH * st.k0 + 2 * half + 2))
            nc.vector.tensor_copy(stat[0:nt, two_chunks, :], psum[0:nt, two_chunks, MEAN:SQ + 1]).then_inc(k["stat"], 1)
            dve.wait_ge(k["stat"], c)
            nc.vector.tensor_tensor(sqm[0:nt, two_chunks], stat[0:nt, two_chunks, 0], stat[0:nt, two_chunks, 0], ALU.mult
                                    ).then_inc(k["square_mean"], 1)
            dve.wait_ge(k["square_mean"], c)
            nc.vector.tensor_tensor(var[0:nt, two_chunks], stat[0:nt, two_chunks, 1], sqm[0:nt, two_chunks], ALU.subtract
                                    ).then_inc(k["var"], 1)
            dve.wait_ge(k["var"], c)
            nc.vector.tensor_scalar(var_eps[0:nt, two_chunks], var[0:nt, two_chunks], 0.0, EPS, ALU.max, ALU.add
                                    ).then_inc(k["var_eps"], 1)

        def dve_z(dve, st, j, par, half):
            n = nth(j, par)
            nt = st.nt
            if not peeled(j):
                dve.wait_ge(k["kvq"], n + (st.k0 - 1))
                dve.wait_ge(k["vb"], n + (st.k0 - 1))
            dve.wait_ge(k["rstd"], n * 2 + (2 * st.k0 + half + 1))
            for i in (2 * half, 2 * half + 1):
                nc.vector.scalar_tensor_tensor(out=z[par][0:nt, i, :], in0=psum[0:nt, i, 0:MEAN],
                                               scalar=rstd[0:nt, i:i + 1], in1=st.bias[0:nt, :],
                                               op0=ALU.mult, op1=ALU.add).then_inc(k["z"], 1)

        def dve_taps(dve, st, j, par):
            if st.stage == 1:
                return
            n = nth(j, par)
            dve.wait_ge(k["xsq"], n + (st.k0 + 1))
            if not peeled(j):
                dve.wait_ge(k["main"], NCH * (n + (st.k0 - 1)))
            nc.vector.tensor_reduce(
                tapsum[par][:, 0:NCH * T2].rearrange("p (c t) -> p c t", c=NCH),
                xsqbuf[:, :].rearrange("p (c k t) -> p c t k", c=NCH, k=NTAP), AX_X, ALU.add).then_inc(k["taps"], 1)

        def dve_xd(dve, st, j, par):
            n = nth(j, par)
            c = n + (st.k0 + 1)
            nt = st.nt
            dve.wait_ge(k["kqsq"], c)
            nc.vector.tensor_reduce(xd[0:nt, :, :], kqsq[0:nt, :, :, :], AX_X, ALU.add).then_inc(k["xd"], 1)

        def dve_arg(dve, st, j, par):
            n = nth(j, par)
            c = n + (st.k0 + 1)
            nt = st.nt
            dve.wait_ge(k["xd"], c)
            dve.wait_ge(k["e"], n + st.k0)
            nc.vector.scalar_tensor_tensor(out=arg[0:nt, :, :, :],
                                           in0=xd[0:nt, :, :].unsqueeze(3).broadcast_to([nt, NCH, 2, M]),
                                           scalar=-0.5, in1=z[par][0:nt, :, WK:WK + 2 * M].rearrange(
                                               "p c (s m) -> p c s m", s=2),
                                           op0=ALU.mult, op1=ALU.add).then_inc(k["arg"], 1)

        def dve_back(dve, st, j, par):
            n = nth(j, par)
            c = n + (st.k0 + 1)
            nt = st.nt
            yp = psum[0:nt, 6, 0:NCH * (EMB + 1)].rearrange("p (c e) -> p c e", c=NCH)
            dve.wait_ge(k["yp"], c)
            nc.vector.tensor_scalar(den[0:nt, :], yp[:, :, EMB], 1e-8, None, ALU.add).then_inc(k["den"], 1)
            dve.wait_ge(k["den"], c)
            nc.vector.reciprocal(rec[0:nt, :], den[0:nt, :]).then_inc(k["rec"], 1)
            dve.wait_ge(k["rec"], c)
            dve.wait_ge(k["y"], n + st.k0)
            nc.vector.tensor_tensor(yn[0:nt, :, :], yp[:, :, 0:EMB],
                                    rec[0:nt, :].unsqueeze(2).broadcast_to([nt, NCH, EMB]), ALU.mult
                                    ).then_inc(k["yn"], 1)

        def dve_gather(dve, st, j, par):
            if st.stage == 2:
                gather_x(dve, nc.vector.tensor_copy, x_made["dve"], j, par, 1)

        def dve_performer(dve, st):
            dve_gather(dve, st, 0, 0)
            dve_taps(dve, st, 0, 0)

            def period(j, par, live):
                if live(-1):
                    dve_gather(dve, st, *before(j, par, -1))
                if live(0):
                    dve_var(dve, st, j, par, 0)
                if live(1) and st.stage == 2:
                    dve_xd(dve, st, *before(j, par, 1))
                if live(0):
                    dve_z(dve, st, j, par, 0)
                if live(1) and st.stage == 1:
                    dve_xd(dve, st, *before(j, par, 1))
                if live(-1):
                    dve_taps(dve, st, *before(j, par, -1))
                if live(1):
                    dve_arg(dve, st, *before(j, par, 1))
                if live(0):
                    dve_var(dve, st, j, par, 1)
                if live(2):
                    dve_back(dve, st, j - 1, par)
                if live(0):
                    dve_z(dve, st, j, par, 1)

            periods(dve, st.units, 3, period)

        def dve_sums(dve, st, j, par):
            n = nth(j, par)
            c = n + (st.m0 + 1)
            nt = st.nt
            rows = mlp_rows(st, j, par).rearrange("p c (i e) -> p (c i) e", i=2)
            nc.vector.tensor_reduce(sum1[0:nt, :], rows, AX_X, ALU.add).then_inc(m["sum1"], 1)
            dve.wait_ge(m["sq"], c)
            nc.vector.tensor_reduce(sum2[0:nt, :], ysq[par][0:nt, :, :], AX_X, ALU.add).then_inc(m["sum2"], 1)
            dve.wait_ge(m["sum1"], c)
            nc.vector.scalar_tensor_tensor(out=sqm[0:nt, :], in0=sum1[0:nt, :], scalar=1.0 / (EMB * EMB),
                                           in1=sum1[0:nt, :], op0=ALU.mult, op1=ALU.mult).then_inc(m["square_mean"], 1)
            dve.wait_ge(m["sum2"], c)
            dve.wait_ge(m["square_mean"], c)
            nc.vector.scalar_tensor_tensor(out=var[0:nt, :], in0=sum2[0:nt, :], scalar=1.0 / EMB,
                                           in1=sqm[0:nt, :], op0=ALU.mult, op1=ALU.subtract).then_inc(m["var"], 1)
            dve.wait_ge(m["var"], c)
            nc.vector.tensor_scalar(var_eps_m[par][0:nt, :], var[0:nt, 0:2 * NCH], 0.0, EPS, ALU.max, ALU.add
                                    ).then_inc(m["var_eps"], 1)

        def dve_scaled(dve, st, j, par):
            n = nth(j, par)
            nt = st.nt
            dve.wait_ge(m["rstd"], n + (st.m0 + 1))
            if not peeled(j):
                dve.wait_ge(m["tr"], n + (st.m0 - 1))
            nc.vector.tensor_tensor(ynm[par][0:nt, :, :].rearrange("p c (i e) -> p (c i) e", i=2),
                                    mlp_rows(st, j, par).rearrange("p c (i e) -> p (c i) e", i=2),
                                    rstd_m[par][0:nt, :].unsqueeze(2).broadcast_to([nt, 2 * NCH, EMB]), ALU.mult
                                    ).then_inc(m["yn"], 1)

        def dve_out(dve, st, j, par):
            n = nth(j, par)
            dve.wait_ge(m["w2"], n + (st.m0 + 1))
            src = psum[:, 4 + par, 0:st.columns]
            if st.stage == 1:
                dst = y1_all[:, bass.ds(n, 1), :].rearrange("p o (r c) -> p (o r) c", c=PAD1)[:, 1:1 + S1, 1:1 + S1]
                src = src.rearrange("p (r c) -> p r c", c=S1)
            else:
                dst = y2_all[:, bass.ds(n * NCH, NCH), :].rearrange("p n (r c) -> p n r c", c=PAD2
                                                                    )[:, :, 1:1 + S2, 1:1 + S2]
                src = src.rearrange("p (n r c) -> p n r c", n=NCH, c=S2)
            nc.vector.tensor_scalar(dst, src, st.cols[:, 3:4], None, ALU.add).then_inc(m["out"], 1)

        def dve_mlp(dve, st):
            dve.wait_ge(k["y"], st.k0 + st.units)

            def period(j, par, live):
                if live(0):
                    dve_sums(dve, st, j, par)
                if live(1):
                    dve_scaled(dve, st, *before(j, par, 1))
                if live(4):
                    dve_out(dve, st, *before(j, par, 4))

            periods(dve, st.mlp_units, MLP_DEPTH, period)

        @block.vector
        def _(dve):
            dve.wait_ge(const_set, 1)
            dve_prepare(dve, one)
            dve_prepare(dve, two)
            dve_performer(dve, one)
            dve.wait_ge(zeroed, 1)
            dve_mlp(dve, one)
            dve.wait_ge(m["out"], two.m0)
            for x in xbuf:
                last = nc.vector.memset(x[EMB:P, :].rearrange("p (c k t) -> p c k t", c=NCH, k=NTAP)[:, :, NTAP - 1, :], 0.0)
            last.then_inc(x_made["zero"], 1)
            dve_performer(dve, two)
            dve.wait_ge(zeroed, 2)
            dve_mlp(dve, two)
            dve.wait_ge(t_in, 16 * 12)
            nc.vector.tensor_scalar(qscale[:, 1:2], qscale[:, 0:1], 0.01, None, ALU.max).then_inc(clipped, 1)
            dve.wait_ge(clipped, 1)
            nc.vector.reciprocal(qscale[:, 2:3], qscale[:, 1:2]).then_inc(clipped, 1)
            nc.vector.memset(qscale[:, 3:4], HD ** -0.5)
            dve.wait_ge(clipped, 2)
            nc.vector.tensor_scalar(qscale[:, 2:3], qscale[:, 2:3], HD ** -0.5, None, ALU.mult).then_inc(scale_set, 1)

            def new_h(g):
                c = nth(*g) + 1
                dve.wait_ge(t["hp"], c)
                if not (isinstance(g[0], int) and g[0] == 0 and g[1] == 0):
                    dve.wait_ge(t["h0"], c - 1)
                nc.vector.tensor_tensor(h_in, psum[0:GT, in_bank, 0:D], pb[0:GT, :], ALU.add).then_inc(t["h"], 1)

            def norm(fr, g):
                c = nth(*g) + 1
                dve.wait_ge(t["h"] if fr.att == 0 else backs[0].sems["h"], c)
                nc.vector.bn_stats(fr.bn, h_of(fr, g)).then_inc(fr.sems["bn"], 1)
                dve.wait_ge(fr.sems["bn"], c)
                plain(dve)
                nc.vector.bn_aggr(fr.mv, fr.bn).then_inc(fr.sems["mv"], 1)
                dve.wait_ge(fr.sems["mv"], c)
                nc.vector.tensor_scalar(fr.veps, fr.mv[:, 1:2], 0.0, EPS, ALU.max, ALU.add
                                        ).then_inc(fr.sems["veps"], 1)

            def h_of(fr, g):
                return h_in if fr.att == 0 else fr.h[g[1]]

            def normed(fr, g):
                dve.wait_ge(fr.sems["r"], nth(*g) + 1)
                nc.vector.tensor_scalar(fr.hn, h_of(fr, g), fr.mv[:, 0:1], fr.r, ALU.subtract, ALU.mult
                                        ).then_inc(fr.sems["hn"], 1)

            router = psum[0:GT, fronts[1].wide, D:D + NEXP + P]

            def choose(g):
                c = nth(*g) + 1
                dve.wait_ge(t["rt"], c)
                nc.vector.tensor_copy(lg[:, 0:NEXP], router[:, 0:NEXP]).then_inc(t["lg"], 1)
                dve.wait_ge(t["lg"], c)
                plain(dve)
                nc.vector.max(out=l8, in_=lg[:, 0:NEXP]).then_inc(t["l8"], 1)
                dve.wait_ge(t["l8"], c)
                nc.vector.tensor_scalar(lm, lg[:, 0:NEXP], l8[:, 0:1], None, ALU.subtract).then_inc(t["lm"], 1)
                nc.vector.tensor_copy(rep[:, 0:TOP_K], l8[:, 0:TOP_K]).then_inc(t["rep"], 1)
                dve.wait_ge(t["rep"], c)
                plain(dve)
                nc.vector.match_replace(out=lg2, in_to_replace=rep, in_values=lg, imm_value=HUGE
                                        ).then_inc(t["found"], 1)
                dve.wait_ge(t["found"], c)
                nc.vector.tensor_scalar(sel, lg2[:, 0:NEXP], HUGE, ALPHA / RANK, ALU.is_ge, ALU.mult
                                        ).then_inc(t["sel"], 1)

            def weigh(g):
                c = nth(*g) + 1
                dve.wait_ge(t["le"], c)
                nc.vector.tensor_reduce(ls, le, AX_X, ALU.add).then_inc(t["lr"], 1)
                dve.wait_ge(t["sel"], c)
                nc.vector.tensor_tensor(lw, le, sel, ALU.mult).then_inc(t["lw"], 1)
                dve.wait_ge(t["lr"], nth(*g) * 2 + 1)
                nc.vector.reciprocal(lr, ls).then_inc(t["lr"], 1)
                dve.wait_ge(t["lr"], nth(*g) * 2 + 2)
                dve.wait_ge(t["lw"], c)
                nc.vector.tensor_scalar(lw2, lw, lr, None, ALU.mult).then_inc(t["lw2"], 1)
                dve.wait_ge(t["lw2"], c)
                nc.vector.tensor_tensor(
                    aw.rearrange("p (n r) -> p n r", r=RANK), router[:, NEXP:NEXP + P].rearrange("p (n r) -> p n r", r=RANK),
                    lw2.unsqueeze(2).broadcast_to([GT, NEXP, RANK]), ALU.mult).then_inc(t["aw"], 1)

            def spread_values(fr, g):
                vx = fr.vx[g[1]]
                third = D * fr.att
                dve.wait_ge(fr.sems["v3"], nth(*g) + 1)
                nc.vector.tensor_tensor(vx[:, 0:2, :], psum[0:GT, fr.wide, 0:2 * D].rearrange(
                    "p (i f) -> p i f", i=2), vmask[:, :].unsqueeze(1).broadcast_to([GT, 2, D]), ALU.mult)
                nc.vector.tensor_tensor(vx[:, 2, :], psum[0:GT, third_bank, third:third + D], vmask[:, :], ALU.mult
                                        ).then_inc(fr.sems["vx"], 1)

            def largest(g):
                dve.wait_ge(fronts[1].sems["scores"], nth(*g) + 1)
                nc.vector.tensor_reduce(backs[1].mx, fronts[1].s[g[1]], AX_X, ALU.max).then_inc(backs[1].sems["mx"], 1)

            found_in = [fronts[0].s, backs[0].s2, keep]

            def tops(g, i):
                src = found_in[i] if i else fronts[0].s[g[1]]
                if i == 0:
                    dve.wait_ge(fronts[0].sems["scores"], nth(*g) + 1)
                else:
                    dve.wait_ge(t["top8"], nth(*g) * 5 + 2 * i)
                plain(dve)
                for hd in range(HEADS):
                    last = nc.vector.max(out=top[i][:, hd, :], in_=src[:, hd, :])
                last.then_inc(t["top8"], 1)
                if i == 0:
                    dve.wait_ge(t["top8"], nth(*g) * 5 + 1)
                    nc.vector.tensor_copy(backs[0].mx, top[0][:, :, 0]).then_inc(backs[0].sems["mx"], 1)

            def without(g, i):
                src = found_in[i] if i else fronts[0].s[g[1]]
                dve.wait_ge(t["top8"], nth(*g) * 5 + (2 * i + 1))
                plain(dve)
                for hd in range(HEADS):
                    last = nc.vector.match_replace(out=found_in[i + 1][:, hd, :], in_to_replace=top[i][:, hd, :],
                                                   in_values=src[:, hd, :], imm_value=-HUGE)
                last.then_inc(t["top8"], 1)

            def kept(g):
                dve.wait_ge(t["top8"], nth(*g) * 5 + 5)
                nc.vector.tensor_tensor(keep, fronts[0].s[g[1]], per_head(top[2][:, :, KEEP - 17]), ALU.is_ge
                                        ).then_inc(t["keep"], 1)

            def kept_only(g):
                c = nth(*g) + 1
                dve.wait_ge(backs[0].sems["exp"], c)
                dve.wait_ge(t["keep"], c)
                nc.vector.tensor_tensor(backs[0].s2, backs[0].s1, keep, ALU.mult).then_inc(t["em"], 1)

            def over_sum(g):
                dve.wait_ge(backs[0].sems["rs"], nth(*g) + 1)
                nc.vector.tensor_tensor(fronts[0].s[g[1]], backs[0].s2, per_head(backs[0].rs), ALU.mult
                                        ).then_inc(backs[0].sems["p"], 1)

            def row_sums(bk, g):
                c = nth(*g) + 1
                dve.wait_ge(t["em"] if bk.att == 0 else bk.sems["exp"], c)
                nc.vector.tensor_reduce(bk.sm, bk.s2 if bk.att == 0 else bk.s1, AX_X, ALU.add).then_inc(bk.sems["sum"], 1)
                dve.wait_ge(bk.sems["sum"], c)
                nc.vector.reciprocal(bk.rs, bk.sm).then_inc(bk.sems["rs"], 1)

            def residual(g):
                c = nth(*g) + 1
                dve.wait_ge(backs[0].sems["pj"], c)
                dve.wait_ge(t["h0"], c)
                if not peeled(g[0]):
                    dve.wait_ge(res_ready[g[1]], g[0])
                nc.vector.tensor_tensor(fronts[1].h[g[1]], fronts[0].h[g[1]], psum[0:GT, backs[0].bank, 0:D], ALU.add
                                        ).then_inc(backs[0].sems["h"], 1)

            def result(g):
                dve.wait_ge(backs[1].sems["pj"], nth(*g) + 1)
                dve.wait_ge(res_out[g[1]], g[0] * 16 + 16)
                nc.vector.tensor_tensor(res[g[1]], fronts[1].h[g[1]], psum[0:GT, backs[1].bank, 0:D], ALU.add
                                        ).then_inc(res_ready[g[1]], 1)

            def period(j, par, live):
                g = [before(j, par, back) for back in range(DEPTH)]
                if live(3):
                    norm(fronts[1], g[3])
                if live(2):
                    tops(g[2], 0)
                if live(4):
                    largest(g[4])
                if live(3):
                    normed(fronts[1], g[3])
                if live(2):
                    without(g[2], 0)
                if live(4):
                    row_sums(backs[1], g[4])
                if live(2):
                    tops(g[2], 1)
                if live(3):
                    choose(g[3])
                if live(3):
                    weigh(g[3])
                if live(2):
                    without(g[2], 1)
                    tops(g[2], 2)
                    kept(g[2])
                    kept_only(g[2])
                    row_sums(backs[0], g[2])
                    over_sum(g[2])
                if live(0):
                    new_h(g[0])
                    norm(fronts[0], g[0])
                if live(4):
                    result(g[4])
                if live(0):
                    normed(fronts[0], g[0])
                if live(3):
                    spread_values(fronts[1], g[3])
                if live(2):
                    residual(g[2])

            periods(dve, NG, DEPTH, period)

        def pe_prepare(pe, st):
            c0 = st.w0 + 1
            pe.wait_ge(w["scaled"], c0)
            if st.w0:
                pe.wait_ge(w["mlp_set"], st.w0)
            for c in range(st.nk):
                last = nc.tensor.matmul(psum[:, 0, 0:C3], ones_sq[0:st.kp, :], st.wcat[:, c, 0:C3],
                                        start=(c == 0), stop=(c == st.nk - 1))
            last.then_inc(w["summed"], 1)
            for c in range(st.nk):
                last = nc.tensor.matmul(psum[:, 1, 0:C3], wide[0:st.kp, c, :], st.wraw[:, c, :],
                                        start=(c == 0), stop=(c == st.nk - 1))
            last.then_inc(w["biased"], 1)
            pe.wait_ge(w["centered"], c0)
            pe.wait_ge(w["bias_set"], c0)
            for c in range(st.nk + 1):
                rows = st.kp if c < st.nk else P
                src = st.wcat[:, c, :] if c < st.nk else st.bias[:, :]
                for s in range(2):
                    last = nc.tensor.transpose(turned_bank(c, 2 * rows)[:, s * rows:(s + 1) * rows],
                                               src[:, EMB * s:EMB * s + EMB], ident[0:rows, 0:rows])
                last.then_inc(w["turned"], 1)
            for c in range(st.nk + 1):
                rows = st.kp if c < st.nk else P
                pe.wait_ge(w["turned_copied"], st.t0 + c + 1)
                for s in range(2):
                    at = 2 * M * c + M * s
                    last = nc.tensor.matmul(psum[0:rows, 5, at:at + M], turned[:, c, s * rows:(s + 1) * rows],
                                            st.wT[:, :], start=True, stop=True)
                last.then_inc(w["folded"], 1)
            pe.wait_ge(w["mlp_scaled"], c0)
            nc.tensor.matmul(psum[:, 0, 0:P], blockmean[:, :], st.w1c[:, :], start=True, stop=True)
            nc.tensor.matmul(psum[:, 1, 0:1], st.w1[:, :], st.cols[:, 1:2], start=True, stop=True
                             ).then_inc(w["mlp_summed"], 1)

        def pe_main(pe, st, j, par, c):
            n = nth(j, par)
            if c == 0:
                pe.wait_ge(k["taps"], n + (st.k0 + 1))
            pe.wait_ge(k["z"], NCH * (n + (st.k0 - 1)) + (c + 1))
            for kk in range(st.nk):
                rows = krows(st, kk)
                columns = SQ + 1 if st.stage == 1 else MEAN + 1
                last = nc.tensor.matmul(psum[0:st.nt, c, 0:columns], patches(st, xbuf[par], c, kk),
                                        st.wcat_all[0:rows, kk, 0:columns], start=(kk == 0), stop=(kk == st.nk - 1))
            if st.stage == 1:
                last.then_inc(k["main"], 1)
                return
            nc.tensor.matmul(psum[0:st.nt, c, SQ:SQ + 1], tapsum[par][0:st.kp, st.nt * c:st.nt * c + st.nt],
                             st.inv[:, 0:1], start=True, stop=True).then_inc(k["main"], 1)

        def pe_channels(pe, st, j, par):
            if st.stage == 2:
                return
            n = nth(j, par)
            pe.wait_ge(k["xsq"], n + (st.k0 + 1))
            nc.tensor.matmul(psum[0:2 * BLK * BLK, 7, 0:GRID * S1], channels[:, :], X1q,
                             start=True, stop=True).then_inc(k["chan"], 1)

        def pe_kvq(pe, st, j, par):
            n = nth(j, par)
            pe.wait_ge(k["e"], n + (st.k0 + 1))
            pe.wait_ge(k["mp_copied"], n + st.k0)
            for c in range(NCH):
                rows = st.real[c]
                kc = 0 if st.shared_kv else c
                nc.tensor.matmul(psum[0:EMB + 1, 4, M * kc:M * kc + M], z[par][0:rows, c, V0:ONE + 1],
                                 e[par][0:rows, 0, c, :], start=(c == 0 or not st.shared_kv),
                                 stop=(c == NCH - 1 or not st.shared_kv))
            nc.tensor.transpose(psum[:, 5, 0:st.nt], e[par][0:st.nt, 1, :, :].rearrange("p c m -> p (c m)"),
                                ident[0:st.nt, 0:st.nt]).then_inc(k["kvq"], 1)

        def pe_mp(pe, st, j, par):
            n = nth(j, par)
            pe.wait_ge(k["kvq_copied"], n + (st.k0 + 1))
            nc.tensor.matmul(psum[:, 4, P:P + EMB + 1], kv[:, :, :].rearrange("p c m -> p (c m)"), st.paug[:, :],
                             start=True, stop=True).then_inc(k["mp"], 1)

        def pe_y(pe, st, j, par):
            n = nth(j, par)
            pe.wait_ge(k["mp_copied"], n + (st.k0 + 1))
            pe.wait_ge(k["yn"], n + st.k0)
            nc.tensor.matmul(psum[0:st.nt, 6, 0:NCH * (EMB + 1)], qT[:, 0:st.nt],
                             mp[:, :, :].rearrange("p c e -> p (c e)"), start=True, stop=True).then_inc(k["yp"], 1)

        def pe_performer(pe, st):
            pe_channels(pe, st, 0, 0)

            def period(j, par, live):
                for c in range(NCH):
                    if live(0):
                        pe_main(pe, st, j, par, c)
                    if live(2) and c == 0:
                        pe_kvq(pe, st, j - 1, par)
                    if live(2) and c == 1:
                        pe_mp(pe, st, j - 1, par)
                    if live(2) and c == 2:
                        pe_y(pe, st, j - 1, par)
                    if live(-1) and c == 2:
                        pe_channels(pe, st, *before(j, par, -1))

            periods(pe, st.units, 3, period)

        def pe_turn(pe, st, j, par):
            n = nth(j, par)
            pe.wait_ge(m["yn"], n + (st.m0 + 1))
            at = 0
            for c in range(NCH):
                rows = st.real[c]
                last = nc.tensor.transpose(psum[:, par, at:at + rows], ynm[par][0:rows, c, :], ident[0:rows, 0:rows])
                at += rows
            last.then_inc(m["tr"], 1)

        def pe_w1(pe, st, j, par):
            n = nth(j, par)
            pe.wait_ge(m["tr_copied"], n + (st.m0 + 1))
            nc.tensor.matmul(psum[:, 2 + par, 0:st.columns], st.w1c[:, :], ynT[par][:, 0:st.columns],
                             start=True, stop=True).then_inc(m["w1"], 1)

        def pe_w2(pe, st, j, par):
            n = nth(j, par)
            pe.wait_ge(m["gelu"], n + (st.m0 + 1))
            pe.wait_ge(m_in[par], j * 16 + (st.y0 + 16))
            if not peeled(j):
                pe.wait_ge(m["out"], n + (st.m0 - 1))
            nc.tensor.matmul(psum[:, 4 + par, 0:st.columns], st.w2[:, :], gel[par][:, 0:st.columns],
                             start=True, stop=False)
            at = 0
            for c in range(NCH):
                rows = st.real[c]
                last = nc.tensor.matmul(psum[:, 4 + par, at:at + rows], yres[par][0:rows, c, :],
                                        ident[0:rows, 0:rows], start=False, stop=(c == NCH - 1))
                at += rows
            last.then_inc(m["w2"], 1)

        def pe_mlp(pe, st):
            def period(j, par, live):
                if live(4):
                    pe_w2(pe, st, *before(j, par, 4))
                if live(2):
                    pe_w1(pe, st, *before(j, par, 2))
                if live(1):
                    pe_turn(pe, st, *before(j, par, 1))

            periods(pe, st.mlp_units, MLP_DEPTH, period)

        @block.tensor
        def _(pe):
            pe.wait_ge(const_in, 64)
            pe.wait_ge(const_set, 1)
            pe_prepare(pe, one)
            pe_prepare(pe, two)
            pe.wait_ge(w["folded_copied"], one.nk + two.nk + 2)
            pe.wait_ge(w["mlp_set"], 2)
            pe_performer(pe, one)
            pe_mlp(pe, one)
            pe_performer(pe, two)
            pe_mlp(pe, two)
            pe.wait_ge(t_in, 16 * 12)
            pe.wait_ge(m["out"], two.m0 + two.mlp_units)

            def project(g, taps):
                pe.wait_ge(t["g"], g[0] + 1)
                for kk in taps:
                    rows = EMB * len(TAPS[kk])
                    last = nc.tensor.matmul(psum[0:GT, in_bank, 0:D], g_tile[0:rows, kk, GT * g[1]:GT * g[1] + GT],
                                            pw[0:rows, kk, :], start=(kk == 0), stop=(kk == NTAP - 1))
                if kk == NTAP - 1:
                    last.then_inc(t["hp"], 1)

            def turn_h(fr, g):
                pe.wait_ge(fr.sems["hn"], nth(*g) + 1)
                if not (isinstance(g[0], int) and g[0] == 0 and g[1] == 0):
                    pe.wait_ge(fr.sems["scores"], nth(*g))
                for half in range(2):
                    last = nc.tensor.transpose(psum[0:HALF, fr.narrow, GT * half:GT * half + GT],
                                               fr.hn[:, HALF * half:HALF * half + HALF], ident[0:GT, 0:GT])
                last.then_inc(fr.sems["tr"], 1)

            def route(g):
                fr = fronts[1]
                pe.wait_ge(fr.sems["hnT"], nth(*g) + 1)
                dst = psum[0:GT, fr.wide, D:D + NEXP + P]
                nc.tensor.matmul(dst, fr.hnT[:, 0, :], wrout[:, 0, :], start=True, stop=False)
                nc.tensor.matmul(dst, fr.hnT[0:HALF, 1, :], wrout[0:HALF, 1, :], start=False, stop=True
                                 ).then_inc(t["rt"], 1)

            def turn_factors(g):
                pe.wait_ge(t["aw"], nth(*g) + 1)
                nc.tensor.transpose(psum[:, fronts[1].narrow, 0:GT], aw, ident[0:GT, 0:GT]).then_inc(t["at"], 1)

            def queries_keys(fr, g):
                w_qkv = wqkv[fr.att]
                pe.wait_ge(fr.sems["hnT"], nth(*g) + 1)
                if fr.att == 1:
                    pe.wait_ge(t["aT"], nth(*g) + 1)
                for part in range(4):
                    dst = psum[0:HALF, fr.narrow, GT * part:GT * part + GT]
                    cols = slice(HALF * part, HALF * part + HALF)
                    nc.tensor.matmul(dst, w_qkv[:, 0, cols], fr.hnT[:, 0, :], start=True, stop=False)
                    last = nc.tensor.matmul(dst, w_qkv[0:HALF, 1, cols], fr.hnT[0:HALF, 1, :],
                                            start=False, stop=(fr.att == 0))
                    if fr.att == 1:
                        last = nc.tensor.matmul(dst, blora[:, cols], aT, start=False, stop=True)
                last.then_inc(fr.sems["qk"], 1)

            def values(fr, g):
                w_qkv = wqkv[fr.att]
                dst = psum[0:GT, fr.wide, 0:D]
                cols = slice(2 * D, 3 * D)
                nc.tensor.matmul(dst, fr.hnT[:, 0, :], w_qkv[:, 0, cols], start=True, stop=False)
                last = nc.tensor.matmul(dst, fr.hnT[0:HALF, 1, :], w_qkv[0:HALF, 1, cols],
                                        start=False, stop=(fr.att == 0))
                if fr.att == 1:
                    last = nc.tensor.matmul(dst, aT, blora[:, cols], start=False, stop=True)
                last.then_inc(fr.sems["v"], 1)

            def values_thrice(fr, g):
                pe.wait_ge(fr.sems["vt"], nth(*g) + 1)
                third = D * fr.att
                for i in range(GI):
                    dst = (psum[0:GT, fr.wide, D * i:D * i + D] if i < 2 else psum[0:GT, third_bank, third:third + D])
                    last = nc.tensor.matmul(dst, thrice[:, i, :], fr.vt, start=True, stop=True)
                last.then_inc(fr.sems["v3"], 1)

            def score(fr, g):
                for half in range(2):
                    pe.wait_ge(fr.sems["kx"], nth(*g) * 2 + half + 1)
                    for i in range(GI):
                        last = nc.tensor.matmul(psum[0:GT, fr.narrow, 216 * half:216 * half + 216],
                                                fr.qx[:, half, GT * i:GT * i + GT], fr.kx[:, half, 216 * i:216 * i + 216],
                                                start=(i == 0), stop=(i == GI - 1))
                last.then_inc(fr.sems["s"], 1)

            def turn_p(bk, g):
                pe.wait_ge(bk.sems["p"], nth(*g) + 1)
                for tri in range(TRI):
                    last = nc.tensor.transpose(
                        psum[0:GT, bk.bank, GT * tri:GT * tri + GT],
                        fronts[bk.att].s[g[1]][:, 3 * tri:3 * tri + 3, :].rearrange("p h t -> p (h t)"), ident[0:GT, 0:GT])
                last.then_inc(bk.sems["pt"], 1)

            def attend(bk, g):
                c = nth(*g) + 1
                pe.wait_ge(bk.sems["pT"], c)
                pe.wait_ge(fronts[bk.att].sems["vx"], c)
                for tri in range(TRI):
                    for i in range(GI):
                        at = GT * tri + T3 * i
                        row, to = tri % 2 * 64, GT * (tri // 2) + T3 * i
                        last = nc.tensor.matmul(psum[row:row + 3 * HD, bk.bank, to:to + T3],
                                                fronts[bk.att].vx[g[1]][:, i, 3 * HD * tri:3 * HD * tri + 3 * HD],
                                                bk.pT[:, at:at + T3], start=True, stop=True)
                last.then_inc(bk.sems["o"], 1)

            def project_out(bk, g):
                w_proj = wproj[bk.att]
                pe.wait_ge(bk.sems["oT"], nth(*g) + 1)
                for pair in range(TRI // 2):
                    last = nc.tensor.matmul(psum[0:GT, bk.bank, 0:D], bk.oT[:, GT * pair:GT * pair + GT],
                                            w_proj[:, pair, :], start=(pair == 0), stop=(pair == TRI // 2 - 1))
                last.then_inc(bk.sems["pj"], 1)

            def period(j, par, live):
                g = [before(j, par, back) for back in range(DEPTH)]
                if live(1):
                    queries_keys(fronts[0], g[1])
                    values(fronts[0], g[1])
                if live(3):
                    turn_h(fronts[1], g[3])
                if live(0):
                    project(g[0], range(3))
                if live(1):
                    values_thrice(fronts[0], g[1])
                if live(3):
                    route(g[3])
                if live(1):
                    score(fronts[0], g[1])
                if live(4):
                    turn_p(backs[1], g[4])
                if live(0):
                    project(g[0], range(3, NTAP))
                if live(3):
                    turn_factors(g[3])
                if live(4):
                    attend(backs[1], g[4])
                if live(3):
                    queries_keys(fronts[1], g[3])
                if live(4):
                    project_out(backs[1], g[4])
                if live(3):
                    values(fronts[1], g[3])
                if live(2):
                    turn_p(backs[0], g[2])
                if live(3):
                    values_thrice(fronts[1], g[3])
                if live(2):
                    attend(backs[0], g[2])
                if live(0):
                    turn_h(fronts[0], g[0])
                if live(2):
                    project_out(backs[0], g[2])
                if live(3):
                    score(fronts[1], g[3])

            periods(pe, NG, DEPTH, period)


def layout(inp):
    f = np.float32
    a = {}
    x = np.asarray(inp["x"])
    pad = np.zeros((B, 3, GRID * BLK, GRID * BLK), f)
    pad[:, :, 2:86, 2:86] = x
    blocks = pad.reshape(B, 3, GRID, BLK, GRID, BLK).transpose(0, 1, 3, 5, 2, 4).reshape(B, PIX, GRID, GRID)
    a["x"] = np.concatenate([blocks[..., 0:S1], blocks[..., 1:GRID]], 1).reshape(B, 2 * PIX, GRID * S1)
    a["ident"] = np.eye(P, dtype=f)
    half = np.arange(P) // EMB
    a["blockmean"] = (half[:, None] == half[None, :]).astype(f) / f(EMB)

    def rows1(v):
        full = np.zeros((3, 8, 8, v.shape[1]), f)
        full[:, :7, :7] = v.reshape(3, 7, 7, -1)
        full = full.reshape(3, 2, BLK, 2, BLK, -1)
        return full.transpose(3, 0, 2, 4, 1, 5).reshape(2 * PIX, 2, -1)

    def rows2(v):
        v = v.reshape(EMB, 3, 3, -1)
        full = np.zeros((P, NTAP, v.shape[-1]), f)
        for kk, taps in enumerate(TAPS):
            for upper, (kh, kw) in enumerate(taps):
                full[EMB * upper:EMB * upper + EMB, kk] = v[:, kh, kw]
        return full

    def twice(v):
        out = np.zeros((P, P), f)
        out[0:EMB, 0:EMB] = v
        out[EMB:P, EMB:P] = v
        return out

    for name, rows, feats in (("a1", rows1, F1), ("a2", rows2, F2)):
        g = {key: np.asarray(inp[f"L0_tok_{name}_{key}"]) for key in
             ("n1g", "n1b", "kqvw", "kqvb", "projw", "projb", "n2g", "n2b", "w1", "b1", "w2", "b2", "w")}
        a[name + "_w"] = rows(g["kqvw"])
        a[name + "_g"] = rows(g["n1g"][:, None])[:, :, 0]
        a[name + "_b"] = rows(g["n1b"][:, None])[:, :, 0]
        real = rows(np.ones((feats, 1), f))[:, :, 0]
        a[name + "_inv"] = (real / f(feats)).astype(f)
        if name == "a1":
            sq = np.zeros((P, 2), f)
            sq[2 * PIX:P] = (real / f(feats)).reshape(2, 3, BLK * BLK, 2)[:, 0].reshape(2 * BLK * BLK, 2)
            a["sq_weights"] = sq
            a["channels"] = np.kron(np.eye(2), np.kron(np.ones((3, 1)), np.eye(BLK * BLK))).astype(f)
        a[name + "_ninv"] = -a[name + "_inv"]
        a[name + "_kqvb"] = np.broadcast_to(g["kqvb"], (P, C3))
        a[name + "_pjb"] = np.broadcast_to(g["projb"], (P, EMB))
        paug = np.zeros((EMB + 1, EMB + 1), f)
        paug[0:EMB, 0:EMB] = g["projw"]
        paug[EMB, EMB] = 1.0
        a[name + "_paug"] = paug
        a[name + "_wT"] = g["w"].T
        a[name + "_w1"] = twice(g["w1"])
        a[name + "_w2"] = twice(g["w2"])
        a[name + "_cols"] = np.stack([np.concatenate([v, v]) for v in (g["n2g"], g["n2b"], g["b1"], g["b2"])], 1)
    a["pw"] = rows2(np.asarray(inp["L0_tok_proj_w"]))
    a["pb"] = np.broadcast_to(np.asarray(inp["L0_tok_proj_b"]), (P, D))

    def with_bias(w, b):
        full = np.zeros((HALF + 1, 2, w.shape[0]), f)
        full[0:HALF] = w.T.reshape(2, HALF, -1).transpose(1, 0, 2)
        full[HALF, 0] = b
        return full

    def by_pair(w, b):
        full = np.zeros((PAIR, TRI // 2, D), f)
        rows = w.T.reshape(TRI // 2, 2, 3 * HD, D)
        full[0:3 * HD] = rows[:, 0].transpose(1, 0, 2)
        full[64:PAIR] = rows[:, 1].transpose(1, 0, 2)
        full[3 * HD, 0] = b
        return full

    v = {key: np.asarray(inp["L0_" + key]) for key in
         ("attn_qkv_w", "attn_qkv_b", "attn_proj_w", "attn_proj_b", "attn_temperature", "ffn_W_qkv", "ffn_b_qkv",
          "ffn_W_gate", "ffn_b_gate", "ffn_A", "ffn_B_lora", "ffn_W_proj", "ffn_b_proj")}
    a["wqkv0"] = with_bias(v["attn_qkv_w"], v["attn_qkv_b"])
    a["wqkv1"] = with_bias(v["ffn_W_qkv"], v["ffn_b_qkv"])
    a["wproj0"] = by_pair(v["attn_proj_w"], v["attn_proj_b"])
    a["wproj1"] = by_pair(v["ffn_W_proj"], v["ffn_b_proj"])
    router = np.concatenate([v["ffn_W_gate"], v["ffn_A"].reshape(NEXP * RANK, D)], 0)
    a["wrout"] = with_bias(router, np.concatenate([v["ffn_b_gate"], np.zeros(P, f)]))
    a["blora"] = v["ffn_B_lora"].transpose(0, 2, 1).reshape(NEXP * RANK, 3 * D)
    a["temp"] = np.broadcast_to(v["attn_temperature"], (HALF, 1))
    a["kmask"] = (np.arange(HALF)[:, None] // HD == np.arange(6)[None, :]).astype(f)
    a["vmask"] = (np.arange(GT)[:, None] // T3 == np.arange(D)[None, :] // HD % 3).astype(f)
    tok = np.arange(GT)
    a["thrice"] = np.stack([(tok[:, None] == i * T3 + tok[None, :] % T3) for i in range(GI)], 1).astype(f)
    return a


def kernel(**inputs):
    import concourse.bacc as _bacc
    from concourse.bass_utils import run_bass_kernel_spmd as _run

    nc = _bacc.Bacc("TRN2", target_bir_lowering=False, num_devices=1)
    arrays, aps = {}, {}
    for name, v in layout(inputs).items():
        v = np.ascontiguousarray(v)
        arrays["in_" + name] = v
        aps[name] = nc.dram_tensor("in_" + name, v.shape, mybir.dt.from_np(v.dtype), kind="ExternalInput").ap()
    out = nc.dram_tensor("out_0", (NG * GT, D), F32, kind="ExternalOutput").ap()
    build(nc, aps, out)
    r = _run(nc, [arrays], core_ids=[0])
    return r.results[0]["out_0"][0:B * T3].reshape(B, T3, D)
```
